# Optimizing a Trainium2 kernel written in Bass

```python
import numpy as np
import jax
import jax.numpy as jnp

def _softmax(x, axis=-1):
    return jax.nn.softmax(x, axis=axis)

def _gelu(x):
    return jax.nn.gelu(x, approximate=True)

def _silu(x):
    return jax.nn.silu(x)

def _sigmoid(x):
    return jax.nn.sigmoid(x)

def _layernorm(x, axis=-1, eps=1e-05):
    m = jnp.mean(x, axis=axis, keepdims=True)
    v = jnp.var(x, axis=axis, keepdims=True)
    return (x - m) / jnp.sqrt(v + eps)

def _scatter_add(tgt, idx, src, axis=0):
    return tgt.at[idx].add(src)

def _segment_sum(src, seg, n):
    return jax.ops.segment_sum(src, seg, n)
kernel_name = 'mk_xattn_ffn_d2_seqx_r4_37ebba'

def setup_inputs(seed: int=0):
    np.random.seed(seed)
    _w = jnp.asarray

    def _rec_inputs():
        import jax
        import jax.numpy as jnp
        _rk = jax.random.key(seed)
        x = 7.22e-05 + 1 * jax.random.normal(jax.random.fold_in(_rk, 1), (16, 256, 256), jnp.float32)
        _lenS = 256 - jax.random.randint(jax.random.fold_in(_rk, 7), (16,), 0, max(1, 256 // 4) + 1, jnp.int32)
        _lenS2 = 256 - jax.random.randint(jax.random.fold_in(_rk, 8), (16,), 0, max(1, 256 // 4) + 1, jnp.int32)
        _ctx_1024P = jax.random.normal(jax.random.fold_in(_rk, 11), (16, 16, 256), jnp.float32)
        _ctx_1024c = jax.random.dirichlet(jax.random.fold_in(_rk, 511), 0.3 * jnp.ones((16,), jnp.float32), (16, 256))
        _ctx_1024t = jnp.einsum('bsk,bkd->bsd', _ctx_1024c, _ctx_1024P)
        _ctx_1024t = _ctx_1024t * jax.lax.rsqrt(jnp.mean(jnp.square(_ctx_1024t)) + 1e-12) * 0.953939
        ctx_1024 = 4.13588e-05 + 0.999923 * (_ctx_1024t + 0.3 * jax.random.normal(jax.random.fold_in(_rk, 611), (16, 256, 256), jnp.float32))
        _validS = jnp.arange(256)[None, :] < _lenS[:, None]
        _validS2 = jnp.arange(256)[None, :] < _lenS2[:, None]
        _causal = jnp.tril(jnp.ones((256, 256), dtype=bool))
        mask_1x1xSxS2_ik0 = jnp.where(jnp.broadcast_to(_validS2[0:1, None, None, :], (1, 1, 256, 256)), 0, 1).astype(jnp.int32)
        return (x, ctx_1024, mask_1x1xSxS2_ik0)
    x, ctx_1024, mask_1x1xSxS2_ik0 = _rec_inputs()

    def _L0_xattn_setup():
        import jax, jax.numpy as jnp
        import numpy as np
        D_MODEL = 256
        NUM_HEADS = 16
        D_K = D_MODEL // NUM_HEADS
        B, S = (4, 512)
        key = jax.random.key(seed)
        ks = jax.random.split(key, 11)
        scale = 1.0 / np.sqrt(D_MODEL)
        inp = {'query': jax.random.normal(ks[0], (B, S, D_MODEL), dtype=jnp.float32), 'key': jax.random.normal(ks[1], (B, S, D_MODEL), dtype=jnp.float32), 'value': jax.random.normal(ks[2], (B, S, D_MODEL), dtype=jnp.float32), 'mask': jnp.tril(jnp.ones((S, S), dtype=jnp.int32))[None, None, :, :], 'Wq': jax.random.normal(ks[3], (D_MODEL, D_MODEL), dtype=jnp.float32) * scale, 'bq': jax.random.normal(ks[4], (D_MODEL,), dtype=jnp.float32) * scale, 'Wk': jax.random.normal(ks[5], (D_MODEL, D_MODEL), dtype=jnp.float32) * scale, 'bk': jax.random.normal(ks[6], (D_MODEL,), dtype=jnp.float32) * scale, 'Wv': jax.random.normal(ks[7], (D_MODEL, D_MODEL), dtype=jnp.float32) * scale, 'bv': jax.random.normal(ks[8], (D_MODEL,), dtype=jnp.float32) * scale, 'Wo': jax.random.normal(ks[9], (D_MODEL, D_MODEL), dtype=jnp.float32) * scale, 'bo': jax.random.normal(ks[10], (D_MODEL,), dtype=jnp.float32) * scale}
        return inp
    _L0_xattn_all = _L0_xattn_setup()
    _L0_xattn_in = {k: v for k, v in _L0_xattn_all.items() if k in ('Wq', 'bq', 'Wk', 'bk', 'Wv', 'bv', 'Wo', 'bo')}
    del _L0_xattn_all

    def _L0_ffn_setup():
        import jax, jax.numpy as jnp
        import numpy as np
        DIM = 256

        def _reference_tuple_inner(x, W_r, W_k, W_v, mu_r, mu_k):
            B, T, C = x.shape
            x_prev = jnp.concatenate([jnp.zeros((B, 1, C), x.dtype), x[:, :-1, :]], axis=1)
            xr = mu_r * x + (1.0 - mu_r) * x_prev
            xk = mu_k * x + (1.0 - mu_k) * x_prev
            r = jax.nn.sigmoid(jnp.einsum('btc,dc->btd', xr, W_r))
            k = jnp.einsum('btc,dc->btd', xk, W_k)
            k_act = jnp.square(jax.nn.relu(k))
            out = r * jnp.einsum('btc,dc->btd', k_act, W_v)
            new_state = x[:, -1, :]
            return (out, new_state)
        key = jax.random.key(seed)
        ks = jax.random.split(key, 6)
        B, T, C = (8, 512, DIM)
        x = jax.random.normal(ks[0], (B, T, C), dtype=jnp.float32)
        s = 1.0 / np.sqrt(C)
        W_r = jax.random.uniform(ks[1], (C, C), jnp.float32, -s, s)
        W_k = jax.random.uniform(ks[2], (C, C), jnp.float32, -s, s)
        W_v = jax.random.uniform(ks[3], (C, C), jnp.float32, -s, s)
        mu_r = jax.random.uniform(ks[4], (C,), jnp.float32)
        mu_k = jax.random.uniform(ks[5], (C,), jnp.float32)
        return {'x': x, 'W_r': W_r, 'W_k': W_k, 'W_v': W_v, 'mu_r': mu_r, 'mu_k': mu_k}
    _L0_ffn_all = _L0_ffn_setup()
    _L0_ffn_in = {k: v for k, v in _L0_ffn_all.items() if k in ('W_r', 'W_k', 'W_v', 'mu_r', 'mu_k')}
    del _L0_ffn_all

    def _L1_xattn_setup():
        import jax, jax.numpy as jnp
        import numpy as np
        D_MODEL = 256
        N_HEADS = 16
        D_K = D_MODEL // N_HEADS

        def _split_heads(x):
            B, S, _ = x.shape
            return x.reshape(B, S, N_HEADS, D_K).transpose(0, 2, 1, 3)
        key = jax.random.key(seed)
        ks = jax.random.split(key, 12)
        B, S = (4, 512)
        sc = 1.0 / np.sqrt(D_MODEL)
        inp = {'query': jax.random.normal(ks[0], (B, S, D_MODEL), jnp.float32), 'key': jax.random.normal(ks[1], (B, S, D_MODEL), jnp.float32), 'value': jax.random.normal(ks[2], (B, S, D_MODEL), jnp.float32), 'Wq': jax.random.normal(ks[3], (D_MODEL, D_MODEL), jnp.float32) * sc, 'bq': jnp.zeros((D_MODEL,), jnp.float32), 'Wk': jax.random.normal(ks[4], (D_MODEL, D_MODEL), jnp.float32) * sc, 'bk': jnp.zeros((D_MODEL,), jnp.float32), 'Wv': jax.random.normal(ks[5], (D_MODEL, D_MODEL), jnp.float32) * sc, 'bv': jnp.zeros((D_MODEL,), jnp.float32), 'Wo': jax.random.normal(ks[6], (D_MODEL, D_MODEL), jnp.float32) * sc, 'bo': jnp.zeros((D_MODEL,), jnp.float32)}
        return inp
    _L1_xattn_all = _L1_xattn_setup()
    _L1_xattn_in = {k: v for k, v in _L1_xattn_all.items() if k in ('Wq', 'bq', 'Wk', 'bk', 'Wv', 'bv', 'Wo', 'bo')}
    del _L1_xattn_all

    def _L1_ffn_setup():
        import jax, jax.numpy as jnp
        import numpy as np
        D_MODEL = 256
        D_FF = 1024
        NUM_EXPERTS = 8
        TOP_K = 2
        BATCH = 4
        SEQ = 512
        key = jax.random.key(seed)
        ks = jax.random.split(key, 8)
        s = 0.02
        x = jax.random.normal(ks[0], (BATCH, SEQ, D_MODEL), dtype=jnp.float32)
        router_w = jax.random.normal(ks[1], (D_MODEL, NUM_EXPERTS), dtype=jnp.float32) * s
        router_b = jnp.zeros((NUM_EXPERTS,), dtype=jnp.float32)
        W1 = jax.random.normal(ks[2], (NUM_EXPERTS, D_MODEL, D_FF), dtype=jnp.float32) * s
        b1 = jnp.zeros((NUM_EXPERTS, D_FF), dtype=jnp.float32)
        W2 = jax.random.normal(ks[3], (NUM_EXPERTS, D_FF, D_MODEL), dtype=jnp.float32) * s
        b2 = jnp.zeros((NUM_EXPERTS, D_MODEL), dtype=jnp.float32)
        return {'x': x, 'router_w': router_w, 'router_b': router_b, 'W1': W1, 'b1': b1, 'W2': W2, 'b2': b2}
    _L1_ffn_all = _L1_ffn_setup()
    _L1_ffn_in = {k: v for k, v in _L1_ffn_all.items() if k in ('router_w', 'router_b', 'W1', 'b1', 'W2', 'b2')}
    del _L1_ffn_all
    return {'x': x, 'ctx_1024': ctx_1024, 'mask_1x1xSxS2_ik0': mask_1x1xSxS2_ik0, 'L0_xattn_Wq': _L0_xattn_in['Wq'], 'L0_xattn_bq': _L0_xattn_in['bq'], 'L0_xattn_Wk': _L0_xattn_in['Wk'], 'L0_xattn_bk': _L0_xattn_in['bk'], 'L0_xattn_Wv': _L0_xattn_in['Wv'], 'L0_xattn_bv': _L0_xattn_in['bv'], 'L0_xattn_Wo': _L0_xattn_in['Wo'], 'L0_xattn_bo': _L0_xattn_in['bo'], 'L0_ffn_W_r': _L0_ffn_in['W_r'], 'L0_ffn_W_k': _L0_ffn_in['W_k'], 'L0_ffn_W_v': _L0_ffn_in['W_v'], 'L0_ffn_mu_r': _L0_ffn_in['mu_r'], 'L0_ffn_mu_k': _L0_ffn_in['mu_k'], 'L1_xattn_Wq': _L1_xattn_in['Wq'], 'L1_xattn_bq': _L1_xattn_in['bq'], 'L1_xattn_Wk': _L1_xattn_in['Wk'], 'L1_xattn_bk': _L1_xattn_in['bk'], 'L1_xattn_Wv': _L1_xattn_in['Wv'], 'L1_xattn_bv': _L1_xattn_in['bv'], 'L1_xattn_Wo': _L1_xattn_in['Wo'], 'L1_xattn_bo': _L1_xattn_in['bo'], 'L1_ffn_router_w': _L1_ffn_in['router_w'], 'L1_ffn_router_b': _L1_ffn_in['router_b'], 'L1_ffn_W1': _L1_ffn_in['W1'], 'L1_ffn_b1': _L1_ffn_in['b1'], 'L1_ffn_W2': _L1_ffn_in['W2'], 'L1_ffn_b2': _L1_ffn_in['b2']}

def reference(x, ctx_1024, mask_1x1xSxS2_ik0, L0_xattn_Wq, L0_xattn_bq, L0_xattn_Wk, L0_xattn_bk, L0_xattn_Wv, L0_xattn_bv, L0_xattn_Wo, L0_xattn_bo, L0_ffn_W_r, L0_ffn_W_k, L0_ffn_W_v, L0_ffn_mu_r, L0_ffn_mu_k, L1_xattn_Wq, L1_xattn_bq, L1_xattn_Wk, L1_xattn_bk, L1_xattn_Wv, L1_xattn_bv, L1_xattn_Wo, L1_xattn_bo, L1_ffn_router_w, L1_ffn_router_b, L1_ffn_W1, L1_ffn_b1, L1_ffn_W2, L1_ffn_b2):
    import jax
    import jax.numpy as jnp

    def _L0_xattn_ref(query, key, value, mask, Wq, bq, Wk, bk, Wv, bv, Wo, bo):
        import jax, jax.numpy as jnp
        import numpy as np
        D_MODEL = 256
        NUM_HEADS = 16
        D_K = D_MODEL // NUM_HEADS
        B, S = (4, 512)
        b, s, _ = query.shape
        Q = (query @ Wq.T + bq).reshape(b, s, NUM_HEADS, D_K).transpose(0, 2, 1, 3)
        K = (key @ Wk.T + bk).reshape(b, s, NUM_HEADS, D_K).transpose(0, 2, 1, 3)
        V = (value @ Wv.T + bv).reshape(b, s, NUM_HEADS, D_K).transpose(0, 2, 1, 3)
        scores = jnp.einsum('bhqd,bhkd->bhqk', Q, K) / jnp.sqrt(jnp.float32(D_K))
        scores = jnp.where(mask == 0, -jnp.inf, scores)
        attn = jax.nn.softmax(scores, axis=-1)
        x = jnp.einsum('bhqk,bhkd->bhqd', attn, V)
        x = x.transpose(0, 2, 1, 3).reshape(b, s, D_MODEL)
        return x @ Wo.T + bo

    def _L0_ffn_ref(x, W_r, W_k, W_v, mu_r, mu_k):
        import jax, jax.numpy as jnp
        import numpy as np
        DIM = 256

        def _reference_tuple_inner(x, W_r, W_k, W_v, mu_r, mu_k):
            B, T, C = x.shape
            x_prev = jnp.concatenate([jnp.zeros((B, 1, C), x.dtype), x[:, :-1, :]], axis=1)
            xr = mu_r * x + (1.0 - mu_r) * x_prev
            xk = mu_k * x + (1.0 - mu_k) * x_prev
            r = jax.nn.sigmoid(jnp.einsum('btc,dc->btd', xr, W_r))
            k = jnp.einsum('btc,dc->btd', xk, W_k)
            k_act = jnp.square(jax.nn.relu(k))
            out = r * jnp.einsum('btc,dc->btd', k_act, W_v)
            new_state = x[:, -1, :]
            return (out, new_state)
        return _reference_tuple_inner(x, W_r, W_k, W_v, mu_r, mu_k)[0]

    def _L1_xattn_ref(query, key, value, Wq, bq, Wk, bk, Wv, bv, Wo, bo):
        import jax, jax.numpy as jnp
        import numpy as np
        D_MODEL = 256
        N_HEADS = 16
        D_K = D_MODEL // N_HEADS

        def _split_heads(x):
            B, S, _ = x.shape
            return x.reshape(B, S, N_HEADS, D_K).transpose(0, 2, 1, 3)
        q = _split_heads(query @ Wq.T + bq)
        k = _split_heads(key @ Wk.T + bk)
        v = _split_heads(value @ Wv.T + bv)
        scores = jnp.einsum('bhqd,bhkd->bhqk', q, k) / jnp.sqrt(jnp.float32(D_K))
        probs = jax.nn.softmax(scores, axis=1)
        attn = jnp.einsum('bhqk,bhkd->bhqd', probs, v)
        B, H, S, Dk = attn.shape
        combined = attn.transpose(0, 2, 1, 3).reshape(B, S, H * Dk)
        return combined @ Wo.T + bo

    def _L1_ffn_ref(x, router_w, router_b, W1, b1, W2, b2):
        import jax, jax.numpy as jnp
        import numpy as np
        D_MODEL = 256
        D_FF = 1024
        NUM_EXPERTS = 8
        TOP_K = 2
        BATCH = 4
        SEQ = 512
        logits = jnp.einsum('bsd,de->bse', x, router_w) + router_b
        topk_scores, topk_idx = jax.lax.top_k(logits, TOP_K)
        topk_gates = jax.nn.softmax(topk_scores, axis=-1)
        onehot = jax.nn.one_hot(topk_idx, NUM_EXPERTS, dtype=x.dtype)
        combine = jnp.einsum('bsk,bske->bse', topk_gates, onehot)
        combine_e = jnp.moveaxis(combine, -1, 0)

        def expert_step(acc, params):
            w1, bb1, w2, bb2, c = params
            h = jax.nn.relu(jnp.einsum('bsd,df->bsf', x, w1) + bb1)
            y = jnp.einsum('bsf,fd->bsd', h, w2) + bb2
            return (acc + y * c[..., None], None)
        out, _ = jax.lax.scan(expert_step, jnp.zeros_like(x), (W1, b1, W2, b2, combine_e))
        return out
    x = x + _L0_xattn_ref(_layernorm(x, axis=-1), ctx_1024, ctx_1024, mask_1x1xSxS2_ik0, L0_xattn_Wq, L0_xattn_bq, L0_xattn_Wk, L0_xattn_bk, L0_xattn_Wv, L0_xattn_bv, L0_xattn_Wo, L0_xattn_bo)
    x = x + _L0_ffn_ref(_layernorm(x, axis=-1), L0_ffn_W_r, L0_ffn_W_k, L0_ffn_W_v, L0_ffn_mu_r, L0_ffn_mu_k)
    x = x + _L1_xattn_ref(_layernorm(x, axis=-1), ctx_1024, ctx_1024, L1_xattn_Wq, L1_xattn_bq, L1_xattn_Wk, L1_xattn_bk, L1_xattn_Wv, L1_xattn_bv, L1_xattn_Wo, L1_xattn_bo)
    x = x + _L1_ffn_ref(_layernorm(x, axis=-1), L1_ffn_router_w, L1_ffn_router_b, L1_ffn_W1, L1_ffn_b1, L1_ffn_W2, L1_ffn_b2)
    return x

_drawn_inputs = setup_inputs


def setup_inputs(seed=0):
    import zlib

    import numpy as np

    out = dict(_drawn_inputs(seed))
    spreads = {'L1_xattn_bq': (0.0, 0.1),
     'L1_xattn_bk': (0.0, 0.1),
     'L1_xattn_bv': (0.0, 0.1),
     'L1_xattn_bo': (0.0, 0.784),
     'L1_ffn_router_b': (0.0, 0.8),
     'L1_ffn_b1': (0.0, 0.8),
     'L1_ffn_b2': (0.0, 0.8)}
    factors = {'L0_xattn_bq': 6.008,
     'L0_xattn_bk': 8.0,
     'L0_ffn_W_r': 5.328,
     'L0_ffn_mu_r': 8.0,
     'L1_ffn_router_w': 5.271,
     'L1_ffn_W1': 6.475,
     'L1_ffn_W2': 5.177}
    for name, (base, spread) in spreads.items():
        noise = np.random.default_rng([zlib.crc32(name.encode()), seed]).standard_normal(out[name].shape)
        drawn = base * np.exp(spread * noise) if base else spread * noise
        out[name] = jnp.asarray(drawn.astype(out[name].dtype))
    for name, factor in factors.items():
        out[name] = (out[name] * factor).astype(out[name].dtype)
    return out
```

```python
from contextlib import ExitStack

import numpy as np

import concourse.bass as bass
from concourse import mybir

F32 = mybir.dt.float32
BF16 = mybir.dt.bfloat16
I32 = mybir.dt.int32
U32 = mybir.dt.uint32
ALU = mybir.AluOpType
ACT = mybir.ActivationFunctionType
AX = mybir.AxisListType

P = 128
B, S, D = 16, 256, 256
H = 16
DK = D // H
QT = S // P
NT = B * QT
KC = D // P
HC = P // DK
G = 4
E, FF = 8, 1024
FC = FF // P
SLOT_TILES = -(-(2 * B * S + E * (P - 1)) // P) // 2 * 2
SCALE = DK ** -0.5
EPS = 1e-5
MASKED = -1e30


class Kit:
    pass


def load_x(nc, kit, x):
    with ExitStack() as ctx:
        x_in = [ctx.enter_context(nc.semaphore(f"x_in{i}")) for i in range(4)]
        const_in = ctx.enter_context(nc.semaphore("const_in"))
        part_stats = ctx.enter_context(nc.semaphore("part_stats"))
        stats = ctx.enter_context(nc.sbuf_tensor("stats0", [P, NT, 6], F32))
        block = ctx.enter_context(nc.Block())
        n = NT // 4

        @block.sync
        def _(sp):
            for i in range(4):
                sp.dma_start(kit.x[:, n * i:n * (i + 1), :],
                             x[P * n * i:P * n * (i + 1), :].rearrange("(t p) c -> p t c", p=P)).then_inc(x_in[i], 16)

        @block.scalar
        def _(act):
            act.dma_start(kit.ident[:, :], kit.ident_d).then_inc(const_in, 16)
            act.wait_ge(const_in, 16)

        @block.vector
        def _(dve):
            for t in range(NT):
                if t % n == 0:
                    dve.wait_ge(x_in[t // n], 16)
                dve.bn_stats(stats[:, t, :], kit.x[:, t, :]).then_inc(part_stats, 1)
            for t in range(NT):
                dve.wait_ge(part_stats, t + 1)
                last = dve.bn_aggr(kit.mv[:, t, :], stats[:, t, :])
            last.then_inc(part_stats, 1)
            dve.wait_ge(part_stats, NT + 1)


def keep_rows(dve, kit, tiles, upd, xnew, stats, aggr, x_ready, i):
    n = upd.shape[1]
    dve.tensor_tensor(xnew[:, :, :], kit.x[:, tiles, :], upd[:, :, :], ALU.add).then_inc(x_ready, 1)
    dve.wait_ge(x_ready, 3 * i + 1)
    for t in range(n):
        last = dve.bn_stats(stats[:, t, :], xnew[:, t, :])
    last.then_inc(x_ready, 1)
    dve.wait_ge(x_ready, 3 * i + 2)
    dve.tensor_scalar(kit.x[:, tiles, :], xnew[:, :, :], 1.0, None, ALU.mult)
    for t in range(n):
        last = dve.bn_aggr(aggr[:, t, :], stats[:, t, :])
    last.then_inc(x_ready, 1)
    dve.wait_ge(x_ready, 3 * i + 3)
    dve.tensor_scalar(kit.mv[:, tiles, :], aggr[:, :, :], 1.0, None, ALU.mult)


def attend_keys(nc, kit, d):
    U = H // 2
    with ExitStack() as ctx:
        def sb(name, shape, dt=F32):
            return ctx.enter_context(nc.sbuf_tensor("a_" + name, shape, dt))

        def sem(name):
            return ctx.enter_context(nc.semaphore("a_" + name))

        wq, wk, wv, wo = (sb(n, [P, KC, D]) for n in ("wq", "wk", "wv", "wo"))
        bq, bk = sb("bq", [P, KC]), sb("bk", [P, KC])
        bv = sb("bv", [P, D])
        added = sb("added", [P, QT, D])
        head_of = sb("head_of", [P, HC])
        mask_i = sb("mask_i", [P, QT, S], I32)
        mask_b = sb("mask_b", [P, QT, S], BF16)
        ident_b = sb("ident_b", [P, P], BF16)
        seen = sb("seen", [P, 3, QT])
        rstd = sb("rstd", [P, 2, NT])
        zeros = sb("zeros", [P, D])
        ctxT = sb("ctxT", [P, 2, KC, S])
        xn = sb("xn", [P, QT, D])
        xnT = sb("xnT", [P, KC, S])
        qT = sb("qT", [P, 2, KC, S])
        kT = sb("kT", [P, KC, S])
        kTh = sb("kTh", [P, 2, H, S])
        va = sb("va", [P, 2, QT, H, 2 * DK])
        mx, nmx = sb("mx", [P, 2, 4]), sb("nmx", [P, 2, 4])
        pr = sb("pr", [P, 2, 4, S])
        prT = sb("prT", [P, 2, 2, QT, S])
        oT = sb("oT", [P, H // G, S])
        rden = sb("rden", [P, QT, H])
        on = sb("on", [P, QT, D])
        onT = sb("onT", [P, KC, S])
        upd = sb("upd", [P, QT, D])
        xnew = sb("xnew", [P, QT, D])
        stats, aggr = sb("stats", [P, QT, 6]), sb("aggr", [P, QT, 2])

        ps_step = ctx.enter_context(nc.psum_tensor("a_ps_step", [P, 512], F32))
        ps_o = ctx.enter_context(nc.psum_tensor("a_ps_o", [P, 512], F32))
        ps_s = ctx.enter_context(nc.psum_tensor("a_ps_s", [P, 2, 2, QT, S], F32))
        ps_t = ctx.enter_context(nc.psum_tensor("a_ps_t", [P, 2, QT, S], F32))
        step4 = ps_step[:, :].rearrange("p (a b) -> p a b", a=2)

        w_in, misc_in, zeroed = sem("w_in"), sem("misc_in"), sem("zeroed")
        ctx_in = [sem("ctx_in0"), sem("ctx_in1")]
        setup = sem("setup")
        sd_ready = sem("sd_ready")
        ones_ready = sem("ones_ready")
        xn_ready, xnT_ps, xnT_ready = sem("xn_ready"), sem("xnT_ps"), sem("xnT_ready")
        k_ps, k_ready, kh_ready = sem("k_ps"), sem("k_ready"), sem("kh_ready")
        q_ps, q_ready = sem("q_ps"), sem("q_ready")
        v_ps, v_ready = sem("v_ps"), sem("v_ready")
        s_ps, mx_ready, nmx_ready, pr_ready = sem("s_ps"), sem("mx_ready"), sem("nmx_ready"), sem("pr_ready")
        t_ps, prT_dve, prT_act = sem("t_ps"), sem("prT_dve"), sem("prT_act")
        o_ps, oT_ready = sem("o_ps"), sem("oT_ready")
        back_ps, rden_ready, on_ready = sem("back_ps"), sem("rden_ready"), sem("on_ready")
        onT_ps, onT_ready = sem("onT_ps"), sem("onT_ready")
        y_ps, upd_ready, x_ready = sem("y_ps"), sem("upd_ready"), sem("x_ready")
        block = ctx.enter_context(nc.Block())

        def batches(eng, body):
            body(0, 0, True, False)
            with eng.Fori(1, B - 2, 2) as b:
                body(b, 1, False, False)
                body(b + 1, 0, False, False)
            body(B - 1, 1, False, True)

        @block.sync
        def _(sp):
            for buf, w in ((wk, "wkT"), (wq, "wqT"), (wv, "wvT"), (wo, "woT")):
                sp.dma_start(buf[:, :, :], d[w].rearrange("(c p) n -> p c n", p=P)).then_inc(w_in, 16)

            def load(b, par):
                sp.dma_start(ctxT[:, par, :, :], d["ctxT"][:, bass.ds(b * S, S)].rearrange("(c p) n -> p c n", p=P))\
                    .then_inc(ctx_in[par], 16)

            load(0, 0)
            load(1, 1)
            sp.wait_ge(ones_ready, 2)
            sp.dma_start(kit.sorted_d.rearrange("(t p) c -> p t c", p=P),
                         zeros[:, :].unsqueeze(1).to_broadcast([P, SLOT_TILES, D])).then_inc(zeroed, 16)
            with sp.Fori(2, B - 1, 2) as b:
                sp.wait_ge(v_ready, b - 1)
                load(b, 0)
                sp.wait_ge(v_ready, b)
                load(b + 1, 1)
            sp.wait_ge(zeroed, 16)

        @block.scalar
        def _(act):
            act.dma_start(mask_i[:, :, :], d["mask"].rearrange("(t p) k -> p t k", p=P)).then_inc(misc_in, 16)
            for buf, n in ((bq, "bq"), (bk, "bk"), (bv, "bv"), (head_of, "head_of")):
                act.dma_start(buf[:, :], d[n]).then_inc(misc_in, 16)
            for t in range(QT):
                act.dma_start(added[:, t, :], d["bo"]).then_inc(misc_in, 16)
            act.wait_ge(setup, 1)
            act.activation(rstd[:, 1, :], rstd[:, 0, :], ACT.Sqrt).then_inc(sd_ready, 1)
            act.wait_ge(misc_in, 16 * (5 + QT))

            def step_xnT(b):
                act.wait_ge(xnT_ps, b + 1)
                act.activation(xnT[:, :, :], step4, ACT.Copy).then_inc(xnT_ready, 1)

            def step_k(b):
                act.wait_ge(k_ps, b + 1)
                if not isinstance(b, int) or b > 0:
                    act.wait_ge(kh_ready, 2 * b)
                for c in range(KC):
                    last = act.activation(kT[:, c, :], step4[:, c, :], ACT.Identity, bias=bk[:, c:c + 1])
                last.then_inc(k_ready, 1)

            def step_q(b, par):
                act.wait_ge(q_ps, b + 1)
                for c in range(KC):
                    last = act.activation(qT[:, par, c, :], step4[:, c, :], ACT.Identity, bias=bq[:, c:c + 1])
                last.then_inc(q_ready, 1)

            def numerators(b, u, par):
                n = b * U + u
                act.wait_ge(nmx_ready, n + 1)
                for i in range(4):
                    last = act.activation(pr[:, par, i, :], ps_s[:, par, i // 2, i % 2, :], ACT.Exp,
                                          bias=nmx[:, par, i:i + 1], scale=SCALE)
                last.then_inc(pr_ready, 1)

            step_xnT(0)
            step_k(0)
            step_q(0, 0)
            numerators(0, 0, 0)

            def body(b, par, first, last):
                for u in range(U):
                    if not (last and u == U - 1):
                        numerators(b, u + 1, (u + 1) % 2)
                    if u == 0 and not last:
                        step_xnT(b + 1)
                    if u == 1 and not last:
                        step_k(b + 1)
                    if u == 4 and not last:
                        step_q(b + 1, 1 - par)
                    if u == 5 and not first:
                        act.wait_ge(onT_ps, b)
                        act.activation(onT[:, :, :], step4, ACT.Copy).then_inc(onT_ready, 1)
                    act.wait_ge(t_ps, b * U + u + 1)
                    act.activation(prT[:, u % 2, 1, :, :], ps_t[:, 1, :, :], ACT.Copy).then_inc(prT_act, 1)

            batches(act, body)
            act.wait_ge(onT_ps, B)
            act.activation(onT[:, :, :], step4, ACT.Copy).then_inc(onT_ready, 1)

        @block.gpsimd
        def _(pool):
            pool.memset(va[:, :, :, :, :], 1.0).then_inc(ones_ready, 1)
            pool.memset(zeros[:, :], 0.0).then_inc(ones_ready, 1)
            pool.wait_ge(misc_in, 16 * (5 + QT))

            def split_heads(b, par, after):
                pool.wait_ge(k_ready, b + 1)
                if after is not None:
                    pool.wait_ge(s_ps, after)
                for c in range(KC):
                    pool.tensor_tensor(kTh[:, par, HC * c:HC * (c + 1), :],
                                       kT[:, c, :].unsqueeze(1).to_broadcast([P, HC, S]),
                                       head_of[:, :].unsqueeze(2).to_broadcast([P, HC, S]), ALU.mult)\
                        .then_inc(kh_ready, 1)

            split_heads(0, 0, None)
            split_heads(1, 1, None)
            with pool.Fori(2, B - 1, 2) as b:
                split_heads(b, 0, (b - 1) * U)
                split_heads(b + 1, 1, b * U)

        @block.vector
        def _(dve):
            dve.tensor_scalar(rstd[:, 0, :], kit.mv[:, :, 1], EPS, None, ALU.add).then_inc(setup, 1)
            dve.tensor_copy(ident_b[:, :], kit.ident[:, :]).then_inc(setup, 1)
            dve.wait_ge(misc_in, 16 * (5 + QT))
            dve.tensor_scalar(mask_b[:, :, :], mask_i[:, :, :], 0.0, MASKED, ALU.is_equal, ALU.mult).then_inc(setup, 1)
            dve.wait_ge(setup, 3)
            dve.tensor_reduce(seen[:, 0, :], mask_b[:, :, :], AX.X, ALU.max).then_inc(setup, 1)
            dve.wait_ge(setup, 4)
            dve.tensor_scalar(seen[:, 1, :], seen[:, 0, :], 0.0, None, ALU.is_equal).then_inc(setup, 1)
            dve.wait_ge(setup, 5)
            dve.reciprocal(seen[:, 2, :], seen[:, 1, :]).then_inc(setup, 1)
            dve.wait_ge(setup, 6)
            dve.tensor_scalar(seen[:, 0, :], seen[:, 2, :], 0.0, None, ALU.mult).then_inc(setup, 1)
            dve.wait_ge(setup, 7)
            for t in range(QT):
                dve.tensor_scalar(added[:, t, :], added[:, t, :], seen[:, 0, t:t + 1], None, ALU.add).then_inc(setup, 1)
            dve.wait_ge(sd_ready, 1)
            dve.reciprocal(rstd[:, 0, :], rstd[:, 1, :]).then_inc(setup, 1)
            dve.wait_ge(setup, 10)
            dve.wait_ge(ones_ready, 1)

            def normalize(b):
                if not isinstance(b, int) or b > 0:
                    dve.wait_ge(xnT_ps, b)
                for t in range(QT):
                    last = dve.tensor_scalar(xn[:, t, :], kit.x[:, QT * b + t, :],
                                             kit.mv[:, QT * b + t, 0:1],
                                             rstd[:, 0, bass.ds(QT * b + t, 1)], ALU.subtract, ALU.mult)
                last.then_inc(xn_ready, 1)

            def step_v(b, par):
                dve.wait_ge(v_ps, b + 1)
                dve.tensor_tensor(va[:, par, :, :, 0:DK],
                                  ps_step[:, :].rearrange("p (t h k) -> p t h k", t=QT, h=H),
                                  bv[:, :].rearrange("p (h k) -> p h k", h=H).unsqueeze(1).to_broadcast([P, QT, H, DK]),
                                  ALU.add).then_inc(v_ready, 1)

            def maxima(b, u, par):
                n = b * U + u
                dve.wait_ge(s_ps, n + 1)
                dve.tensor_reduce(mx[:, par, :], ps_s[:, par, :, :, :].rearrange("p a b k -> p (a b) k"),
                                  AX.X, ALU.max).then_inc(mx_ready, 1)
                dve.wait_ge(mx_ready, n + 1)
                dve.tensor_scalar(nmx[:, par, :], mx[:, par, :], -SCALE, None, ALU.mult).then_inc(nmx_ready, 1)

            def step_back(b, half):
                dve.wait_ge(back_ps, 2 * b + half + 1)
                back = ps_step[:, :].rearrange("p (t h k) -> p t h k", t=QT, k=2 * DK)
                h0 = half * 2 * G
                dve.reciprocal(rden[:, :, h0:h0 + 2 * G], back[:, :, :, DK]).then_inc(rden_ready, 1)
                dve.wait_ge(rden_ready, 2 * b + half + 1)
                dve.tensor_tensor(on[:, :, h0 * DK:(h0 + 2 * G) * DK].rearrange("p t (h k) -> p t h k", k=DK),
                                  back[:, :, :, 0:DK],
                                  rden[:, :, h0:h0 + 2 * G].unsqueeze(3).to_broadcast([P, QT, 2 * G, DK]),
                                  ALU.mult).then_inc(on_ready, 1)

            def step_y(b):
                dve.wait_ge(y_ps, b + 1)
                dve.tensor_tensor(upd[:, :, :], step4, added[:, :, :], ALU.add).then_inc(upd_ready, 1)
                dve.wait_ge(upd_ready, b + 1)
                keep_rows(dve, kit, bass.ds(QT * b, QT), upd, xnew, stats, aggr, x_ready, b)

            normalize(0)
            step_v(0, 0)
            maxima(0, 0, 0)

            def body(b, par, first, last):
                for u in range(U):
                    if not (last and u == U - 1):
                        maxima(b, u + 1, (u + 1) % 2)
                    if u == 2 and not first:
                        step_back(b - 1, 0)
                    if u == 3 and not first:
                        step_back(b - 1, 1)
                    if u == 6 and not first:
                        step_y(b - 1)
                    if u == 7 and not last:
                        step_v(b + 1, 1 - par)
                    dve.wait_ge(t_ps, b * U + u + 1)
                    dve.tensor_copy(prT[:, u % 2, 0, :, :], ps_t[:, 0, :, :]).then_inc(prT_dve, 1)
                    if u % 2 == 0 and not (first and u == 0):
                        dve.wait_ge(o_ps, b * (H // G) + u // 2)
                        take_group(b - 1 if u == 0 else b, (u // 2 - 1) % (H // G), first)

            def take_group(bb, group, first):
                if not first and group < H // G - 1:
                    dve.wait_ge(back_ps, 2 * bb - 1 + group // 2)
                dve.tensor_copy(oT[:, group, :], ps_o[:, 0:S]).then_inc(oT_ready, 1)

            def normalized_body(b, par, first, last):
                if not last:
                    normalize(b + 1)
                body(b, par, first, last)

            batches(dve, normalized_body)
            dve.wait_ge(o_ps, B * H // G)
            take_group(B - 1, H // G - 1, False)
            step_back(B - 1, 0)
            step_back(B - 1, 1)
            step_y(B - 1)

        @block.tensor
        def _(pe):
            pe.wait_ge(setup, 2)
            pe.wait_ge(w_in, 64)

            def product(out, lhsT, rhs, n):
                for c in range(n):
                    last = pe.matmul(out, lhsT(c), rhs(c), start=c == 0, stop=c == n - 1)
                return last

            def step_xnT(b):
                pe.wait_ge(xn_ready, b + 1)
                for c in range(KC):
                    for t in range(QT):
                        last = pe.transpose(step4[:, c, P * t:P * (t + 1)], xn[:, t, P * c:P * (c + 1)], kit.ident[:, :])
                last.then_inc(xnT_ps, 1)

            def step_k(b, par):
                pe.wait_ge(ctx_in[par], (b - par) * 8 + 16)
                pe.wait_ge(xnT_ready, b + 1)
                for m in range(KC):
                    last = product(step4[:, m, :], lambda c: wk[:, c, P * m:P * (m + 1)], lambda c: ctxT[:, par, c, :], KC)
                last.then_inc(k_ps, 1)

            def step_q(b, par, bank_free=None):
                pe.wait_ge(xnT_ready, b + 1)
                if bank_free:
                    pe.wait_ge(*bank_free)
                for m in range(KC):
                    last = product(step4[:, m, :], lambda c: wq[:, c, P * m:P * (m + 1)], lambda c: xnT[:, c, :], KC)
                last.then_inc(q_ps, 1)

            def step_v(b, par, bank_free):
                pe.wait_ge(*bank_free)
                for t in range(QT):
                    last = product(step4[:, t, :], lambda c: ctxT[:, par, c, P * t:P * (t + 1)], lambda c: wv[:, c, :], KC)
                last.then_inc(v_ps, 1)

            def step_back(b, half, bank_free):
                pe.wait_ge(*bank_free)
                pe.wait_ge(oT_ready, b * (H // G) + 2 * half + 2)
                for t in range(QT):
                    for i in range(2):
                        last = pe.transpose(ps_step[:, (2 * t + i) * P:(2 * t + i + 1) * P],
                                            oT[:, 2 * half + i, P * t:P * (t + 1)], kit.ident[:, :])
                last.then_inc(back_ps, 1)

            def step_onT(b, bank_free):
                pe.wait_ge(*bank_free)
                pe.wait_ge(on_ready, 2 * b + 2)
                for c in range(KC):
                    for t in range(QT):
                        last = pe.transpose(step4[:, c, P * t:P * (t + 1)], on[:, t, P * c:P * (c + 1)], kit.ident[:, :])
                last.then_inc(onT_ps, 1)

            def step_y(b):
                pe.wait_ge(onT_ready, b + 1)
                for t in range(QT):
                    last = product(step4[:, t, :], lambda c: onT[:, c, P * t:P * (t + 1)], lambda c: wo[:, c, :], KC)
                last.then_inc(y_ps, 1)

            def scores(b, u, par):
                n = b * U + u
                if u == 0:
                    pe.wait_ge(q_ready, b + 1)
                    pe.wait_ge(kh_ready, 2 * b + 2)
                if not isinstance(b, int) or n >= 2:
                    pe.wait_ge(pr_ready, n - 1)
                c = 2 * u // HC
                for i in range(2):
                    pe.matmul(ps_s[:, u % 2, i, :, :], ident_b[:, :], mask_b[:, :, :], start=True, stop=False)
                    for t in range(QT):
                        last = pe.matmul(ps_s[:, u % 2, i, t, :], qT[:, par, c, P * t:P * (t + 1)],
                                         kTh[:, par, 2 * u + i, :], start=False, stop=t == QT - 1)
                last.then_inc(s_ps, 1)

            def turn(b, u):
                n = b * U + u
                pe.wait_ge(pr_ready, n + 1)
                if not isinstance(b, int) or n >= 1:
                    pe.wait_ge(prT_dve, n)
                    pe.wait_ge(prT_act, n)
                for i in range(2):
                    for k in range(QT):
                        for t in range(QT):
                            last = pe.transpose(ps_t[:, i, k, P * t:P * (t + 1)],
                                                pr[:, u % 2, 2 * i + t, P * k:P * (k + 1)], kit.ident[:, :])
                last.then_inc(t_ps, 1)

            def values(b, u, par):
                n = b * U + u
                if u == 0:
                    pe.wait_ge(v_ready, b + 1)
                if u % 2 == 0 and (not isinstance(b, int) or n >= 2):
                    pe.wait_ge(oT_ready, b * (H // G) + u // 2)
                pe.wait_ge(prT_dve, n + 1)
                pe.wait_ge(prT_act, n + 1)
                for i in range(2):
                    h = 2 * u + i
                    j = 2 * DK * (h % G)
                    for k in range(QT):
                        last = pe.matmul(ps_o[j:j + 2 * DK, 0:S], va[:, par, k, h, :], prT[:, u % 2, i, k, :],
                                         start=k == 0, stop=k == QT - 1)
                if u % 2 == 1:
                    last.then_inc(o_ps, 1)

            step_xnT(0)
            step_k(0, 0)
            step_q(0, 0, (k_ready, 1))
            step_v(0, 0, (q_ready, 1))
            scores(0, 0, 0)

            def body(b, par, first, last):
                for u in range(U):
                    if u < U - 1:
                        scores(b, u + 1, par)
                    elif not last:
                        scores(b + 1, 0, 1 - par)
                    if u == 0 and not last:
                        pe.wait_ge(v_ready, b + 1)
                        step_xnT(b + 1)
                    if u == 1 and not last:
                        step_k(b + 1, 1 - par)
                    if u == 2 and not first:
                        step_back(b - 1, 0, (k_ready, b + 2) if not last else (v_ready, b + 1))
                    if u == 3 and not first:
                        step_back(b - 1, 1, (on_ready, 2 * b - 1))
                    if u == 4 and not last:
                        step_q(b + 1, 1 - par, (on_ready, 2 * b) if not first else (k_ready, 2))
                    if u == 5 and not first:
                        step_onT(b - 1, (q_ready, b + 2) if not last else (on_ready, 2 * b))
                    if u == 6 and not first:
                        step_y(b - 1)
                    if u == 7 and not last:
                        step_v(b + 1, 1 - par, (upd_ready, b) if not first else (q_ready, 2))
                    turn(b, u)
                    if u > 0:
                        values(b, u - 1, par)
                    elif not first:
                        values(b - 1, U - 1, 1 - par)

            batches(pe, body)
            values(B - 1, U - 1, 1)
            step_back(B - 1, 0, (upd_ready, B - 1))
            step_back(B - 1, 1, (on_ready, 2 * B - 1))
            step_onT(B - 1, (on_ready, 2 * B))
            step_y(B - 1)


def channel_mix(nc, kit, d):
    with ExitStack() as ctx:
        def sb(name, shape, dt=F32):
            return ctx.enter_context(nc.sbuf_tensor("b_" + name, shape, dt))

        def sem(name):
            return ctx.enter_context(nc.semaphore("b_" + name))

        def psum(name):
            return ctx.enter_context(nc.psum_tensor("b_" + name, [P, 2, S], F32))

        wr, wk, wv = (sb(n, [P, KC, D]) for n in ("wr", "wk", "wv"))
        mu, rest = sb("mu", [P, 2, KC]), sb("rest", [P, 2, KC])
        rstd = sb("rstd", [P, 2, NT])
        xn = sb("xn", [P, QT, D])
        xT = sb("xT", [P, KC, S + 1])
        part = sb("part", [P, 2, KC, S])
        mix = sb("mix", [P, 2, 2, KC, S])
        kk = sb("kk", [P, KC, S])
        gate = sb("gate", [P, QT, D])
        upd, xnew = sb("upd", [P, QT, D]), sb("xnew", [P, QT, D])
        stats, aggr = sb("stats", [P, QT, 6]), sb("aggr", [P, QT, 2])
        ps_x, ps_r, ps_k, ps_y = (psum(n) for n in ("ps_x", "ps_r", "ps_k", "ps_y"))

        w_in, mu_in = sem("w_in"), sem("mu_in")
        setup, sd_ready = sem("setup"), sem("sd_ready")
        xn_ready, x_ps, xT_ready, part_ready = sem("xn_ready"), sem("x_ps"), sem("xT_ready"), sem("part_ready")
        mixed = sem("mixed")
        k_ps, kk_ready, r_ps, gate_ready = sem("k_ps"), sem("kk_ready"), sem("r_ps"), sem("gate_ready")
        y_ps, upd_ready, x_ready = sem("y_ps"), sem("upd_ready"), sem("x_ready")
        block = ctx.enter_context(nc.Block())

        def batches(eng, body):
            body(0, 0, False)
            with eng.Fori(1, B - 2, 2) as b:
                body(b, 1, False)
                body(b + 1, 0, False)
            body(B - 1, 1, True)

        @block.sync
        def _(sp):
            for i, n in enumerate(("mu_r", "mu_k")):
                sp.dma_start(mu[:, i, :], d[n]).then_inc(mu_in, 16)
            for buf, w in ((wk, "wkT"), (wr, "wrT"), (wv, "wvT")):
                sp.dma_start(buf[:, :, :], d[w].rearrange("(c p) n -> p c n", p=P)).then_inc(w_in, 16)

        @block.scalar
        def _(act):
            act.wait_ge(setup, 1)
            act.activation(rstd[:, 1, :], rstd[:, 0, :], ACT.Sqrt).then_inc(sd_ready, 1)
            act.wait_ge(mu_in, 32)

            def turned(b):
                act.wait_ge(x_ps, b + 1)
                if not isinstance(b, int) or b > 0:
                    act.wait_ge(mixed, b)
                act.activation(xT[:, :, 1:S + 1], ps_x[:, :, :], ACT.Copy).then_inc(xT_ready, 1)
                for i in range(2):
                    for c in range(KC):
                        last = act.activation(part[:, i, c, :], ps_x[:, c, :], ACT.Copy, scale=mu[:, i, c:c + 1])
                last.then_inc(part_ready, 1)

            def gates(b):
                act.wait_ge(r_ps, b + 1)
                if not isinstance(b, int) or b > 0:
                    act.wait_ge(upd_ready, b)
                act.activation(gate[:, :, :], ps_r[:, :, :], ACT.Sigmoid).then_inc(gate_ready, 1)

            turned(0)

            def body(b, par, last):
                gates(b)
                if not last:
                    turned(b + 1)

            batches(act, body)

        @block.vector
        def _(dve):
            dve.tensor_scalar(rstd[:, 0, :], kit.mv[:, :, 1], EPS, None, ALU.add).then_inc(setup, 1)
            dve.memset(xT[:, :, 0:1], 0.0).then_inc(setup, 1)
            dve.wait_ge(mu_in, 32)
            dve.tensor_scalar(rest[:, :, :], mu[:, :, :], -1.0, 1.0, ALU.mult, ALU.add).then_inc(setup, 1)
            dve.wait_ge(sd_ready, 1)
            dve.reciprocal(rstd[:, 0, :], rstd[:, 1, :]).then_inc(setup, 1)
            dve.wait_ge(setup, 4)

            def normalize(b):
                if not isinstance(b, int) or b > 0:
                    dve.wait_ge(x_ps, b)
                for t in range(QT):
                    last = dve.tensor_scalar(xn[:, t, :], kit.x[:, QT * b + t, :], kit.mv[:, QT * b + t, 0:1],
                                             rstd[:, 0, bass.ds(QT * b + t, 1)], ALU.subtract, ALU.mult)
                last.then_inc(xn_ready, 1)

            def mixing(b, par):
                dve.wait_ge(xT_ready, b + 1)
                dve.wait_ge(part_ready, b + 1)
                for i in range(2):
                    for c in range(KC):
                        last = dve.scalar_tensor_tensor(out=mix[:, par, i, c, :], in0=xT[:, c, 0:S],
                                                        scalar=rest[:, i, c:c + 1], in1=part[:, i, c, :],
                                                        op0=ALU.mult, op1=ALU.add)
                last.then_inc(mixed, 1)

            normalize(0)
            mixing(0, 0)

            def body(b, par, last):
                if not last:
                    normalize(b + 1)
                dve.wait_ge(k_ps, b + 1)
                dve.tensor_scalar(kk[:, :, :], ps_k[:, :, :], 0.0, None, ALU.max).then_inc(kk_ready, 1)
                dve.wait_ge(kk_ready, 2 * b + 1)
                dve.tensor_tensor(kk[:, :, :], kk[:, :, :], kk[:, :, :], ALU.mult).then_inc(kk_ready, 1)
                if not last:
                    mixing(b + 1, 1 - par)
                dve.wait_ge(y_ps, b + 1)
                dve.wait_ge(gate_ready, b + 1)
                dve.tensor_tensor(upd[:, :, :], ps_y[:, :, :], gate[:, :, :], ALU.mult).then_inc(upd_ready, 1)
                dve.wait_ge(upd_ready, b + 1)
                keep_rows(dve, kit, bass.ds(QT * b, QT), upd, xnew, stats, aggr, x_ready, b)

            batches(dve, body)

        @block.tensor
        def _(pe):
            pe.wait_ge(w_in, 48)

            def turn(b):
                pe.wait_ge(xn_ready, b + 1)
                if not isinstance(b, int) or b > 0:
                    pe.wait_ge(part_ready, b)
                for c in range(KC):
                    for t in range(QT):
                        last = pe.transpose(ps_x[:, c, P * t:P * (t + 1)], xn[:, t, P * c:P * (c + 1)], kit.ident[:, :])
                last.then_inc(x_ps, 1)

            turn(0)

            def body(b, par, last):
                pe.wait_ge(mixed, b + 1)
                for m in range(KC):
                    for c in range(KC):
                        mm = pe.matmul(ps_k[:, m, :], wk[:, c, P * m:P * (m + 1)], mix[:, par, 1, c, :],
                                       start=c == 0, stop=c == KC - 1)
                mm.then_inc(k_ps, 1)
                if not isinstance(b, int) or b > 0:
                    pe.wait_ge(gate_ready, b)
                for t in range(QT):
                    for c in range(KC):
                        mm = pe.matmul(ps_r[:, t, :], mix[:, par, 0, c, P * t:P * (t + 1)], wr[:, c, :],
                                       start=c == 0, stop=c == KC - 1)
                mm.then_inc(r_ps, 1)
                if not last:
                    turn(b + 1)
                pe.wait_ge(kk_ready, 2 * b + 2)
                if not isinstance(b, int) or b > 0:
                    pe.wait_ge(upd_ready, b)
                for t in range(QT):
                    for c in range(KC):
                        mm = pe.matmul(ps_y[:, t, :], kk[:, c, P * t:P * (t + 1)], wv[:, c, :],
                                       start=c == 0, stop=c == KC - 1)
                mm.then_inc(y_ps, 1)

            batches(pe, body)


def attend_heads(nc, kit, d):
    U = QT * QT
    HB = H // G
    HALF = H // 2
    HV = 12
    W = G * P
    with ExitStack() as ctx:
        def sb(name, shape, dt=F32):
            return ctx.enter_context(nc.sbuf_tensor("c_" + name, shape, dt))

        def sem(name):
            return ctx.enter_context(nc.semaphore("c_" + name))

        wq, wk, wv = (sb(n, [P, KC, D]) for n in ("wq", "wk", "wv"))
        wo = sb("wo", [P, H // G, D])
        bq, bk = sb("bq", [P, KC]), sb("bk", [P, KC])
        bv, bo = sb("bv", [P, D]), sb("bo", [P, D])
        head_of = sb("head_of", [P, HC])
        minus_i = sb("minus_i", [P, P], BF16)
        rstd = sb("rstd", [P, 2, NT])
        ctxT = sb("ctxT", [P, 2, KC, S])
        xn = sb("xn", [P, QT, D])
        xnT = sb("xnT", [P, KC, S])
        qT = sb("qT", [P, 2, KC, S])
        kT = sb("kT", [P, KC, S])
        kTh = sb("kTh", [P, 2, H, S])
        va = sb("va", [P, 2, QT, H, 2 * DK])
        mx = sb("mx", [P, 2, P])
        mxb = sb("mxb", [P, P], BF16)
        pr = sb("pr", [P, U, H, P])
        tree = sb("tree", [P, HALF, P])
        den, rden = sb("den", [P, P]), sb("rden", [P, P])
        oT = sb("oT", [P, H // G, P])
        upd, xnew = sb("upd", [P, 1, D]), sb("xnew", [P, 1, D])
        stats, aggr = sb("stats", [P, 1, 6]), sb("aggr", [P, 1, 2])

        ps_a = ctx.enter_context(nc.psum_tensor("c_ps_a", [P, 2, S], F32))
        ps_b = ctx.enter_context(nc.psum_tensor("c_ps_b", [P, 2, S], F32))
        ps_o = ctx.enter_context(nc.psum_tensor("c_ps_o", [P, H // G, P], F32))
        ps_s = ctx.enter_context(nc.psum_tensor("c_ps_s", [P, H, P], F32))

        w_in, misc_in = sem("w_in"), sem("misc_in")
        ctx_in = [sem("ctx_in0"), sem("ctx_in1")]
        setup, sd_ready, zeros_ready = sem("setup"), sem("sd_ready"), sem("zeros_ready")
        xn_ready, xnT_ps, xnT_ready = sem("xn_ready"), sem("xnT_ps"), sem("xnT_ready")
        k_ps, k_ready, kh_ready = sem("k_ps"), sem("k_ready"), sem("kh_ready")
        q_ps, q_ready, v_ps, v_ready = sem("q_ps"), sem("q_ready"), sem("v_ps"), sem("v_ready")
        s_ps, halves_ready, max_ready, shifted = sem("s_ps"), sem("halves_ready"), sem("max_ready"), sem("shifted")
        e_ready, tree_ready, den_ready, rden_ready = sem("e_ready"), sem("tree_ready"), sem("den_ready"), sem("rden_ready")
        pr_dve, pr_pool, pv_done = sem("pr_dve"), sem("pr_pool"), sem("pv_done")
        oT_ready, y_ps, upd_ready, x_ready = sem("oT_ready"), sem("y_ps"), sem("upd_ready"), sem("x_ready")
        block = ctx.enter_context(nc.Block())

        def batches(eng, body):
            body(0, 0, True, False)
            with eng.Fori(1, B - 2, 2) as b:
                body(b, 1, False, False)
                body(b + 1, 0, False, False)
            body(B - 1, 1, False, True)

        @block.sync
        def _(sp):
            for buf, w in ((wk, "wkT"), (wq, "wqT"), (wv, "wvT"), (wo, "woT")):
                sp.dma_start(buf[:, :, :], d[w].rearrange("(c p) n -> p c n", p=P)).then_inc(w_in, 16)

            def load(b, par):
                sp.dma_start(ctxT[:, par, :, :], d["ctxT"][:, bass.ds(b * S, S)].rearrange("(c p) n -> p c n", p=P))\
                    .then_inc(ctx_in[par], 16)

            load(0, 0)
            load(1, 1)
            with sp.Fori(2, B - 1, 2) as b:
                sp.wait_ge(v_ready, b - 1)
                load(b, 0)
                sp.wait_ge(v_ready, b)
                load(b + 1, 1)

        @block.scalar
        def _(act):
            for buf, n in ((bq, "bq"), (bk, "bk"), (bv, "bv"), (bo, "bo"), (head_of, "head_of")):
                act.dma_start(buf[:, :], d[n]).then_inc(misc_in, 16)
            act.wait_ge(setup, 1)
            act.activation(rstd[:, 1, :], rstd[:, 0, :], ACT.Sqrt).then_inc(sd_ready, 1)
            act.wait_ge(misc_in, 16 * 5)

            def step_xnT(b):
                act.wait_ge(xnT_ps, b + 1)
                act.activation(xnT[:, :, :], ps_b[:, :, :], ACT.Copy).then_inc(xnT_ready, 1)

            def step_k(b):
                act.wait_ge(k_ps, b + 1)
                for c in range(KC):
                    last = act.activation(kT[:, c, :], ps_a[:, c, :], ACT.Identity, bias=bk[:, c:c + 1])
                last.then_inc(k_ready, 1)
                act.wait_ge(k_ready, b + 1)

            def split_heads(b, par, c):
                for i in range(HC):
                    last = act.activation(kTh[:, par, HC * c + i, :], kT[:, c, :], ACT.Copy, scale=head_of[:, i:i + 1])
                last.then_inc(kh_ready, 1)

            def step_q(b, par):
                act.wait_ge(q_ps, b + 1)
                for c in range(KC):
                    last = act.activation(qT[:, par, c, :], ps_b[:, c, :], ACT.Identity, bias=bq[:, c:c + 1])
                last.then_inc(q_ready, 1)

            def numerators(b, i):
                n = b * U + i
                if not isinstance(b, int) or b > 0:
                    act.wait_ge(pv_done, n - U + 1)
                act.wait_ge(shifted, n + 1)
                for half in range(2):
                    hs = slice(HALF * half, HALF * (half + 1))
                    act.activation(pr[:, i, hs, :], ps_s[:, hs, :], ACT.Exp, scale=SCALE).then_inc(e_ready, 1)

            def take_o(j):
                act.wait_ge(pv_done, 2 * j + 2)
                if not isinstance(j, int) or j > 0:
                    act.wait_ge(y_ps, j)
                act.activation(oT[:, :, :], ps_o[:, :, :], ACT.Copy).then_inc(oT_ready, 1)

            step_xnT(0)
            step_k(0)
            step_q(0, 0)
            split_heads(0, 0, 0)
            split_heads(0, 0, 1)

            def body(b, par, first, last):
                for i in range(U):
                    if i == 0 and not last:
                        step_xnT(b + 1)
                    if i == 1 and not last:
                        step_k(b + 1)
                        step_q(b + 1, 1 - par)
                    numerators(b, i)
                    if i == 1 and not last:
                        split_heads(b + 1, 1 - par, 0)
                    if i == 2 and not last:
                        split_heads(b + 1, 1 - par, 1)
                    if i == 3:
                        take_o(2 * b)
                    if i == 1 and not first:
                        take_o(2 * b - 1)

            batches(act, body)
            take_o(2 * B - 1)

        @block.gpsimd
        def _(pool):
            pool.memset(va[:, :, :, :, :], 0.0).then_inc(zeros_ready, 1)

            def body(b, par, first, last):
                for i in range(U):
                    n = b * U + i
                    pool.wait_ge(e_ready, 2 * n + 2)
                    pool.tensor_tensor(tree[:, :, :], pr[:, i, 0:8, :], pr[:, i, 8:16, :], ALU.add).then_inc(tree_ready, 1)
                    pool.wait_ge(tree_ready, 3 * n + 1)
                    pool.tensor_tensor(tree[:, 0:4, :], tree[:, 0:4, :], tree[:, 4:8, :], ALU.add).then_inc(tree_ready, 1)
                    pool.wait_ge(tree_ready, 3 * n + 2)
                    pool.tensor_tensor(tree[:, 0:2, :], tree[:, 0:2, :], tree[:, 2:4, :], ALU.add).then_inc(tree_ready, 1)
                    if not first or i > 0:
                        pool.wait_ge(rden_ready, n)
                    pool.wait_ge(tree_ready, 3 * n + 3)
                    pool.tensor_tensor(den[:, :], tree[:, 0, :], tree[:, 1, :], ALU.add).then_inc(den_ready, 1)
                    pool.wait_ge(rden_ready, n + 1)
                    pool.tensor_tensor(pr[:, i, HV:H, :], pr[:, i, HV:H, :],
                                       rden[:, :].unsqueeze(1).to_broadcast([P, H - HV, P]), ALU.mult).then_inc(pr_pool, 1)

            batches(pool, body)

        @block.vector
        def _(dve):
            dve.tensor_scalar(rstd[:, 0, :], kit.mv[:, :, 1], EPS, None, ALU.add).then_inc(setup, 1)
            dve.tensor_scalar(minus_i[:, :], kit.ident[:, :], -1.0, None, ALU.mult).then_inc(setup, 1)
            dve.wait_ge(misc_in, 16 * 5)
            dve.wait_ge(sd_ready, 1)
            dve.reciprocal(rstd[:, 0, :], rstd[:, 1, :]).then_inc(setup, 1)
            dve.wait_ge(setup, 3)
            dve.wait_ge(zeros_ready, 1)

            def normalize(b):
                if not isinstance(b, int) or b > 0:
                    dve.wait_ge(xnT_ps, b)
                for t in range(QT):
                    last = dve.tensor_scalar(xn[:, t, :], kit.x[:, QT * b + t, :], kit.mv[:, QT * b + t, 0:1],
                                             rstd[:, 0, bass.ds(QT * b + t, 1)], ALU.subtract, ALU.mult)
                last.then_inc(xn_ready, 1)

            def step_v(b, par, ps):
                dve.wait_ge(v_ps, b + 1)
                dve.tensor_tensor(va[:, par, :, :, 0:DK], ps[:, :, :].rearrange("p t (h k) -> p t h k", h=H),
                                  bv[:, :].rearrange("p (h k) -> p h k", h=H).unsqueeze(1).to_broadcast([P, QT, H, DK]),
                                  ALU.add).then_inc(v_ready, 1)

            def maxima(b, i):
                n = b * U + i
                for half in range(2):
                    hs = slice(HALF * half, HALF * (half + 1))
                    dve.wait_ge(s_ps, 2 * n + half + 1)
                    dve.tensor_reduce(mx[:, half, :], ps_s[:, hs, :].rearrange("p h q -> p q h"), AX.X, ALU.max)\
                        .then_inc(halves_ready, 1)
                dve.wait_ge(halves_ready, 2 * n + 2)
                dve.tensor_tensor(mxb[:, :], mx[:, 0, :], mx[:, 1, :], ALU.max).then_inc(max_ready, 1)

            def probabilities(n, i, par):
                dve.wait_ge(den_ready, n + 1)
                if not isinstance(n, int) or n > 0:
                    dve.wait_ge(pr_pool, n)
                    dve.wait_ge(pr_dve, n)
                dve.reciprocal(rden[:, :], den[:, :]).then_inc(rden_ready, 1)
                dve.wait_ge(rden_ready, n + 1)
                dve.tensor_tensor(pr[:, i, 0:HV, :], pr[:, i, 0:HV, :],
                                  rden[:, :].unsqueeze(1).to_broadcast([P, HV, P]), ALU.mult).then_inc(pr_dve, 1)

            def step_y(j):
                dve.wait_ge(y_ps, j + 1)
                dve.tensor_tensor(upd[:, 0, :], ps_a[:, 0, :], bo[:, :], ALU.add).then_inc(upd_ready, 1)
                dve.wait_ge(upd_ready, j + 1)
                keep_rows(dve, kit, bass.ds(j, 1), upd, xnew, stats, aggr, x_ready, j)

            normalize(0)
            step_v(0, 0, ps_a)

            def body(b, par, first, last):
                for i in range(U):
                    maxima(b, i)
                    if i == 0 and not last:
                        normalize(b + 1)
                    if i == 0 and not first:
                        step_y(2 * b - 2)
                    if i == 2 and not first:
                        step_y(2 * b - 1)
                    if i == 2 and not last:
                        step_v(b + 1, 1 - par, ps_b)
                    if not first or i > 0:
                        probabilities(b * U + i - 1, (i - 1) % U, par)

            batches(dve, body)
            probabilities(B * U - 1, U - 1, 1)
            step_y(2 * B - 2)
            step_y(2 * B - 1)

        @block.tensor
        def _(pe):
            pe.wait_ge(setup, 3)
            pe.wait_ge(w_in, 64)

            def product(out, lhsT, rhs, n):
                for c in range(n):
                    last = pe.matmul(out, lhsT(c), rhs(c), start=c == 0, stop=c == n - 1)
                return last

            def step_xnT(b):
                pe.wait_ge(xn_ready, b + 1)
                for c in range(KC):
                    for t in range(QT):
                        last = pe.transpose(ps_b[:, c, P * t:P * (t + 1)], xn[:, t, P * c:P * (c + 1)], kit.ident[:, :])
                last.then_inc(xnT_ps, 1)

            def step_k(b, par):
                pe.wait_ge(ctx_in[par], (b - par) * 8 + 16)
                for m in range(KC):
                    last = product(ps_a[:, m, :], lambda c: wk[:, c, P * m:P * (m + 1)], lambda c: ctxT[:, par, c, :], KC)
                last.then_inc(k_ps, 1)

            def step_q(b):
                pe.wait_ge(xnT_ready, b + 1)
                for m in range(KC):
                    last = product(ps_b[:, m, :], lambda c: wq[:, c, P * m:P * (m + 1)], lambda c: xnT[:, c, :], KC)
                last.then_inc(q_ps, 1)

            def step_v(b, par, ps):
                for t in range(QT):
                    last = product(ps[:, t, :], lambda c: ctxT[:, par, c, P * t:P * (t + 1)], lambda c: wv[:, c, :], KC)
                last.then_inc(v_ps, 1)

            def step_y(j):
                pe.wait_ge(oT_ready, j + 1)
                product(ps_a[:, 0, :], lambda g: oT[:, g, :], lambda g: wo[:, g, :], H // G).then_inc(y_ps, 1)

            def scores(b, i, par):
                t, k = i // QT, i % QT
                n = b * U + i
                if i == 0:
                    pe.wait_ge(q_ready, b + 1)
                    pe.wait_ge(kh_ready, 2 * b + 2)
                for h in range(H):
                    if h % HALF == 0 and (not isinstance(b, int) or n > 0):
                        pe.wait_ge(e_ready, 2 * n - 1 + h // HALF)
                    c = h // HC
                    last = pe.matmul(ps_s[:, h, :], kTh[:, par, h, P * k:P * (k + 1)], qT[:, par, c, P * t:P * (t + 1)],
                                     start=h % G == 0, stop=False, skip_group_check=True)
                    if h % HALF == HALF - 1:
                        last.then_inc(s_ps, 1)

            def shift(b, i):
                n = b * U + i
                pe.wait_ge(max_ready, n + 1)
                for g in range(HB):
                    last = pe.matmul(ps_s[:, G * g:G * (g + 1), :], minus_i[:, :],
                                     mxb[:, :].unsqueeze(1).to_broadcast([P, G, P]),
                                     start=False, stop=True, skip_group_check=True)
                last.then_inc(shifted, 1)

            def values(b, i, par):
                k = i % QT
                n = b * U + i
                if i == 0:
                    pe.wait_ge(v_ready, b + 1)
                if k == 0 and (not isinstance(b, int) or n > 0):
                    pe.wait_ge(oT_ready, 2 * b + i // QT)
                pe.wait_ge(pr_dve, n + 1)
                pe.wait_ge(pr_pool, n + 1)
                for h in range(H):
                    j = 2 * DK * (h % G)
                    last = pe.matmul(ps_o[j:j + 2 * DK, h // G, :], va[:, par, k, h, :], pr[:, i, h, :],
                                     start=k == 0 and h < G, stop=k == QT - 1, skip_group_check=True)
                last.then_inc(pv_done, 1)

            step_xnT(0)
            step_k(0, 0)
            step_q(0)
            pe.wait_ge(k_ready, 1)
            step_v(0, 0, ps_a)
            scores(0, 0, 0)

            def body(b, par, first, last):
                for i in range(U):
                    if i == 0 and not first:
                        pe.wait_ge(k_ready, b + 1)
                        step_y(2 * b - 2)
                    if i == 0 and not last:
                        if not first:
                            pe.wait_ge(v_ready, b + 1)
                        else:
                            pe.wait_ge(q_ready, 1)
                        step_xnT(b + 1)
                    if i == 1 and not last:
                        if not first:
                            pe.wait_ge(upd_ready, 2 * b - 1)
                        else:
                            pe.wait_ge(v_ready, 1)
                        step_k(b + 1, 1 - par)
                        step_q(b + 1)
                    if i == 2 and not first:
                        pe.wait_ge(k_ready, b + 2 if not last else b + 1)
                        pe.wait_ge(upd_ready, 2 * b - 1)
                        step_y(2 * b - 1)
                    if i == 2 and not last:
                        pe.wait_ge(q_ready, b + 2)
                        step_v(b + 1, 1 - par, ps_b)
                    shift(b, i)
                    if i >= 2:
                        values(b, i - 2, par)
                    elif not first:
                        values(b - 1, i + 2, 1 - par)
                    if i < U - 1:
                        scores(b, i + 1, par)
                    elif not last:
                        scores(b + 1, 0, 1 - par)

            batches(pe, body)
            values(B - 1, 2, 1)
            values(B - 1, 3, 1)
            pe.wait_ge(upd_ready, 2 * B - 3)
            step_y(2 * B - 2)
            pe.wait_ge(upd_ready, 2 * B - 1)
            step_y(2 * B - 1)


def route(nc, kit, d):
    PAIR = 2
    NJ = NT // PAIR
    with ExitStack() as ctx:
        def sb(name, shape, dt=F32):
            return ctx.enter_context(nc.sbuf_tensor("r_" + name, shape, dt))

        def sem(name):
            return ctx.enter_context(nc.semaphore("r_" + name))

        wr, br = sb("wr", [P, KC, E]), sb("br", [P, E])
        order = sb("order", [P, E])
        tile_no = sb("tile_no", [P, SLOT_TILES])
        before = sb("before", [P, P])
        before_b, ones_b = sb("before_b", [P, P], BF16), sb("ones_b", [P, P], BF16)
        ones = sb("ones", [P, NT])
        rstd = sb("rstd", [P, 2, NT])
        xn = sb("xn", [P, 2, PAIR, D])
        xnT = sb("xnT", [P, KC, PAIR * P])
        lg = sb("lg", [P, NT, E])
        low, hit = sb("low", [P, NT, E]), sb("hit", [P, NT, E])
        top = sb("top", [P, 2, NT])
        first_at = sb("first_at", [P, NT])
        one_hot = sb("one_hot", [P, 2, NT, E])
        taken = sb("taken", [P, NT, E], BF16)
        ex = sb("ex", [P, NT])
        rank, total, upto = sb("rank", [P, NT, E]), sb("total", [P, NT, E]), sb("upto", [P, NT, E])
        tiles_i, tiles_f = sb("tiles_i", [P, E], I32), sb("tiles_f", [P, E])
        upto_e, start_e = sb("upto_e", [P, E]), sb("start_e", [P, E])
        slot_f = sb("slot_f", [P, NT])
        past = sb("past", [P, SLOT_TILES, E])
        past_n = sb("past_n", [P, SLOT_TILES])
        ps_x = ctx.enter_context(nc.psum_tensor("r_ps_x", [P, KC, PAIR * P], F32))
        ps_l = ctx.enter_context(nc.psum_tensor("r_ps_l", [P, PAIR, E], F32))
        ps_r = ctx.enter_context(nc.psum_tensor("r_ps_r", [P, NT * E], F32))
        ps_n = ctx.enter_context(nc.psum_tensor("r_ps_n", [P, NT * E], F32))

        misc_in, x_saved = sem("misc_in"), [sem(f"x_saved{i}") for i in range(4)]
        setup, sd_ready = sem("setup"), sem("sd_ready")
        xn_ready, xn_kept, x_ps, xnT_ready = sem("xn_ready"), sem("xn_kept"), sem("x_ps"), sem("xnT_ready")
        l_ps, lg_ready = sem("l_ps"), sem("lg_ready")
        pick = sem("pick")
        ex_ready, taken_ready, counts_ps, place = sem("ex_ready"), sem("taken_ready"), sem("counts_ps"), sem("place")
        moved = sem("moved")
        block = ctx.enter_context(nc.Block())

        n4 = NT // 4

        @block.sync
        def _(sp):
            for i in range(4):
                sp.dma_start(kit.x_d[P * n4 * i:P * n4 * (i + 1), :].rearrange("(t p) c -> p t c", p=P),
                             kit.x[:, n4 * i:n4 * (i + 1), :]).then_inc(x_saved[i], 16)
            for e in range(E):
                sp.dma_start(kit.w1[:, e, :, :], d["w1"][e].rearrange("(c p) f -> p c f", p=P)).then_inc(kit.w_in, 16)
                sp.dma_start(kit.w2[:, e, :, :], d["w2"][e].rearrange("(f p) n -> p f n", p=P)).then_inc(kit.w_in, 16)
            for buf, n in ((kit.b1, "b1"), (kit.b2, "b2")):
                sp.dma_start(buf[:, :, :], d[n]).then_inc(kit.w_in, 16)
            sp.wait_ge(kit.w_in, 16 * (2 * E + 2))
            for i in range(4):
                sp.wait_ge(x_saved[i], 16)

        @block.scalar
        def _(act):
            act.dma_start(wr[:, :, :], d["wr"].rearrange("(c p) e -> p c e", p=P)).then_inc(misc_in, 16)
            for buf, n in ((br, "br"), (order, "order"), (tile_no, "tile_no"), (before, "before")):
                act.dma_start(buf[:, :], d[n]).then_inc(misc_in, 16)
            act.wait_ge(setup, 1)
            act.activation(rstd[:, 1, :], rstd[:, 0, :], ACT.Sqrt).then_inc(sd_ready, 1)
            act.wait_ge(misc_in, 16 * 5)

            with act.Fori(0, NJ) as j:
                act.wait_ge(x_ps, j + 1)
                act.activation(xnT[:, :, :], ps_x[:, :, :], ACT.Copy).then_inc(xnT_ready, 1)
            act.wait_ge(pick, 8)
            act.activation(ex[:, :], first_at[:, :], ACT.Exp).then_inc(ex_ready, 1)

        @block.vector
        def _(dve):
            dve.tensor_scalar(rstd[:, 0, :], kit.mv[:, :, 1], EPS, None, ALU.add).then_inc(setup, 1)
            dve.wait_ge(misc_in, 16 * 5)
            dve.tensor_copy(before_b[:, :], before[:, :]).then_inc(setup, 1)
            dve.memset(ones_b[:, :], 1.0).then_inc(setup, 1)
            dve.memset(ones[:, :], 1.0).then_inc(setup, 1)
            dve.wait_ge(sd_ready, 1)
            dve.reciprocal(rstd[:, 0, :], rstd[:, 1, :]).then_inc(setup, 1)
            dve.wait_ge(setup, 5)

            def rows(j, par):
                for t in range(PAIR):
                    last = dve.tensor_scalar(xn[:, par, t, :], kit.x[:, PAIR * j + t, :], kit.mv[:, PAIR * j + t, 0:1],
                                             rstd[:, 0, bass.ds(PAIR * j + t, 1)], ALU.subtract, ALU.mult)
                last.then_inc(xn_ready, 1)
                dve.wait_ge(xn_ready, j + 1)
                dve.tensor_scalar(kit.x[:, bass.ds(PAIR * j, PAIR), :], xn[:, par, :, :], 1.0, None, ALU.mult).then_inc(xn_kept, 1)

            for i in range(4):
                dve.wait_ge(x_saved[i], 16)
            rows(0, 0)

            def logits(j):
                dve.wait_ge(l_ps, j + 1)
                dve.tensor_tensor(lg[:, bass.ds(PAIR * j, PAIR), :], ps_l[:, :, :],
                                  br[:, :].unsqueeze(1).to_broadcast([P, PAIR, E]), ALU.add).then_inc(lg_ready, 1)

            rows(1, 1)
            logits(0)
            with dve.Fori(2, NJ - 1, 2) as j:
                dve.wait_ge(x_ps, j - 1)
                rows(j, 0)
                logits(j - 1)
                dve.wait_ge(x_ps, j)
                rows(j + 1, 1)
                logits(j)
            logits(NJ - 1)
            dve.wait_ge(lg_ready, NJ)
            dve.wait_ge(xn_kept, NJ)

            every = [P, NT, E]
            order_b = order[:, :].unsqueeze(1).to_broadcast(every)

            def spread(v):
                return v.unsqueeze(2).to_broadcast(every)

            for i in range(2):
                of = low if i else lg
                dve.tensor_reduce(top[:, i, :], of[:, :, :], AX.X, ALU.max).then_inc(pick, 1)
                dve.wait_ge(pick, 4 * i + 1)
                dve.tensor_tensor(hit[:, :, :], of[:, :, :], spread(top[:, i, :]), ALU.is_equal).then_inc(pick, 1)
                dve.wait_ge(pick, 4 * i + 2)
                dve.tensor_tensor(hit[:, :, :], hit[:, :, :], order_b, ALU.mult).then_inc(pick, 1)
                dve.wait_ge(pick, 4 * i + 3)
                dve.tensor_reduce(first_at[:, :], hit[:, :, :], AX.X, ALU.min).then_inc(place, 1)
                dve.wait_ge(place, 3 * i + 1)
                dve.tensor_tensor(one_hot[:, i, :, :], order_b, spread(first_at[:, :]), ALU.is_equal).then_inc(place, 1)
                dve.wait_ge(place, 3 * i + 2)
                if i == 0:
                    dve.tensor_scalar(low[:, :, :], one_hot[:, 0, :, :], -3e38, None, ALU.mult).then_inc(place, 1)
                    dve.wait_ge(place, 3)
                    dve.tensor_tensor(low[:, :, :], low[:, :, :], lg[:, :, :], ALU.add).then_inc(pick, 1)
                    dve.wait_ge(pick, 4)
                else:
                    dve.tensor_tensor(taken[:, :, :], one_hot[:, 0, :, :], one_hot[:, 1, :, :], ALU.add).then_inc(taken_ready, 1)
                    dve.tensor_tensor(first_at[:, :], top[:, 1, :], top[:, 0, :], ALU.subtract).then_inc(pick, 1)
            dve.wait_ge(ex_ready, 1)
            dve.tensor_scalar(top[:, 0, :], ex[:, :], 1.0, None, ALU.add).then_inc(pick, 1)
            dve.wait_ge(pick, 9)
            dve.reciprocal(kit.gate[:, 0, :], top[:, 0, :]).then_inc(pick, 1)
            dve.wait_ge(pick, 10)
            dve.tensor_tensor(kit.gate[:, 1, :], kit.gate[:, 0, :], ex[:, :], ALU.mult).then_inc(pick, 1)
            dve.wait_ge(counts_ps, 1)
            dve.tensor_copy(rank[:, :, :], ps_r[:, :].rearrange("p (t e) -> p t e", e=E)).then_inc(place, 1)
            dve.tensor_copy(total[:, :, :], ps_n[:, :].rearrange("p (t e) -> p t e", e=E)).then_inc(place, 1)
            dve.wait_ge(place, 7)
            for e in range(E):
                last = dve.tensor_tensor_scan(upto[:, :, e], ones[:, :], total[:, :, e], 0.0, ALU.mult, ALU.add)
            last.then_inc(place, 1)
            dve.wait_ge(place, 8)
            dve.tensor_tensor(rank[:, :, :], rank[:, :, :], upto[:, :, :], ALU.add).then_inc(place, 1)
            dve.tensor_scalar(tiles_i[:, :], upto[:, NT - 1, :], float(P - 1), None, ALU.add).then_inc(place, 1)
            dve.wait_ge(place, 10)
            dve.tensor_tensor(rank[:, :, :], rank[:, :, :], total[:, :, :], ALU.subtract).then_inc(place, 1)
            dve.tensor_scalar(tiles_i[:, :], tiles_i[:, :], P.bit_length() - 1, None, ALU.logical_shift_right).then_inc(place, 1)
            dve.wait_ge(place, 12)
            dve.tensor_copy(tiles_f[:, :], tiles_i[:, :]).then_inc(place, 1)
            dve.wait_ge(place, 13)
            dve.tensor_tensor_scan(upto_e[:, :], ones[:, 0:E], tiles_f[:, :], 0.0, ALU.mult, ALU.add).then_inc(place, 1)
            dve.wait_ge(place, 14)
            dve.tensor_tensor(start_e[:, :], upto_e[:, :], tiles_f[:, :], ALU.subtract).then_inc(place, 1)
            dve.wait_ge(place, 15)
            dve.tensor_scalar(start_e[:, :], start_e[:, :], float(P), None, ALU.mult).then_inc(place, 1)
            dve.wait_ge(place, 16)
            dve.tensor_tensor(rank[:, :, :], rank[:, :, :], start_e[:, :].unsqueeze(1).to_broadcast(every), ALU.add)\
                .then_inc(place, 1)
            dve.wait_ge(place, 17)
            for i in range(2):
                dve.tensor_tensor(hit[:, :, :], one_hot[:, i, :, :], rank[:, :, :], ALU.mult).then_inc(place, 1)
                dve.wait_ge(place, 18 + 3 * i)
                dve.tensor_reduce(slot_f[:, :], hit[:, :, :], AX.X, ALU.add).then_inc(place, 1)
                dve.wait_ge(place, 19 + 3 * i)
                dve.tensor_copy(kit.slot[:, i, :], slot_f[:, :]).then_inc(place, 1)
                dve.wait_ge(place, 20 + 3 * i)
            whole = [P, SLOT_TILES, E]
            dve.tensor_tensor(past[:, :, :], tile_no[:, :].unsqueeze(2).to_broadcast(whole),
                              upto_e[:, :].unsqueeze(1).to_broadcast(whole), ALU.is_ge).then_inc(place, 1)
            dve.wait_ge(place, 24)
            dve.tensor_reduce(past_n[:, :], past[:, :, :], AX.X, ALU.add).then_inc(place, 1)
            dve.wait_ge(place, 25)
            dve.tensor_scalar(kit.expert[:, :], past_n[:, :], float(E - 1), None, ALU.min).then_inc(place, 1)
            dve.wait_ge(place, 26)

        @block.gpsimd
        def _(pool):
            pool.wait_ge(place, 23)
            for i in range(2):
                for t in range(NT):
                    pool.indirect_dma_start(out=kit.sorted_d, out_offset=bass.IndirectOffsetOnAxis(ap=kit.slot[:, i, t:t + 1], axis=0),
                                            in_=kit.x[:, t, :], in_offset=None).then_inc(moved, 16)
            pool.wait_ge(moved, 16 * 2 * NT)

        @block.tensor
        def _(pe):
            pe.wait_ge(misc_in, 16 * 5)

            def turn(j, par):
                pe.wait_ge(xn_ready, j + 1)
                for c in range(KC):
                    for t in range(PAIR):
                        last = pe.transpose(ps_x[:, c, P * t:P * (t + 1)], xn[:, par, t, P * c:P * (c + 1)], kit.ident[:, :])
                last.then_inc(x_ps, 1)

            def logits(j):
                pe.wait_ge(xnT_ready, j + 1)
                if not isinstance(j, int) or j > 0:
                    pe.wait_ge(lg_ready, j)
                for t in range(PAIR):
                    for c in range(KC):
                        last = pe.matmul(ps_l[:, t, :], xnT[:, c, P * t:P * (t + 1)], wr[:, c, :],
                                         start=c == 0, stop=c == KC - 1)
                last.then_inc(l_ps, 1)

            turn(0, 0)
            logits(0)
            with pe.Fori(1, NJ - 2, 2) as j:
                turn(j, 1)
                logits(j)
                turn(j + 1, 0)
                logits(j + 1)
            turn(NJ - 1, 1)
            logits(NJ - 1)
            pe.wait_ge(taken_ready, 1)
            pe.wait_ge(setup, 3)
            flat = taken[:, :, :].rearrange("p t e -> p (t e)")
            pe.matmul(ps_r[:, :], before_b[:, :], flat, start=True, stop=True)
            pe.matmul(ps_n[:, :], ones_b[:, :], flat, start=True, stop=True).then_inc(counts_ps, 1)


def experts(nc, kit, d):
    T = SLOT_TILES
    HF = FF // 2
    with ExitStack() as ctx:
        def sb(name, shape, dt=F32):
            return ctx.enter_context(nc.sbuf_tensor("e_" + name, shape, dt))

        def sem(name):
            return ctx.enter_context(nc.semaphore("e_" + name))

        rows = sb("rows", [P, 2, D])
        rowsT = sb("rowsT", [P, 2, KC, P])
        h = sb("h", [P, 2, FF])
        hT = sb("hT", [P, 2, FC, P])
        y = sb("y", [P, 2, D])
        ps_x = ctx.enter_context(nc.psum_tensor("e_ps_x", [P, KC, P], F32))
        ps_h = ctx.enter_context(nc.psum_tensor("e_ps_h", [P, 2, HF], F32))
        ps_t = ctx.enter_context(nc.psum_tensor("e_ps_t", [P, FC, P], F32))
        ps_y = ctx.enter_context(nc.psum_tensor("e_ps_y", [P, D], F32))

        rows_in, y_out = [sem("rows_in0"), sem("rows_in1")], [sem("y_out0"), sem("y_out1")]
        x_ps, rowsT_ready, h_ps, h_ready = sem("x_ps"), sem("rowsT_ready"), sem("h_ps"), sem("h_ready")
        t_ps, hT_ready, y_ps, y_ready = sem("t_ps"), sem("hT_ready"), sem("y_ps"), sem("y_ready")
        block = ctx.enter_context(nc.Block())

        def expert_of(eng, j):
            return eng.value_load(kit.expert[0:1, bass.ds(j, 1)], min_val=0, max_val=E - 1)

        @block.sync
        def _(sp):
            def load(j, par):
                sp.dma_start(rows[:, par, :], kit.sorted_d[bass.ds(j * P, P), :]).then_inc(rows_in[par], 16)

            def store(j, par):
                sp.wait_ge(y_ready, j + 1)
                sp.dma_start(kit.outs_d[bass.ds(j * P, P), :], y[:, par, :]).then_inc(y_out[par], 16)

            load(0, 0)
            load(1, 1)
            sp.wait_ge(x_ps, 1)
            load(2, 0)
            sp.wait_ge(x_ps, 2)
            load(3, 1)
            with sp.Fori(4, T - 1, 2) as j:
                sp.wait_ge(x_ps, j - 1)
                load(j, 0)
                store(j - 4, 0)
                sp.wait_ge(x_ps, j)
                load(j + 1, 1)
                store(j - 3, 1)
            for j in range(T - 4, T):
                store(j, j % 2)
            sp.wait_ge(y_out[0], 8 * T)
            sp.wait_ge(y_out[1], 8 * T)

        @block.scalar
        def _(act):
            def take_rows(j, par):
                act.wait_ge(x_ps, j + 1)
                act.activation(rowsT[:, par, :, :], ps_x[:, :, :], ACT.Copy).then_inc(rowsT_ready, 1)

            def hidden(j, par):
                act.wait_ge(t_ps, j + 1)
                e = expert_of(act, j)
                for f in range(FC):
                    last = act.activation(hT[:, par, f, :], ps_t[:, f, :], ACT.Relu, bias=kit.b1[:, e, f:f + 1])
                last.then_inc(hT_ready, 1)

            take_rows(0, 0)
            take_rows(1, 1)
            take_rows(2, 0)
            hidden(0, 0)
            with act.Fori(1, T - 4, 2) as j:
                take_rows(j + 2, 1)
                hidden(j, 1)
                take_rows(j + 3, 0)
                hidden(j + 1, 0)
            take_rows(T - 1, 1)
            hidden(T - 3, 1)
            hidden(T - 2, 0)
            hidden(T - 1, 1)

        @block.vector
        def _(dve):
            def inner(j, par):
                for half in range(2):
                    dve.wait_ge(h_ps, 2 * j + half + 1)
                    dve.tensor_copy(h[:, par, HF * half:HF * (half + 1)], ps_h[:, half, :]).then_inc(h_ready, 1)

            def outer(j, par, first):
                dve.wait_ge(y_ps, j + 1)
                if not first:
                    dve.wait_ge(y_out[par], (j - par) * 8)
                e = expert_of(dve, j)
                dve.tensor_tensor(y[:, par, :], ps_y[:, :], kit.b2[:, e, :], ALU.add).then_inc(y_ready, 1)

            inner(0, 0)
            inner(1, 1)
            inner(2, 0)
            outer(0, 0, True)
            inner(3, 1)
            outer(1, 1, True)
            with dve.Fori(2, T - 3, 2) as j:
                inner(j + 2, 0)
                outer(j, 0, False)
                inner(j + 3, 1)
                outer(j + 1, 1, False)
            outer(T - 2, 0, False)
            outer(T - 1, 1, False)

        @block.tensor
        def _(pe):
            def turn_rows(j, par):
                pe.wait_ge(rows_in[par], (j - par) * 8 + 16)
                if not isinstance(j, int) or j > 0:
                    pe.wait_ge(rowsT_ready, j)
                for c in range(KC):
                    last = pe.transpose(ps_x[:, c, :], rows[:, par, P * c:P * (c + 1)], kit.ident[:, :])
                last.then_inc(x_ps, 1)

            def inner(j, par):
                pe.wait_ge(rowsT_ready, j + 1)
                e = expert_of(pe, j)
                for half in range(2):
                    if not isinstance(j, int) or j > 0:
                        pe.wait_ge(h_ready, 2 * j - 1 + half)
                    for c in range(KC):
                        last = pe.matmul(ps_h[:, half, :], rowsT[:, par, c, :],
                                         kit.w1[:, e, c, HF * half:HF * (half + 1)], start=c == 0, stop=c == KC - 1)
                    last.then_inc(h_ps, 1)

            def turn_hidden(j, par):
                pe.wait_ge(h_ready, 2 * j + 2)
                if not isinstance(j, int) or j > 0:
                    pe.wait_ge(hT_ready, j)
                for f in range(FC):
                    last = pe.transpose(ps_t[:, f, :], h[:, par, P * f:P * (f + 1)], kit.ident[:, :])
                last.then_inc(t_ps, 1)

            def outer(j, par):
                pe.wait_ge(hT_ready, j + 1)
                if not isinstance(j, int) or j > 0:
                    pe.wait_ge(y_ready, j)
                e = expert_of(pe, j)
                for f in range(FC):
                    last = pe.matmul(ps_y[:, :], hT[:, par, f, :], kit.w2[:, e, f, :], start=f == 0, stop=f == FC - 1)
                last.then_inc(y_ps, 1)

            turn_rows(0, 0)
            turn_rows(1, 1)
            inner(0, 0)
            inner(1, 1)
            turn_rows(2, 0)
            turn_hidden(0, 0)
            with pe.Fori(1, T - 4, 2) as j:
                for i, par in ((0, 1), (1, 0)):
                    inner(j + i + 1, 1 - par)
                    turn_rows(j + i + 2, par)
                    outer(j + i - 1, 1 - par)
                    turn_hidden(j + i, par)
            inner(T - 2, 0)
            turn_rows(T - 1, 1)
            outer(T - 4, 0)
            turn_hidden(T - 3, 1)
            inner(T - 1, 1)
            outer(T - 3, 1)
            turn_hidden(T - 2, 0)
            outer(T - 2, 0)
            turn_hidden(T - 1, 1)
            outer(T - 1, 1)


def combine(nc, kit, out):
    N = 4
    with ExitStack() as ctx:
        x = kit.x
        y = ctx.enter_context(nc.sbuf_tensor("f_y", [P, N, 2, D], F32))
        x_in = [ctx.enter_context(nc.semaphore(f"f_x_in{i}")) for i in range(4)]
        y_in = [ctx.enter_context(nc.semaphore(f"f_y_in{i}")) for i in range(N)]
        half_sum, row_sum, stored = (ctx.enter_context(nc.semaphore("f_" + n)) for n in ("half_sum", "row_sum", "stored"))
        block = ctx.enter_context(nc.Block())
        n4 = NT // 4

        @block.sync
        def _(sp):
            for i in range(4):
                sp.dma_start(x[:, n4 * i:n4 * (i + 1), :],
                             kit.x_d[P * n4 * i:P * n4 * (i + 1), :].rearrange("(t p) c -> p t c", p=P)).then_inc(x_in[i], 16)
            for i in range(8):
                sp.wait_ge(row_sum, 4 * (i + 1))
                sp.dma_start(out[P * 4 * i:P * 4 * (i + 1), :].rearrange("(t p) c -> p t c", p=P),
                             x[:, 4 * i:4 * (i + 1), :]).then_inc(stored, 16)
            sp.wait_ge(stored, 16 * 8)

        @block.gpsimd
        def _(pool):
            for t in range(NT):
                if t >= N:
                    pool.wait_ge(row_sum, t - N + 1)
                for i in range(2):
                    pool.indirect_dma_start(out=y[:, t % N, i, :], out_offset=None, in_=kit.outs_d,
                                            in_offset=bass.IndirectOffsetOnAxis(ap=kit.slot[:, i, t:t + 1], axis=0))\
                        .then_inc(y_in[t % N], 16)

        @block.vector
        def _(dve):
            for t in range(NT):
                if t % n4 == 0:
                    dve.wait_ge(x_in[t // n4], 16)
                dve.wait_ge(y_in[t % N], 32 * (t // N + 1))
                for i in range(2):
                    dve.scalar_tensor_tensor(out=x[:, t, :], in0=y[:, t % N, i, :], scalar=kit.gate[:, i, t:t + 1],
                                             in1=x[:, t, :], op0=ALU.mult, op1=ALU.add).then_inc((half_sum, row_sum)[i], 1)
                    if i == 0:
                        dve.wait_ge(half_sum, t + 1)


def network(nc, d, out):
    with ExitStack() as ctx:
        kit = Kit()
        kit.x = ctx.enter_context(nc.sbuf_tensor("x_rows", [P, NT, D], F32))
        kit.mv = ctx.enter_context(nc.sbuf_tensor("mean_var", [P, NT, 2], F32))
        kit.ident = ctx.enter_context(nc.sbuf_tensor("identity", [P, P], F32))
        kit.ident_d = d["ident"]
        kit.sorted_d = nc.dram_tensor("sorted_rows", [SLOT_TILES * P, D], F32, kind="Internal").ap()
        kit.outs_d = nc.dram_tensor("expert_rows", [SLOT_TILES * P, D], F32, kind="Internal").ap()
        kit.x_d = nc.dram_tensor("x_waiting", [NT * P, D], F32, kind="Internal").ap()

        def of(prefix):
            return {k[len(prefix):]: v for k, v in d.items() if k.startswith(prefix)} | \
                {k: d[k] for k in ("ctxT", "head_of", "mask")}

        load_x(nc, kit, d["x"])
        attend_keys(nc, kit, of("A_"))
        channel_mix(nc, kit, of("B_"))
        attend_heads(nc, kit, of("C_"))
        with ExitStack() as moe:
            kit.w1 = moe.enter_context(nc.sbuf_tensor("w1", [P, E, KC, FF], F32))
            kit.w2 = moe.enter_context(nc.sbuf_tensor("w2", [P, E, FC, D], F32))
            kit.b1 = moe.enter_context(nc.sbuf_tensor("b1", [P, E, FC], F32))
            kit.b2 = moe.enter_context(nc.sbuf_tensor("b2", [P, E, D], F32))
            kit.gate = moe.enter_context(nc.sbuf_tensor("gate", [P, 2, NT], F32))
            kit.slot = moe.enter_context(nc.sbuf_tensor("slot", [P, 2, NT], U32))
            kit.expert = moe.enter_context(nc.sbuf_tensor("expert", [P, SLOT_TILES], I32))
            kit.w_in = moe.enter_context(nc.semaphore("w_in"))
            route(nc, kit, of("D_"))
            experts(nc, kit, of("D_"))
            combine(nc, kit, out)


def kernel(**inputs):
    from concourse import bacc
    from concourse.bass_utils import run_bass_kernel_spmd

    def turned(w):
        return np.ascontiguousarray(w.T)

    def columns(v):
        return np.ascontiguousarray(v.reshape(-1, P).T)

    def to_all(v):
        return np.ascontiguousarray(np.broadcast_to(v, (P,) + v.shape))

    z = {k: np.asarray(v) for k, v in inputs.items()}
    a = {"x": z["x"].reshape(B * S, D), "ctxT": turned(z["ctx_1024"].reshape(B * S, D)),
         "mask": z["mask_1x1xSxS2_ik0"].reshape(S, S), "ident": np.eye(P, dtype=np.float32),
         "head_of": np.repeat(np.eye(HC, dtype=np.float32), DK, 0)}
    for to, p in (("A_", "L0_xattn_"), ("C_", "L1_xattn_")):
        for w in "qkvo":
            a[f"{to}w{w}T"] = turned(z[f"{p}W{w}"])
        for b in "qk":
            a[f"{to}b{b}"] = columns(z[f"{p}b{b}"])
        for b in "vo":
            a[f"{to}b{b}"] = to_all(z[f"{p}b{b}"])
    spaced = np.zeros((H, 2 * DK, D), np.float32)
    spaced[:, :DK] = a["C_woT"].reshape(H, DK, D)
    a["C_woT"] = spaced.reshape(2 * D, D)
    for w in "rkv":
        a[f"B_w{w}T"] = turned(z[f"L0_ffn_W_{w}"])
    for m in "rk":
        a[f"B_mu_{m}"] = columns(z[f"L0_ffn_mu_{m}"])
    a["D_w1"], a["D_w2"] = z["L1_ffn_W1"], z["L1_ffn_W2"]
    a["D_b1"] = np.ascontiguousarray(z["L1_ffn_b1"].reshape(E, FC, P).transpose(2, 0, 1))
    a["D_b2"] = to_all(z["L1_ffn_b2"])
    a["D_wr"], a["D_br"] = z["L1_ffn_router_w"], to_all(z["L1_ffn_router_b"])
    a["D_order"] = to_all(np.arange(-E, 0, dtype=np.float32))
    a["D_tile_no"] = to_all(np.arange(SLOT_TILES, dtype=np.float32))
    a["D_before"] = np.triu(np.ones((P, P), np.float32), 1)

    nc = bacc.Bacc("TRN2", target_bir_lowering=False, num_devices=1)
    d = {k: nc.dram_tensor("in_" + k, v.shape, mybir.dt.from_np(v.dtype), kind="ExternalInput").ap() for k, v in a.items()}
    out = nc.dram_tensor("out", [B * S, D], F32, kind="ExternalOutput").ap()
    network(nc, d, out)
    r = run_bass_kernel_spmd(nc, [{"in_" + k: v for k, v in a.items()}], core_ids=[0])
    return r.results[0]["out"].reshape(B, S, D)
```

```python
from contextlib import ExitStack

import numpy as np

import concourse.bass as bass
from concourse import mybir

F32 = mybir.dt.float32
BF16 = mybir.dt.bfloat16
F32R = mybir.dt.float32r
I32 = mybir.dt.int32
U32 = mybir.dt.uint32
ALU = mybir.AluOpType
ACT = mybir.ActivationFunctionType
AX = mybir.AxisListType

P = 128
B, S, D = 16, 256, 256
H = 16
DK = D // H
QT = S // P
NT = B * QT
KC = D // P
HC = P // DK
G = 4
E, FF = 8, 1024
FC = FF // P
R = 2 * P
RT = R // P
SLOT_TILES = (2 * B * S + E * (R - 1)) // R
Q_PART, K_PART = (0, 1, 2, 0, 1, 0), (0, 0, 0, 1, 1, 2)
PAIRS = len(Q_PART)
SCALE = DK ** -0.5
EPS = 1e-5
MASKED = -1e30


class Kit:
    pass


def load_x(nc, kit, x):
    with ExitStack() as ctx:
        x_in = [ctx.enter_context(nc.semaphore(f"x_in{i}")) for i in range(4)]
        const_in = ctx.enter_context(nc.semaphore("const_in"))
        part_stats = ctx.enter_context(nc.semaphore("part_stats"))
        stats = ctx.enter_context(nc.sbuf_tensor("stats0", [P, NT, 6], F32))
        block = ctx.enter_context(nc.Block())
        n = NT // 4

        @block.sync
        def _(sp):
            for i in range(4):
                sp.dma_start(kit.x[:, n * i:n * (i + 1), :],
                             x[P * n * i:P * n * (i + 1), :].rearrange("(t p) c -> p t c", p=P)).then_inc(x_in[i], 16)

        @block.scalar
        def _(act):
            act.dma_start(kit.ident[:, :], kit.ident_d).then_inc(const_in, 16)
            act.wait_ge(const_in, 16)

        @block.vector
        def _(dve):
            for t in range(NT):
                if t % n == 0:
                    dve.wait_ge(x_in[t // n], 16)
                dve.bn_stats(stats[:, t, :], kit.x[:, t, :]).then_inc(part_stats, 1)
            for t in range(NT):
                dve.wait_ge(part_stats, t + 1)
                last = dve.bn_aggr(kit.mv[:, t, :], stats[:, t, :])
            last.then_inc(part_stats, 1)
            dve.wait_ge(part_stats, NT + 1)


def keep_rows(dve, kit, tiles, upd, xnew, stats, aggr, x_ready, i):
    n = upd.shape[1]
    dve.tensor_tensor(xnew[:, :, :], kit.x[:, tiles, :], upd[:, :, :], ALU.add).then_inc(x_ready, 1)
    dve.wait_ge(x_ready, 3 * i + 1)
    for t in range(n):
        last = dve.bn_stats(stats[:, t, :], xnew[:, t, :])
    last.then_inc(x_ready, 1)
    dve.wait_ge(x_ready, 3 * i + 2)
    dve.tensor_scalar(kit.x[:, tiles, :], xnew[:, :, :], 1.0, None, ALU.mult)
    for t in range(n):
        last = dve.bn_aggr(aggr[:, t, :], stats[:, t, :])
    last.then_inc(x_ready, 1)
    dve.wait_ge(x_ready, 3 * i + 3)
    dve.tensor_scalar(kit.mv[:, tiles, :], aggr[:, :, :], 1.0, None, ALU.mult)


class Split:

    def __init__(self, nc, ctx, name, parts_d, part_of_pair, zero=None):
        def sb(n, shape, dt=BF16):
            return ctx.enter_context(nc.sbuf_tensor(f"{name}_{n}", shape, dt))

        def sem(n):
            return nc.alloc_semaphore(f"{name}_{n}")

        self.parts_d, self.part_of_pair = parts_d, part_of_pair
        if zero is not None:
            self.zero = zero
            self.whole = sb("whole", [P, KC, S], F32)
            self.taken = sem("taken")
        else:
            self.highs, self.rested, self.middles = sem("high"), sem("rested"), sem("middle")
        self.rest = sb("rest", [P, KC, S], F32)
        self.parts = sb("parts", [P, 2, 3, KC, S])
        self.stacked = sb("stacked", [PAIRS * DK, 2, H, S])
        self.parting, self.parted = sem("parting"), sem("parted")
        self.written, self.stacks = [sem("written0"), sem("written1")], [sem("stack0"), sem("stack1")]

    def take(self, act, b, ps, bias):
        if not isinstance(b, int) or b > 0:
            act.wait_ge(self.parted, b)
        for c in range(KC):
            last = act.activation(self.whole[:, c, :], ps[:, c, :], ACT.Identity, bias=bias[:, c:c + 1])
        last.then_inc(self.taken, 1)

    def split(self, eng, b, par):
        high, middle, low = (self.parts[:, par, j, :, :] for j in range(3))
        eng.wait_ge(self.taken, b + 1)
        if not isinstance(b, int) or b >= 2:
            eng.wait_ge(self.written[par], (b - par) * 8)
        eng.tensor_tensor(high, self.whole[:, :, :], self.zero[:, 0:1].unsqueeze(2).to_broadcast([P, KC, S]), ALU.add)\
            .then_inc(self.parting, 1)
        eng.wait_ge(self.parting, 2 * b + 1)
        eng.tensor_tensor(self.rest[:, :, :], self.whole[:, :, :], high, ALU.subtract)
        eng.tensor_tensor(middle, self.whole[:, :, :], high, ALU.subtract).then_inc(self.parting, 1)
        eng.wait_ge(self.parting, 2 * b + 2)
        eng.tensor_tensor(low, self.rest[:, :, :], middle, ALU.subtract).then_inc(self.parted, 1)

    def free_parts(self, eng, b, par):
        if not isinstance(b, int) or b >= 2:
            eng.wait_ge(self.written[par], (b - par) * 8)

    def take_high(self, act, b, par, ready, ps, bias):
        self.free_parts(act, b, par)
        act.wait_ge(ready, b + 1)
        for c in range(KC):
            last = act.activation(self.parts[:, par, 0, c, :], ps[:, c, :], ACT.Identity, bias=bias[:, c:c + 1])
        last.then_inc(self.highs, 1)

    def take_rest(self, dve, b, par, ps, bias):
        dve.wait_ge(self.highs, b + 1)
        for c in range(KC):
            last = dve.scalar_tensor_tensor(out=self.rest[:, c, :], in0=ps[:, c, :], scalar=bias[:, c:c + 1],
                                            in1=self.parts[:, par, 0, c, :], op0=ALU.add, op1=ALU.subtract)
        last.then_inc(self.rested, 1)

    def take_middle(self, act, b, par):
        act.wait_ge(self.rested, b + 1)
        act.activation(self.parts[:, par, 1, :, :], self.rest[:, :, :], ACT.Copy).then_inc(self.middles, 1)

    def take_low(self, dve, b, par):
        dve.wait_ge(self.middles, b + 1)
        dve.tensor_tensor(self.parts[:, par, 2, :, :], self.rest[:, :, :], self.parts[:, par, 1, :, :], ALU.subtract)\
            .then_inc(self.parted, 1)

    def stack(self, sp, b, par):
        sp.wait_ge(self.parted, b + 1)
        sp.dma_start(self.parts_d[par].rearrange("j (p c) t -> p j c t", c=KC), self.parts[:, par, :, :, :])\
            .then_inc(self.written[par], 16)
        sp.wait_ge(self.written[par], (b - par) * 8 + 16)
        rows = self.parts_d[par].rearrange("j (d h) t -> j d h t", h=H)
        i = 0
        for n in (3, 2, 1):
            j = self.part_of_pair[i]
            src = rows[j:j + 1, :, :, :].to_broadcast([n, DK, H, S]) if self.part_of_pair is K_PART else rows[j:j + n, :, :, :]
            sp.dma_start(self.stacked[DK * i:DK * (i + n), par, :, :], src).then_inc(self.stacks[par], 16)
            i += n

    def wait_stacked(self, pe, b, par):
        pe.wait_ge(self.stacks[par], (b - par) * 24 + 48)


def attend_keys(nc, kit, d):
    U = H // 2
    with ExitStack() as ctx:
        def sb(name, shape, dt=F32):
            return ctx.enter_context(nc.sbuf_tensor("a_" + name, shape, dt))

        def sem(name):
            return nc.alloc_semaphore("a_" + name)

        wq, wk, wv, wo = (sb(n, [P, KC, D]) for n in ("wq", "wk", "wv", "wo"))
        bq, bk = sb("bq", [P, KC]), sb("bk", [P, KC])
        bv = sb("bv", [P, D])
        added = sb("added", [P, QT, D])
        mask_i = sb("mask_i", [P, QT, S], I32)
        mask_b = sb("mask_b", [P, QT, S], BF16)
        ident_b = sb("ident_b", [P, P], BF16)
        seen = sb("seen", [P, 3, QT])
        rstd = sb("rstd", [P, 2, NT])
        zeros = sb("zeros", [P, D])
        ctxT = sb("ctxT", [P, 2, KC, S])
        centred, xn = sb("centred", [P, QT, D]), sb("xn", [P, QT, D])
        xnT = sb("xnT", [P, KC, S])
        q, k = Split(nc, ctx, "a_q", kit.q_parts_d, Q_PART, zeros), Split(nc, ctx, "a_k", kit.k_parts_d, K_PART, zeros)
        va = sb("va", [P, 2, QT, H, 2 * DK])
        mx, nmx = sb("mx", [P, 2, 4]), sb("nmx", [P, 2, 4])
        pr = sb("pr", [P, 2, 4, S])
        prT = sb("prT", [P, 2, 2, QT, S])
        oT = sb("oT", [P, 2, H // G, S])
        rden = sb("rden", [P, QT, H])
        on = sb("on", [P, QT, D])
        onT = sb("onT", [P, KC, S])
        upd = sb("upd", [P, QT, D])
        xnew = sb("xnew", [P, QT, D])
        stats, aggr = sb("stats", [P, QT, 6]), sb("aggr", [P, QT, 2])

        ps_step = ctx.enter_context(nc.psum_tensor("a_ps_step", [P, 512], F32))
        ps_o = ctx.enter_context(nc.psum_tensor("a_ps_o", [P, 512], F32))
        ps_s = ctx.enter_context(nc.psum_tensor("a_ps_s", [P, 2, 2, QT, S], F32))
        ps_t = ctx.enter_context(nc.psum_tensor("a_ps_t", [P, 2, QT, S], F32))
        step4 = ps_step[:, :].rearrange("p (a b) -> p a b", a=2)

        w_in, misc_in = sem("w_in"), sem("misc_in")
        ctx_in = [sem("ctx_in0"), sem("ctx_in1")]
        setup = sem("setup")
        sd_ready = sem("sd_ready")
        ones_ready = sem("ones_ready")
        centred_ready, xn_ready, xnT_ps, xnT_ready = sem("centred_ready"), sem("xn_ready"), sem("xnT_ps"), sem("xnT_ready")
        k_ps, q_ps = sem("k_ps"), sem("q_ps")
        v_ps, v_ready = sem("v_ps"), sem("v_ready")
        s_ps, mx_ready, nmx_ready, pr_ready = sem("s_ps"), sem("mx_ready"), sem("nmx_ready"), sem("pr_ready")
        t_ps, prT_dve, prT_act = sem("t_ps"), sem("prT_dve"), sem("prT_act")
        o_ps, oT_ready = sem("o_ps"), sem("oT_ready")
        back_ps, rden_ready, on_ready = sem("back_ps"), sem("rden_ready"), sem("on_ready")
        onT_ps, onT_ready = sem("onT_ps"), sem("onT_ready")
        y_ps, upd_ready, x_ready = sem("y_ps"), sem("upd_ready"), sem("x_ready")
        block = ctx.enter_context(nc.Block())

        def batches(eng, body):
            body(0, 0, True, False)
            with eng.Fori(1, B - 2, 2) as b:
                body(b, 1, False, False)
                body(b + 1, 0, False, False)
            body(B - 1, 1, False, True)

        @block.sync
        def _(sp):
            for buf, w in ((wk, "wkT"), (wq, "wqT"), (wv, "wvT"), (wo, "woT")):
                sp.dma_start(buf[:, :, :], d[w].rearrange("(c p) n -> p c n", p=P)).then_inc(w_in, 16)

            def load(b, par):
                sp.dma_start(ctxT[:, par, :, :], d["ctxT"][:, bass.ds(b * S, S)].rearrange("(c p) n -> p c n", p=P))\
                    .then_inc(ctx_in[par], 16)

            load(0, 0)
            load(1, 1)
            k.stack(sp, 0, 0)
            q.stack(sp, 0, 0)
            q.stack(sp, 1, 1)
            k.stack(sp, 1, 1)
            with sp.Fori(2, B - 1, 2) as b:
                sp.wait_ge(v_ready, b - 1)
                load(b, 0)
                q.stack(sp, b, 0)
                k.stack(sp, b, 0)
                sp.wait_ge(v_ready, b)
                load(b + 1, 1)
                q.stack(sp, b + 1, 1)
                k.stack(sp, b + 1, 1)

        @block.scalar
        def _(act):
            act.dma_start(mask_i[:, :, :], d["mask"].rearrange("(t p) k -> p t k", p=P)).then_inc(misc_in, 16)
            for buf, n in ((bq, "bq"), (bk, "bk"), (bv, "bv")):
                act.dma_start(buf[:, :], d[n]).then_inc(misc_in, 16)
            for t in range(QT):
                act.dma_start(added[:, t, :], d["bo"]).then_inc(misc_in, 16)
            act.wait_ge(setup, 1)
            act.activation(rstd[:, 1, :], rstd[:, 0, :], ACT.Sqrt).then_inc(sd_ready, 1)
            act.wait_ge(misc_in, 16 * (4 + QT))

            def step_xnT(b):
                act.wait_ge(xnT_ps, b + 1)
                act.activation(xnT[:, :, :], step4, ACT.Copy).then_inc(xnT_ready, 1)

            def step_k(b):
                act.wait_ge(k_ps, b + 1)
                k.take(act, b, step4, bk)

            def step_q(b):
                act.wait_ge(q_ps, b + 1)
                q.take(act, b, step4, bq)

            def numerators(b, u, par):
                n = b * U + u
                for i in range(2):
                    act.wait_ge(nmx_ready, 2 * n + i + 1)
                    for t in range(QT):
                        last = act.activation(pr[:, par, QT * i + t, :], ps_s[:, par, i, t, :], ACT.Exp,
                                              bias=nmx[:, par, QT * i + t:QT * i + t + 1], scale=SCALE)
                    last.then_inc(pr_ready, 1)

            step_xnT(0)
            step_k(0)
            step_q(0)
            numerators(0, 0, 0)

            def body(b, par, first, last):
                for u in range(U):
                    if u == 0 and not last:
                        step_xnT(b + 1)
                    if not (last and u == U - 1):
                        numerators(b, u + 1, (u + 1) % 2)
                    if u == 0 and not last:
                        step_q(b + 1)
                    if u == 1 and not last:
                        step_k(b + 1)
                    if u == 6 and not first:
                        act.wait_ge(onT_ps, b)
                        act.activation(onT[:, :, :], step4, ACT.Copy).then_inc(onT_ready, 1)
                    act.wait_ge(t_ps, 2 * (b * U + u) + 2)
                    act.activation(prT[:, u % 2, 1, :, :], ps_t[:, 1, :, :], ACT.Copy).then_inc(prT_act, 1)

            batches(act, body)
            act.wait_ge(onT_ps, B)
            act.activation(onT[:, :, :], step4, ACT.Copy).then_inc(onT_ready, 1)

        @block.gpsimd
        def _(pool):
            pool.memset(va[:, :, :, :, :], 1.0).then_inc(ones_ready, 1)
            pool.memset(zeros[:, :], 0.0).then_inc(ones_ready, 1)
            pool.wait_ge(ones_ready, 2)

            def normalize(b):
                if not isinstance(b, int) or b > 0:
                    pool.wait_ge(xnT_ps, b)
                rows = bass.ds(QT * b, QT)
                pool.tensor_tensor(centred[:, :, :], kit.x[:, rows, :], kit.mv[:, rows, 0:1].to_broadcast([P, QT, D]),
                                   ALU.subtract).then_inc(centred_ready, 1)
                pool.wait_ge(centred_ready, b + 1)
                pool.tensor_tensor(xn[:, :, :], centred[:, :, :],
                                   rstd[:, 0, rows].unsqueeze(2).to_broadcast([P, QT, D]), ALU.mult).then_inc(xn_ready, 1)

            pool.wait_ge(upd_ready, 1)
            normalize(0)
            k.split(pool, 0, 0)
            q.split(pool, 0, 0)
            normalize(1)
            q.split(pool, 1, 1)
            k.split(pool, 1, 1)
            with pool.Fori(2, B - 1, 2) as b:
                for i in range(2):
                    normalize(b + i)
                    q.split(pool, b + i, i)
                    k.split(pool, b + i, i)

        @block.vector
        def _(dve):
            dve.tensor_scalar(rstd[:, 0, :], kit.mv[:, :, 1], EPS, None, ALU.add).then_inc(setup, 1)
            dve.tensor_copy(ident_b[:, :], kit.ident[:, :]).then_inc(setup, 1)
            dve.wait_ge(misc_in, 16 * (4 + QT))
            dve.tensor_scalar(mask_b[:, :, :], mask_i[:, :, :], 0.0, MASKED, ALU.is_equal, ALU.mult).then_inc(setup, 1)
            dve.wait_ge(setup, 3)
            dve.tensor_reduce(seen[:, 0, :], mask_b[:, :, :], AX.X, ALU.max).then_inc(setup, 1)
            dve.wait_ge(setup, 4)
            dve.tensor_scalar(seen[:, 1, :], seen[:, 0, :], 0.0, None, ALU.is_equal).then_inc(setup, 1)
            dve.wait_ge(setup, 5)
            dve.reciprocal(seen[:, 2, :], seen[:, 1, :]).then_inc(setup, 1)
            dve.wait_ge(setup, 6)
            dve.tensor_scalar(seen[:, 0, :], seen[:, 2, :], 0.0, None, ALU.mult).then_inc(setup, 1)
            dve.wait_ge(setup, 7)
            for t in range(QT):
                dve.tensor_scalar(added[:, t, :], added[:, t, :], seen[:, 0, t:t + 1], None, ALU.add).then_inc(setup, 1)
            dve.wait_ge(sd_ready, 1)
            dve.reciprocal(rstd[:, 0, :], rstd[:, 1, :]).then_inc(upd_ready, 1)
            dve.wait_ge(ones_ready, 1)

            def step_v(b, par):
                dve.wait_ge(v_ps, b + 1)
                dve.tensor_tensor(va[:, par, :, :, 0:DK],
                                  ps_step[:, :].rearrange("p (t h k) -> p t h k", t=QT, h=H),
                                  bv[:, :].rearrange("p (h k) -> p h k", h=H).unsqueeze(1).to_broadcast([P, QT, H, DK]),
                                  ALU.add).then_inc(v_ready, 1)

            def maxima(b, u, par):
                n = b * U + u
                if not isinstance(b, int) or n >= 2:
                    dve.wait_ge(pr_ready, 2 * (n - 1))
                for i in range(2):
                    rows = slice(QT * i, QT * (i + 1))
                    dve.wait_ge(s_ps, 2 * n + i + 1)
                    dve.tensor_reduce(mx[:, par, rows], ps_s[:, par, i, :, :], AX.X, ALU.max).then_inc(mx_ready, 1)
                    dve.wait_ge(mx_ready, 2 * n + i + 1)
                    dve.tensor_scalar(nmx[:, par, rows], mx[:, par, rows], -SCALE, None, ALU.mult).then_inc(nmx_ready, 1)

            def step_back(b, half):
                dve.wait_ge(back_ps, 2 * b + half + 1)
                back = ps_step[:, :].rearrange("p (t h k) -> p t h k", t=QT, k=2 * DK)
                h0 = half * 2 * G
                dve.reciprocal(rden[:, :, h0:h0 + 2 * G], back[:, :, :, DK]).then_inc(rden_ready, 1)
                dve.wait_ge(rden_ready, 2 * b + half + 1)
                dve.tensor_tensor(on[:, :, h0 * DK:(h0 + 2 * G) * DK].rearrange("p t (h k) -> p t h k", k=DK),
                                  back[:, :, :, 0:DK],
                                  rden[:, :, h0:h0 + 2 * G].unsqueeze(3).to_broadcast([P, QT, 2 * G, DK]),
                                  ALU.mult).then_inc(on_ready, 1)

            def step_y(b):
                dve.wait_ge(y_ps, b + 1)
                dve.tensor_tensor(upd[:, :, :], step4, added[:, :, :], ALU.add).then_inc(upd_ready, 1)
                dve.wait_ge(upd_ready, b + 2)

            step_v(0, 0)
            maxima(0, 0, 0)
            maxima(0, 1, 1)

            def body(b, par, first, last):
                for u in range(U):
                    dve.wait_ge(t_ps, 2 * (b * U + u) + 1)
                    dve.tensor_copy(prT[:, u % 2, 0, :, :], ps_t[:, 0, :, :]).then_inc(prT_dve, 1)
                    if u == 3 and not last:
                        step_v(b + 1, 1 - par)
                    if u == 4 and not first:
                        step_back(b - 1, 0)
                    if u == 5 and not first:
                        step_back(b - 1, 1)
                    if u == 7 and not first:
                        step_y(b - 1)
                    if not (last and u >= U - 2):
                        maxima(b, u + 2, u % 2)
                    if u % 2 == 0 and not (first and u == 0):
                        dve.wait_ge(o_ps, b * (H // G) + u // 2)
                        take_group((u // 2 - 1) % (H // G), 1 - par if u == 0 else par)
                    if u == 7 and not first:
                        keep_rows(dve, kit, bass.ds(QT * (b - 1), QT), upd, xnew, stats, aggr, x_ready, b - 1)

            def take_group(group, par):
                dve.tensor_copy(oT[:, par, group, :], ps_o[:, 0:S]).then_inc(oT_ready, 1)

            batches(dve, body)
            dve.wait_ge(o_ps, B * H // G)
            take_group(H // G - 1, 1)
            step_back(B - 1, 0)
            step_back(B - 1, 1)
            step_y(B - 1)
            keep_rows(dve, kit, bass.ds(QT * (B - 1), QT), upd, xnew, stats, aggr, x_ready, B - 1)

        @block.tensor
        def _(pe):
            pe.wait_ge(setup, 2)
            pe.wait_ge(w_in, 64)

            def product(out, lhsT, rhs, n):
                for c in range(n):
                    last = pe.matmul(out, lhsT(c), rhs(c), start=c == 0, stop=c == n - 1)
                return last

            def step_xnT(b):
                pe.wait_ge(xn_ready, b + 1)
                for c in range(KC):
                    for t in range(QT):
                        last = pe.transpose(step4[:, c, P * t:P * (t + 1)], xn[:, t, P * c:P * (c + 1)], kit.ident[:, :])
                last.then_inc(xnT_ps, 1)

            def step_k(b, par, bank_free):
                pe.wait_ge(ctx_in[par], (b - par) * 8 + 16)
                pe.wait_ge(*bank_free)
                for m in range(KC):
                    last = product(step4[:, m, :], lambda c: wk[:, c, P * m:P * (m + 1)], lambda c: ctxT[:, par, c, :], KC)
                last.then_inc(k_ps, 1)

            def step_q(b, bank_free=None):
                pe.wait_ge(xnT_ready, b + 1)
                if bank_free:
                    pe.wait_ge(*bank_free)
                for m in range(KC):
                    last = product(step4[:, m, :], lambda c: wq[:, c, P * m:P * (m + 1)], lambda c: xnT[:, c, :], KC)
                last.then_inc(q_ps, 1)

            def step_v(b, par, bank_free):
                pe.wait_ge(*bank_free)
                for t in range(QT):
                    last = product(step4[:, t, :], lambda c: ctxT[:, par, c, P * t:P * (t + 1)], lambda c: wv[:, c, :], KC)
                last.then_inc(v_ps, 1)

            def step_back(b, par, half, bank_free):
                pe.wait_ge(*bank_free)
                pe.wait_ge(oT_ready, b * (H // G) + 2 * half + 2)
                for t in range(QT):
                    for i in range(2):
                        last = pe.transpose(ps_step[:, (2 * t + i) * P:(2 * t + i + 1) * P],
                                            oT[:, par, 2 * half + i, P * t:P * (t + 1)], kit.ident[:, :])
                last.then_inc(back_ps, 1)

            def step_onT(b, bank_free):
                pe.wait_ge(*bank_free)
                pe.wait_ge(on_ready, 2 * b + 2)
                for c in range(KC):
                    for t in range(QT):
                        last = pe.transpose(step4[:, c, P * t:P * (t + 1)], on[:, t, P * c:P * (c + 1)], kit.ident[:, :])
                last.then_inc(onT_ps, 1)

            def step_y(b):
                pe.wait_ge(onT_ready, b + 1)
                for t in range(QT):
                    last = product(step4[:, t, :], lambda c: onT[:, c, P * t:P * (t + 1)], lambda c: wo[:, c, :], KC)
                last.then_inc(y_ps, 1)

            def scores(b, u, par, i):
                if u == 0 and i == 0:
                    q.wait_stacked(pe, b, par)
                    k.wait_stacked(pe, b, par)
                pe.matmul(ps_s[:, u % 2, i, :, :], ident_b[:, :], mask_b[:, :, :], start=True, stop=False)
                for t in range(QT):
                    last = pe.matmul(ps_s[:, u % 2, i, t, :], q.stacked[:, par, 2 * u + i, P * t:P * (t + 1)],
                                     k.stacked[:, par, 2 * u + i, :], start=False, stop=t == QT - 1)
                last.then_inc(s_ps, 1)

            def turn(b, u, i):
                n = b * U + u
                pe.wait_ge(pr_ready, 2 * n + i + 1)
                if not isinstance(b, int) or n >= 1:
                    pe.wait_ge((prT_dve, prT_act)[i], n)
                for k in range(QT):
                    for t in range(QT):
                        last = pe.transpose(ps_t[:, i, k, P * t:P * (t + 1)],
                                            pr[:, u % 2, 2 * i + t, P * k:P * (k + 1)], kit.ident[:, :])
                last.then_inc(t_ps, 1)

            def values(b, u, par):
                n = b * U + u
                if u == 0:
                    pe.wait_ge(v_ready, b + 1)
                if u % 2 == 0 and (not isinstance(b, int) or n >= 2):
                    pe.wait_ge(oT_ready, b * (H // G) + u // 2)
                pe.wait_ge(prT_dve, n + 1)
                pe.wait_ge(prT_act, n + 1)
                for k in range(QT):
                    for i in range(2):
                        h = 2 * u + i
                        j = 2 * DK * (h % G)
                        last = pe.matmul(ps_o[j:j + 2 * DK, 0:S], va[:, par, k, h, :], prT[:, u % 2, i, k, :],
                                         start=k == 0, stop=k == QT - 1)
                if u % 2 == 1:
                    last.then_inc(o_ps, 1)

            step_xnT(0)
            step_k(0, 0, (xnT_ready, 1))
            step_q(0, (k.taken, 1))
            step_v(0, 0, (q.taken, 1))
            for u in range(2):
                for i in range(2):
                    scores(0, u, 0, i)

            def body(b, par, first, last):
                for u in range(U):
                    if u == 0 and not last:
                        if first:
                            pe.wait_ge(v_ready, 1)
                        else:
                            pe.wait_ge(upd_ready, b)
                            pe.wait_ge(v_ready, b + 1)
                        step_xnT(b + 1)
                    if u == 1 and not last:
                        step_k(b + 1, 1 - par, (q.taken, b + 2))
                    if u == 3 and not last:
                        step_v(b + 1, 1 - par, (k.taken, b + 2))
                    if u == 4 and not first:
                        step_back(b - 1, 1 - par, 0, (v_ready, b + 2) if not last else (upd_ready, b))
                    if u == 5 and not first:
                        step_back(b - 1, 1 - par, 1, (on_ready, 2 * b - 1))
                    if u == 6 and not first:
                        step_onT(b - 1, (on_ready, 2 * b))
                    if u == 7 and not first:
                        step_y(b - 1)
                    for i in range(2):
                        turn(b, u, i)
                        if u < U - 2:
                            scores(b, u + 2, par, i)
                        elif not last:
                            scores(b + 1, u + 2 - U, 1 - par, i)
                        if u == 0 and i == 0 and not last:
                            step_q(b + 1)
                    if u > 0:
                        values(b, u - 1, par)
                    elif not first:
                        values(b - 1, U - 1, 1 - par)

            batches(pe, body)
            values(B - 1, U - 1, 1)
            step_back(B - 1, 1, 0, (upd_ready, B))
            step_back(B - 1, 1, 1, (on_ready, 2 * B - 1))
            step_onT(B - 1, (on_ready, 2 * B))
            step_y(B - 1)


def channel_mix(nc, kit, d):
    with ExitStack() as ctx:
        def sb(name, shape, dt=F32):
            return ctx.enter_context(nc.sbuf_tensor("b_" + name, shape, dt))

        def sem(name):
            return nc.alloc_semaphore("b_" + name)

        def psum(name):
            return ctx.enter_context(nc.psum_tensor("b_" + name, [P, 2, S], F32))

        wr, wk, wv = (sb(n, [P, KC, D]) for n in ("wr", "wk", "wv"))
        mu, rest = sb("mu", [P, 2, KC]), sb("rest", [P, 2, KC])
        rstd = sb("rstd", [P, 2, NT])
        xn = sb("xn", [P, QT, D])
        xT = sb("xT", [P, KC, S + 1])
        part = sb("part", [P, 2, KC, S])
        mix = sb("mix", [P, 2, 2, KC, S])
        kk = sb("kk", [P, KC, S])
        gate = sb("gate", [P, QT, D])
        upd, xnew = sb("upd", [P, QT, D]), sb("xnew", [P, QT, D])
        stats, aggr = sb("stats", [P, QT, 6]), sb("aggr", [P, QT, 2])
        zeros = sb("zeros", [P, D])
        zeros_ready, zeroed = sem("zeros_ready"), sem("zeroed")
        ps_x, ps_r, ps_k, ps_y = (psum(n) for n in ("ps_x", "ps_r", "ps_k", "ps_y"))

        w_in, mu_in = sem("w_in"), sem("mu_in")
        setup, sd_ready = sem("setup"), sem("sd_ready")
        xn_ready, x_ps, xT_ready, part_ready = sem("xn_ready"), sem("x_ps"), sem("xT_ready"), sem("part_ready")
        mixed = sem("mixed")
        k_ps, kk_ready, r_ps, gate_ready = sem("k_ps"), sem("kk_ready"), sem("r_ps"), sem("gate_ready")
        y_ps, upd_ready, x_ready = sem("y_ps"), sem("upd_ready"), sem("x_ready")
        block = ctx.enter_context(nc.Block())

        def batches(eng, body):
            body(0, 0, False)
            with eng.Fori(1, B - 2, 2) as b:
                body(b, 1, False)
                body(b + 1, 0, False)
            body(B - 1, 1, True)

        @block.sync
        def _(sp):
            for i, n in enumerate(("mu_r", "mu_k")):
                sp.dma_start(mu[:, i, :], d[n]).then_inc(mu_in, 16)
            for buf, w in ((wk, "wkT"), (wr, "wrT"), (wv, "wvT")):
                sp.dma_start(buf[:, :, :], d[w].rearrange("(c p) n -> p c n", p=P)).then_inc(w_in, 16)
            sp.wait_ge(zeros_ready, 1)
            sp.dma_start(kit.sorted_d.rearrange("(t p) c -> p t c", p=P),
                         zeros[:, :].unsqueeze(1).to_broadcast([P, kit.sorted_d.shape[0] // P, D])).then_inc(zeroed, 16)
            sp.wait_ge(zeroed, 16)

        @block.gpsimd
        def _(pool):
            pool.memset(zeros[:, :], 0.0).then_inc(zeros_ready, 1)

        @block.scalar
        def _(act):
            act.wait_ge(setup, 1)
            act.activation(rstd[:, 1, :], rstd[:, 0, :], ACT.Sqrt).then_inc(sd_ready, 1)
            act.wait_ge(mu_in, 32)

            def turned(b):
                act.wait_ge(x_ps, b + 1)
                if not isinstance(b, int) or b > 0:
                    act.wait_ge(mixed, b)
                act.activation(xT[:, :, 1:S + 1], ps_x[:, :, :], ACT.Copy).then_inc(xT_ready, 1)
                for i in range(2):
                    for c in range(KC):
                        last = act.activation(part[:, i, c, :], ps_x[:, c, :], ACT.Copy, scale=mu[:, i, c:c + 1])
                last.then_inc(part_ready, 1)

            def gates(b):
                act.wait_ge(r_ps, b + 1)
                if not isinstance(b, int) or b > 0:
                    act.wait_ge(upd_ready, b)
                act.activation(gate[:, :, :], ps_r[:, :, :], ACT.Sigmoid).then_inc(gate_ready, 1)

            turned(0)

            def body(b, par, last):
                gates(b)
                if not last:
                    turned(b + 1)

            batches(act, body)

        @block.vector
        def _(dve):
            dve.tensor_scalar(rstd[:, 0, :], kit.mv[:, :, 1], EPS, None, ALU.add).then_inc(setup, 1)
            dve.memset(xT[:, :, 0:1], 0.0).then_inc(setup, 1)
            dve.wait_ge(mu_in, 32)
            dve.tensor_scalar(rest[:, :, :], mu[:, :, :], -1.0, 1.0, ALU.mult, ALU.add).then_inc(setup, 1)
            dve.wait_ge(sd_ready, 1)
            dve.reciprocal(rstd[:, 0, :], rstd[:, 1, :]).then_inc(setup, 1)
            dve.wait_ge(setup, 4)

            def normalize(b):
                if not isinstance(b, int) or b > 0:
                    dve.wait_ge(x_ps, b)
                for t in range(QT):
                    last = dve.tensor_scalar(xn[:, t, :], kit.x[:, QT * b + t, :], kit.mv[:, QT * b + t, 0:1],
                                             rstd[:, 0, bass.ds(QT * b + t, 1)], ALU.subtract, ALU.mult)
                last.then_inc(xn_ready, 1)

            def mixing(b, par):
                dve.wait_ge(xT_ready, b + 1)
                dve.wait_ge(part_ready, b + 1)
                for i in range(2):
                    for c in range(KC):
                        last = dve.scalar_tensor_tensor(out=mix[:, par, i, c, :], in0=xT[:, c, 0:S],
                                                        scalar=rest[:, i, c:c + 1], in1=part[:, i, c, :],
                                                        op0=ALU.mult, op1=ALU.add)
                last.then_inc(mixed, 1)

            normalize(0)
            mixing(0, 0)

            def body(b, par, last):
                if not last:
                    normalize(b + 1)
                dve.wait_ge(k_ps, b + 1)
                dve.tensor_scalar(kk[:, :, :], ps_k[:, :, :], 0.0, None, ALU.max).then_inc(kk_ready, 1)
                dve.wait_ge(kk_ready, 2 * b + 1)
                dve.tensor_tensor(kk[:, :, :], kk[:, :, :], kk[:, :, :], ALU.mult).then_inc(kk_ready, 1)
                if not last:
                    mixing(b + 1, 1 - par)
                dve.wait_ge(y_ps, b + 1)
                dve.wait_ge(gate_ready, b + 1)
                dve.tensor_tensor(upd[:, :, :], ps_y[:, :, :], gate[:, :, :], ALU.mult).then_inc(upd_ready, 1)
                dve.wait_ge(upd_ready, b + 1)
                keep_rows(dve, kit, bass.ds(QT * b, QT), upd, xnew, stats, aggr, x_ready, b)

            batches(dve, body)

        @block.tensor
        def _(pe):
            pe.wait_ge(w_in, 48)

            def turn(b):
                pe.wait_ge(xn_ready, b + 1)
                if not isinstance(b, int) or b > 0:
                    pe.wait_ge(part_ready, b)
                for c in range(KC):
                    for t in range(QT):
                        last = pe.transpose(ps_x[:, c, P * t:P * (t + 1)], xn[:, t, P * c:P * (c + 1)], kit.ident[:, :])
                last.then_inc(x_ps, 1)

            turn(0)

            def body(b, par, last):
                pe.wait_ge(mixed, b + 1)
                for m in range(KC):
                    for c in range(KC):
                        mm = pe.matmul(ps_k[:, m, :], wk[:, c, P * m:P * (m + 1)], mix[:, par, 1, c, :],
                                       start=c == 0, stop=c == KC - 1)
                mm.then_inc(k_ps, 1)
                if not isinstance(b, int) or b > 0:
                    pe.wait_ge(gate_ready, b)
                for t in range(QT):
                    for c in range(KC):
                        mm = pe.matmul(ps_r[:, t, :], mix[:, par, 0, c, P * t:P * (t + 1)], wr[:, c, :],
                                       start=c == 0, stop=c == KC - 1)
                mm.then_inc(r_ps, 1)
                if not last:
                    turn(b + 1)
                pe.wait_ge(kk_ready, 2 * b + 2)
                if not isinstance(b, int) or b > 0:
                    pe.wait_ge(upd_ready, b)
                for t in range(QT):
                    for c in range(KC):
                        mm = pe.matmul(ps_y[:, t, :], kk[:, c, P * t:P * (t + 1)], wv[:, c, :],
                                       start=c == 0, stop=c == KC - 1)
                mm.then_inc(y_ps, 1)

            batches(pe, body)


def attend_heads(nc, kit, d):
    U = QT * QT
    HB = H // G
    HALF = H // 2
    HV = 12
    W = G * P
    with ExitStack() as ctx:
        def sb(name, shape, dt=F32):
            return ctx.enter_context(nc.sbuf_tensor("c_" + name, shape, dt))

        def sem(name):
            return nc.alloc_semaphore("c_" + name)

        wq, wk, wv = (sb(n, [P, KC, D]) for n in ("wq", "wk", "wv"))
        wo = sb("wo", [P, H // G, D])
        bq, bk = sb("bq", [P, KC]), sb("bk", [P, KC])
        bv, bo = sb("bv", [P, D]), sb("bo", [P, D])
        minus_i = sb("minus_i", [P, P], BF16)
        rstd = sb("rstd", [P, 2, NT])
        shift_mean = sb("shift_mean", [P, 2, NT])
        ctxT = sb("ctxT", [P, 2, KC, S])
        xn = sb("xn", [P, QT, D])
        xnT = sb("xnT", [P, KC, S])
        q, k = Split(nc, ctx, "c_q", kit.q_parts_d, Q_PART), Split(nc, ctx, "c_k", kit.k_parts_d, K_PART)
        va = sb("va", [P, 2, QT, H, 2 * DK])
        mx = sb("mx", [P, 2, P])
        mxb = sb("mxb", [P, P], BF16)
        pr = sb("pr", [P, U, H, P])
        tree = sb("tree", [P, HALF, P])
        den, rden = sb("den", [P, 2, P]), sb("rden", [P, 2, P])
        oT = sb("oT", [P, H // G, P])
        upd, xnew = sb("upd", [P, 1, D]), sb("xnew", [P, 1, D])
        stats, aggr = sb("stats", [P, 1, 6]), sb("aggr", [P, 1, 2])

        ps_a = ctx.enter_context(nc.psum_tensor("c_ps_a", [P, 2, S], F32))
        ps_b = ctx.enter_context(nc.psum_tensor("c_ps_b", [P, 2, S], F32))
        ps_o = ctx.enter_context(nc.psum_tensor("c_ps_o", [P, H // G, P], F32))
        ps_s = ctx.enter_context(nc.psum_tensor("c_ps_s", [P, H, P], F32))

        w_in, misc_in = sem("w_in"), sem("misc_in")
        ctx_in = [sem("ctx_in0"), sem("ctx_in1")]
        setup, sd_ready, zeros_ready = sem("setup"), sem("sd_ready"), sem("zeros_ready")
        xn_ready, xnT_ps, xnT_ready = sem("xn_ready"), sem("xnT_ps"), sem("xnT_ready")
        k_ps, q_ps, v_ps, v_ready = sem("k_ps"), sem("q_ps"), sem("v_ps"), sem("v_ready")
        s_ps, halves_ready, max_ready, shifted = sem("s_ps"), sem("halves_ready"), sem("max_ready"), sem("shifted")
        e_ready, tree_ready, den_ready, rden_ready = sem("e_ready"), sem("tree_ready"), sem("den_ready"), sem("rden_ready")
        pr_dve, pr_pool, pv_done = sem("pr_dve"), sem("pr_pool"), sem("pv_done")
        oT_ready, y_ps, upd_ready, x_ready = sem("oT_ready"), sem("y_ps"), sem("upd_ready"), sem("x_ready")
        block = ctx.enter_context(nc.Block())

        def batches(eng, body):
            body(0, 0, True, False)
            with eng.Fori(1, B - 2, 2) as b:
                body(b, 1, False, False)
                body(b + 1, 0, False, False)
            body(B - 1, 1, False, True)

        @block.sync
        def _(sp):
            for buf, w in ((wk, "wkT"), (wq, "wqT"), (wv, "wvT"), (wo, "woT")):
                sp.dma_start(buf[:, :, :], d[w].rearrange("(c p) n -> p c n", p=P)).then_inc(w_in, 16)

            def load(b, par):
                sp.dma_start(ctxT[:, par, :, :], d["ctxT"][:, bass.ds(b * S, S)].rearrange("(c p) n -> p c n", p=P))\
                    .then_inc(ctx_in[par], 16)

            load(0, 0)
            load(1, 1)
            for b in range(2):
                k.stack(sp, b, b)
                q.stack(sp, b, b)
            with sp.Fori(2, B - 1, 2) as b:
                for i in range(2):
                    sp.wait_ge(v_ready, b + i - 1)
                    load(b + i, i)
                    k.stack(sp, b + i, i)
                    q.stack(sp, b + i, i)

        @block.scalar
        def _(act):
            for buf, n in ((bq, "bq"), (bk, "bk"), (bv, "bv"), (bo, "bo")):
                act.dma_start(buf[:, :], d[n]).then_inc(misc_in, 16)
            act.wait_ge(setup, 1)
            act.activation(rstd[:, 1, :], rstd[:, 0, :], ACT.Sqrt).then_inc(sd_ready, 1)
            act.wait_ge(misc_in, 16 * 4)
            act.wait_ge(upd_ready, 1)

            def step_xnT(b):
                act.wait_ge(xnT_ps, b + 1)
                act.activation(xnT[:, :, :], ps_b[:, :, :], ACT.Copy).then_inc(xnT_ready, 1)

            def normalize(b):
                for t in range(QT):
                    tile = bass.ds(QT * b + t, 1)
                    last = act.activation(xn[:, t, :], kit.x[:, tile, :].rearrange("p t c -> p (t c)"), ACT.Identity,
                                          bias=shift_mean[:, 1, tile], scale=rstd[:, 0, tile])
                last.then_inc(xn_ready, 1)

            def numerators(b, i):
                n = b * U + i
                if not isinstance(b, int) or b > 0:
                    act.wait_ge(pv_done, n - U + 1)
                act.wait_ge(shifted, n + 1)
                for half in range(2):
                    hs = slice(HALF * half, HALF * (half + 1))
                    act.activation(pr[:, i, hs, :], ps_s[:, hs, :], ACT.Exp, scale=SCALE).then_inc(e_ready, 1)

            def take_o(j):
                act.wait_ge(pv_done, 2 * j + 2)
                if not isinstance(j, int) or j > 0:
                    act.wait_ge(y_ps, j)
                act.activation(oT[:, :, :], ps_o[:, :, :], ACT.Copy).then_inc(oT_ready, 1)

            normalize(0)
            step_xnT(0)
            k.take_high(act, 0, 0, k_ps, ps_a, bk)
            q.take_high(act, 0, 0, q_ps, ps_b, bq)
            k.take_middle(act, 0, 0)
            q.take_middle(act, 0, 0)

            def body(b, par, first, last):
                for i in range(U):
                    if i == 0 and not last:
                        normalize(b + 1)
                    numerators(b, i)
                    if i == 0 and not last:
                        step_xnT(b + 1)
                        k.take_high(act, b + 1, 1 - par, k_ps, ps_a, bk)
                        q.take_high(act, b + 1, 1 - par, q_ps, ps_b, bq)
                    if i == 1 and not last:
                        k.take_middle(act, b + 1, 1 - par)
                        q.take_middle(act, b + 1, 1 - par)
                    if i == 3:
                        take_o(2 * b)
                    if i == 1 and not first:
                        take_o(2 * b - 1)

            batches(act, body)
            take_o(2 * B - 1)

        @block.gpsimd
        def _(pool):
            pool.memset(va[:, :, :, :, :], 0.0).then_inc(zeros_ready, 1)

            def add_heads(n, i, early):
                if not isinstance(n, int) or n > 0:
                    pool.wait_ge(den_ready, n)
                pool.wait_ge(e_ready, 2 * n + 2)
                pool.tensor_tensor(tree[:, :, :], pr[:, i, 0:8, :], pr[:, i, 8:16, :], ALU.add).then_inc(tree_ready, 1)
                pool.wait_ge(tree_ready, 3 * n + 1)
                pool.tensor_tensor(tree[:, 0:4, :], tree[:, 0:4, :], tree[:, 4:8, :], ALU.add).then_inc(tree_ready, 1)
                pool.wait_ge(tree_ready, 3 * n + 2)
                pool.tensor_tensor(tree[:, 0:2, :], tree[:, 0:2, :], tree[:, 2:4, :], ALU.add).then_inc(tree_ready, 1)
                if not early:
                    pool.wait_ge(rden_ready, n - 1)
                pool.wait_ge(tree_ready, 3 * n + 3)
                pool.tensor_tensor(den[:, i % 2, :], tree[:, 0, :], tree[:, 1, :], ALU.add).then_inc(den_ready, 1)

            def probabilities(n, i):
                pool.wait_ge(rden_ready, n + 1)
                pool.tensor_tensor(pr[:, i, HV:H, :], pr[:, i, HV:H, :],
                                   rden[:, i % 2, :].unsqueeze(1).to_broadcast([P, H - HV, P]), ALU.mult).then_inc(pr_pool, 1)

            def body(b, par, first, last):
                for i in range(U):
                    n = b * U + i
                    add_heads(n, i, first and i < 2)
                    if not first or i > 0:
                        probabilities(n - 1, (i - 1) % U)

            batches(pool, body)
            probabilities(B * U - 1, U - 1)

        @block.vector
        def _(dve):
            dve.tensor_scalar(rstd[:, 0, :], kit.mv[:, :, 1], EPS, None, ALU.add).then_inc(setup, 1)
            dve.tensor_scalar(minus_i[:, :], kit.ident[:, :], -1.0, None, ALU.mult).then_inc(setup, 1)
            dve.wait_ge(misc_in, 16 * 4)
            dve.wait_ge(sd_ready, 1)
            dve.reciprocal(rstd[:, 0, :], rstd[:, 1, :]).then_inc(setup, 1)
            dve.tensor_scalar(shift_mean[:, 0, :], kit.mv[:, :, 0], -1.0, None, ALU.mult).then_inc(setup, 1)
            dve.wait_ge(setup, 4)
            dve.tensor_tensor(shift_mean[:, 1, :], shift_mean[:, 0, :], rstd[:, 0, :], ALU.mult)\
                .then_inc(upd_ready, 1)
            dve.wait_ge(zeros_ready, 1)

            def step_v(b, par):
                dve.wait_ge(v_ps, b + 1)
                dve.tensor_tensor(va[:, par, :, :, 0:DK], ps_b[:, :, :].rearrange("p t (h k) -> p t h k", h=H),
                                  bv[:, :].rearrange("p (h k) -> p h k", h=H).unsqueeze(1).to_broadcast([P, QT, H, DK]),
                                  ALU.add).then_inc(v_ready, 1)

            def maxima(b, i):
                n = b * U + i
                for half in range(2):
                    hs = slice(HALF * half, HALF * (half + 1))
                    dve.wait_ge(s_ps, 2 * n + half + 1)
                    dve.tensor_reduce(mx[:, half, :], ps_s[:, hs, :].rearrange("p h q -> p q h"), AX.X, ALU.max)\
                        .then_inc(halves_ready, 1)
                dve.wait_ge(halves_ready, 2 * n + 2)
                dve.tensor_tensor(mxb[:, :], mx[:, 0, :], mx[:, 1, :], ALU.max).then_inc(max_ready, 1)

            def denominators(n, i, early):
                dve.wait_ge(den_ready, n + 1)
                if not early:
                    dve.wait_ge(pr_pool, n - 1)
                    dve.wait_ge(pr_dve, n - 1)
                dve.reciprocal(rden[:, i % 2, :], den[:, i % 2, :]).then_inc(rden_ready, 1)

            def probabilities(n, i):
                dve.wait_ge(rden_ready, n + 1)
                dve.tensor_tensor(pr[:, i, 0:HV, :], pr[:, i, 0:HV, :],
                                  rden[:, i % 2, :].unsqueeze(1).to_broadcast([P, HV, P]), ALU.mult).then_inc(pr_dve, 1)

            def step_y(j):
                dve.wait_ge(y_ps, j + 1)
                dve.tensor_tensor(upd[:, 0, :], ps_a[:, 0, :], bo[:, :], ALU.add).then_inc(upd_ready, 1)

            def keep(j):
                dve.wait_ge(upd_ready, j + 2)
                keep_rows(dve, kit, bass.ds(j, 1), upd, xnew, stats, aggr, x_ready, j)

            k.take_rest(dve, 0, 0, ps_a, bk)
            q.take_rest(dve, 0, 0, ps_b, bq)
            k.take_low(dve, 0, 0)
            q.take_low(dve, 0, 0)
            step_v(0, 0)

            def body(b, par, first, last):
                for i in range(U):
                    maxima(b, i)
                    if i == 0 and not first:
                        step_v(b, par)
                    if i == 1 and not last:
                        k.take_rest(dve, b + 1, 1 - par, ps_a, bk)
                    if i >= 2 and not first:
                        step_y(2 * b - 4 + i)
                    if not first or i > 1:
                        probabilities(b * U + i - 2, (i - 2) % U)
                    if not first or i > 0:
                        denominators(b * U + i - 1, (i - 1) % U, first and i < 3)
                    if i == 1 and not last:
                        q.take_rest(dve, b + 1, 1 - par, ps_b, bq)
                        k.take_low(dve, b + 1, 1 - par)
                        q.take_low(dve, b + 1, 1 - par)
                    if i >= 2 and not first:
                        keep(2 * b - 4 + i)

            batches(dve, body)
            probabilities(B * U - 2, U - 2)
            denominators(B * U - 1, U - 1, False)
            probabilities(B * U - 1, U - 1)
            for j in (2 * B - 2, 2 * B - 1):
                step_y(j)
                keep(j)

        @block.tensor
        def _(pe):
            pe.wait_ge(setup, 2)
            pe.wait_ge(w_in, 64)

            def product(out, lhsT, rhs, n):
                for c in range(n):
                    last = pe.matmul(out, lhsT(c), rhs(c), start=c == 0, stop=c == n - 1)
                return last

            def step_xnT(b):
                pe.wait_ge(xn_ready, b + 1)
                for c in range(KC):
                    for t in range(QT):
                        last = pe.transpose(ps_b[:, c, P * t:P * (t + 1)], xn[:, t, P * c:P * (c + 1)], kit.ident[:, :])
                last.then_inc(xnT_ps, 1)

            def step_k(b, par):
                pe.wait_ge(ctx_in[par], (b - par) * 8 + 16)
                for m in range(KC):
                    last = product(ps_a[:, m, :], lambda c: wk[:, c, P * m:P * (m + 1)], lambda c: ctxT[:, par, c, :], KC)
                last.then_inc(k_ps, 1)

            def step_q(b):
                pe.wait_ge(xnT_ready, b + 1)
                for m in range(KC):
                    last = product(ps_b[:, m, :], lambda c: wq[:, c, P * m:P * (m + 1)], lambda c: xnT[:, c, :], KC)
                last.then_inc(q_ps, 1)

            def step_v(b, par):
                for t in range(QT):
                    last = product(ps_b[:, t, :], lambda c: ctxT[:, par, c, P * t:P * (t + 1)], lambda c: wv[:, c, :], KC)
                last.then_inc(v_ps, 1)

            def step_y(j):
                pe.wait_ge(oT_ready, j + 1)
                product(ps_a[:, 0, :], lambda g: oT[:, g, :], lambda g: wo[:, g, :], H // G).then_inc(y_ps, 1)

            def scores(b, i, par):
                t, kt = i // QT, i % QT
                n = b * U + i
                if i == 0:
                    k.wait_stacked(pe, b, par)
                    q.wait_stacked(pe, b, par)
                for h in range(H):
                    if h % HALF == 0 and (not isinstance(b, int) or n > 0):
                        pe.wait_ge(e_ready, 2 * n - 1 + h // HALF)
                    last = pe.matmul(ps_s[:, h, :], k.stacked[:, par, h, P * kt:P * (kt + 1)],
                                     q.stacked[:, par, h, P * t:P * (t + 1)],
                                     start=h % G == 0, stop=False, skip_group_check=True)
                    if h % HALF == HALF - 1:
                        last.then_inc(s_ps, 1)

            def shift(b, i):
                n = b * U + i
                pe.wait_ge(max_ready, n + 1)
                for g in range(HB):
                    last = pe.matmul(ps_s[:, G * g:G * (g + 1), :], minus_i[:, :],
                                     mxb[:, :].unsqueeze(1).to_broadcast([P, G, P]),
                                     start=False, stop=True, skip_group_check=True)
                last.then_inc(shifted, 1)

            def values(b, i, par):
                k = i % QT
                n = b * U + i
                if i == 0:
                    pe.wait_ge(v_ready, b + 1)
                if k == 0 and (not isinstance(b, int) or n > 0):
                    pe.wait_ge(oT_ready, 2 * b + i // QT)
                pe.wait_ge(pr_dve, n + 1)
                pe.wait_ge(pr_pool, n + 1)
                for h in range(H):
                    j = 2 * DK * (h % G)
                    last = pe.matmul(ps_o[j:j + 2 * DK, h // G, :], va[:, par, k, h, :], pr[:, i, h, :],
                                     start=k == 0 and h < G, stop=k == QT - 1, skip_group_check=True)
                last.then_inc(pv_done, 1)

            step_k(0, 0)
            step_xnT(0)
            step_q(0)
            pe.wait_ge(q.rested, 1)
            step_v(0, 0)
            scores(0, 0, 0)

            def body(b, par, first, last):
                for i in range(U):
                    shift(b, i)
                    if i < U - 1:
                        scores(b, i + 1, par)
                    elif not last:
                        scores(b + 1, 0, 1 - par)
                    if i == 0 and not last:
                        pe.wait_ge(v_ready, b + 1)
                        step_xnT(b + 1)
                    if i >= 2:
                        values(b, i - 2, par)
                    elif not first:
                        values(b - 1, i + 2, 1 - par)
                    if i == 0 and not last:
                        pe.wait_ge(k.rested, b + 1)
                        if not first:
                            pe.wait_ge(upd_ready, 2 * b - 1)
                        step_k(b + 1, 1 - par)
                        step_q(b + 1)
                    if i == 1 and not first:
                        pe.wait_ge(upd_ready, 2 * b - 1)
                        if not last:
                            pe.wait_ge(k.rested, b + 2)
                        step_y(2 * b - 2)
                    if i == 2 and not first:
                        pe.wait_ge(upd_ready, 2 * b)
                        step_y(2 * b - 1)
                    if i == 3 and not last:
                        pe.wait_ge(q.rested, b + 2)
                        step_v(b + 1, 1 - par)

            batches(pe, body)
            values(B - 1, 2, 1)
            values(B - 1, 3, 1)
            pe.wait_ge(upd_ready, 2 * B - 1)
            step_y(2 * B - 2)
            pe.wait_ge(upd_ready, 2 * B)
            step_y(2 * B - 1)


def route(nc, kit, d):
    PAIR = 2
    NJ = NT // PAIR
    with ExitStack() as ctx:
        def sb(name, shape, dt=F32):
            return ctx.enter_context(nc.sbuf_tensor("r_" + name, shape, dt))

        def sem(name):
            return ctx.enter_context(nc.semaphore("r_" + name))

        wr, br = sb("wr", [P, KC, E]), sb("br", [P, E])
        order = sb("order", [P, E])
        tile_no = sb("tile_no", [P, SLOT_TILES])
        before = sb("before", [P, P])
        before_b, ones_b = sb("before_b", [P, P], BF16), sb("ones_b", [P, P], BF16)
        ones = sb("ones", [P, NT])
        rstd = sb("rstd", [P, 2, NT])
        xn = sb("xn", [P, 2, PAIR, D])
        xnT = sb("xnT", [P, KC, PAIR * P])
        lg = sb("lg", [P, NT, E])
        low, hit = sb("low", [P, NT, E]), sb("hit", [P, NT, E])
        top = sb("top", [P, 2, NT])
        first_at = sb("first_at", [P, NT])
        one_hot = sb("one_hot", [P, 2, NT, E])
        taken = sb("taken", [P, NT, E], BF16)
        ex = sb("ex", [P, NT])
        rank, total, upto = sb("rank", [P, NT, E]), sb("total", [P, NT, E]), sb("upto", [P, NT, E])
        tiles_i, tiles_f = sb("tiles_i", [P, E], I32), sb("tiles_f", [P, E])
        upto_e, start_e = sb("upto_e", [P, E]), sb("start_e", [P, E])
        slot_f = sb("slot_f", [P, NT])
        past = sb("past", [P, SLOT_TILES, E])
        past_n = sb("past_n", [P, SLOT_TILES])
        ps_x = ctx.enter_context(nc.psum_tensor("r_ps_x", [P, KC, PAIR * P], F32))
        ps_l = ctx.enter_context(nc.psum_tensor("r_ps_l", [P, PAIR, E], F32))
        ps_r = ctx.enter_context(nc.psum_tensor("r_ps_r", [P, NT * E], F32))
        ps_n = ctx.enter_context(nc.psum_tensor("r_ps_n", [P, NT * E], F32))

        misc_in, x_saved = sem("misc_in"), [sem(f"x_saved{i}") for i in range(4)]
        setup, sd_ready = sem("setup"), sem("sd_ready")
        xn_ready, xn_kept, x_ps, xnT_ready = sem("xn_ready"), sem("xn_kept"), sem("x_ps"), sem("xnT_ready")
        l_ps, lg_ready = sem("l_ps"), sem("lg_ready")
        pick = sem("pick")
        ex_ready, taken_ready, counts_ps, place = sem("ex_ready"), sem("taken_ready"), sem("counts_ps"), sem("place")
        moved = sem("moved")
        block = ctx.enter_context(nc.Block())

        n4 = NT // 4

        @block.sync
        def _(sp):
            for i in range(4):
                sp.dma_start(kit.x_d[P * n4 * i:P * n4 * (i + 1), :].rearrange("(t p) c -> p t c", p=P),
                             kit.x[:, n4 * i:n4 * (i + 1), :]).then_inc(x_saved[i], 16)
            for e in range(E):
                sp.dma_start(kit.w1[:, e, :, :], d["w1"][e].rearrange("(c p) f -> p c f", p=P)).then_inc(kit.w_in, 16)
                sp.dma_start(kit.w2[:, e, :, :], d["w2"][e].rearrange("(f p) n -> p f n", p=P)).then_inc(kit.w_in, 16)
            for buf, n in ((kit.b1, "b1"), (kit.b2, "b2")):
                sp.dma_start(buf[:, :, :], d[n]).then_inc(kit.w_in, 16)
            sp.wait_ge(kit.w_in, 16 * (2 * E + 2))
            for i in range(4):
                sp.wait_ge(x_saved[i], 16)

        @block.scalar
        def _(act):
            act.dma_start(wr[:, :, :], d["wr"].rearrange("(c p) e -> p c e", p=P)).then_inc(misc_in, 16)
            for buf, n in ((br, "br"), (order, "order"), (tile_no, "tile_no"), (before, "before")):
                act.dma_start(buf[:, :], d[n]).then_inc(misc_in, 16)
            act.wait_ge(setup, 1)
            act.activation(rstd[:, 1, :], rstd[:, 0, :], ACT.Sqrt).then_inc(sd_ready, 1)
            act.wait_ge(misc_in, 16 * 5)

            with act.Fori(0, NJ) as j:
                act.wait_ge(x_ps, j + 1)
                act.activation(xnT[:, :, :], ps_x[:, :, :], ACT.Copy).then_inc(xnT_ready, 1)
            act.wait_ge(pick, 8)
            act.activation(ex[:, :], first_at[:, :], ACT.Exp).then_inc(ex_ready, 1)

        @block.vector
        def _(dve):
            dve.tensor_scalar(rstd[:, 0, :], kit.mv[:, :, 1], EPS, None, ALU.add).then_inc(setup, 1)
            dve.wait_ge(misc_in, 16 * 5)
            dve.tensor_copy(before_b[:, :], before[:, :]).then_inc(setup, 1)
            dve.memset(ones_b[:, :], 1.0).then_inc(setup, 1)
            dve.memset(ones[:, :], 1.0).then_inc(setup, 1)
            dve.wait_ge(sd_ready, 1)
            dve.reciprocal(rstd[:, 0, :], rstd[:, 1, :]).then_inc(setup, 1)
            dve.wait_ge(setup, 5)

            def rows(j, par):
                for t in range(PAIR):
                    last = dve.tensor_scalar(xn[:, par, t, :], kit.x[:, PAIR * j + t, :], kit.mv[:, PAIR * j + t, 0:1],
                                             rstd[:, 0, bass.ds(PAIR * j + t, 1)], ALU.subtract, ALU.mult)
                last.then_inc(xn_ready, 1)
                dve.wait_ge(xn_ready, j + 1)
                dve.tensor_scalar(kit.x[:, bass.ds(PAIR * j, PAIR), :], xn[:, par, :, :], 1.0, None, ALU.mult).then_inc(xn_kept, 1)

            for i in range(4):
                dve.wait_ge(x_saved[i], 16)
            rows(0, 0)

            def logits(j):
                dve.wait_ge(l_ps, j + 1)
                dve.tensor_tensor(lg[:, bass.ds(PAIR * j, PAIR), :], ps_l[:, :, :],
                                  br[:, :].unsqueeze(1).to_broadcast([P, PAIR, E]), ALU.add).then_inc(lg_ready, 1)

            rows(1, 1)
            logits(0)
            with dve.Fori(2, NJ - 1, 2) as j:
                dve.wait_ge(x_ps, j - 1)
                rows(j, 0)
                logits(j - 1)
                dve.wait_ge(x_ps, j)
                rows(j + 1, 1)
                logits(j)
            logits(NJ - 1)
            dve.wait_ge(lg_ready, NJ)
            dve.wait_ge(xn_kept, NJ)

            every = [P, NT, E]
            order_b = order[:, :].unsqueeze(1).to_broadcast(every)

            def spread(v):
                return v.unsqueeze(2).to_broadcast(every)

            for i in range(2):
                of = low if i else lg
                dve.tensor_reduce(top[:, i, :], of[:, :, :], AX.X, ALU.max).then_inc(pick, 1)
                dve.wait_ge(pick, 4 * i + 1)
                dve.tensor_tensor(hit[:, :, :], of[:, :, :], spread(top[:, i, :]), ALU.is_equal).then_inc(pick, 1)
                dve.wait_ge(pick, 4 * i + 2)
                dve.tensor_tensor(hit[:, :, :], hit[:, :, :], order_b, ALU.mult).then_inc(pick, 1)
                dve.wait_ge(pick, 4 * i + 3)
                dve.tensor_reduce(first_at[:, :], hit[:, :, :], AX.X, ALU.min).then_inc(place, 1)
                dve.wait_ge(place, 3 * i + 1)
                dve.tensor_tensor(one_hot[:, i, :, :], order_b, spread(first_at[:, :]), ALU.is_equal).then_inc(place, 1)
                dve.wait_ge(place, 3 * i + 2)
                if i == 0:
                    dve.tensor_scalar(low[:, :, :], one_hot[:, 0, :, :], -3e38, None, ALU.mult).then_inc(place, 1)
                    dve.wait_ge(place, 3)
                    dve.tensor_tensor(low[:, :, :], low[:, :, :], lg[:, :, :], ALU.add).then_inc(pick, 1)
                    dve.wait_ge(pick, 4)
                else:
                    dve.tensor_tensor(taken[:, :, :], one_hot[:, 0, :, :], one_hot[:, 1, :, :], ALU.add).then_inc(taken_ready, 1)
                    dve.tensor_tensor(first_at[:, :], top[:, 1, :], top[:, 0, :], ALU.subtract).then_inc(pick, 1)
            dve.wait_ge(ex_ready, 1)
            dve.tensor_scalar(top[:, 0, :], ex[:, :], 1.0, None, ALU.add).then_inc(pick, 1)
            dve.wait_ge(pick, 9)
            dve.reciprocal(kit.gate[:, 0, :], top[:, 0, :]).then_inc(pick, 1)
            dve.wait_ge(pick, 10)
            dve.tensor_tensor(kit.gate[:, 1, :], kit.gate[:, 0, :], ex[:, :], ALU.mult).then_inc(pick, 1)
            dve.wait_ge(counts_ps, 1)
            dve.tensor_copy(rank[:, :, :], ps_r[:, :].rearrange("p (t e) -> p t e", e=E)).then_inc(place, 1)
            dve.tensor_copy(total[:, :, :], ps_n[:, :].rearrange("p (t e) -> p t e", e=E)).then_inc(place, 1)
            dve.wait_ge(place, 7)
            for e in range(E):
                last = dve.tensor_tensor_scan(upto[:, :, e], ones[:, :], total[:, :, e], 0.0, ALU.mult, ALU.add)
            last.then_inc(place, 1)
            dve.wait_ge(place, 8)
            dve.tensor_tensor(rank[:, :, :], rank[:, :, :], upto[:, :, :], ALU.add).then_inc(place, 1)
            dve.tensor_scalar(tiles_i[:, :], upto[:, NT - 1, :], float(R - 1), None, ALU.add).then_inc(place, 1)
            dve.wait_ge(place, 10)
            dve.tensor_tensor(rank[:, :, :], rank[:, :, :], total[:, :, :], ALU.subtract).then_inc(place, 1)
            dve.tensor_scalar(tiles_i[:, :], tiles_i[:, :], R.bit_length() - 1, None, ALU.logical_shift_right).then_inc(place, 1)
            dve.wait_ge(place, 12)
            dve.tensor_copy(tiles_f[:, :], tiles_i[:, :]).then_inc(place, 1)
            dve.wait_ge(place, 13)
            dve.tensor_tensor_scan(upto_e[:, :], ones[:, 0:E], tiles_f[:, :], 0.0, ALU.mult, ALU.add).then_inc(place, 1)
            dve.wait_ge(place, 14)
            dve.tensor_tensor(start_e[:, :], upto_e[:, :], tiles_f[:, :], ALU.subtract).then_inc(place, 1)
            dve.wait_ge(place, 15)
            dve.tensor_scalar(start_e[:, :], start_e[:, :], float(R), None, ALU.mult).then_inc(place, 1)
            dve.wait_ge(place, 16)
            dve.tensor_tensor(rank[:, :, :], rank[:, :, :], start_e[:, :].unsqueeze(1).to_broadcast(every), ALU.add)\
                .then_inc(place, 1)
            dve.wait_ge(place, 17)
            for i in range(2):
                dve.tensor_tensor(hit[:, :, :], one_hot[:, i, :, :], rank[:, :, :], ALU.mult).then_inc(place, 1)
                dve.wait_ge(place, 18 + 3 * i)
                dve.tensor_reduce(slot_f[:, :], hit[:, :, :], AX.X, ALU.add).then_inc(place, 1)
                dve.wait_ge(place, 19 + 3 * i)
                dve.tensor_copy(kit.slot[:, i, :], slot_f[:, :]).then_inc(place, 1)
                dve.wait_ge(place, 20 + 3 * i)
            whole = [P, SLOT_TILES, E]
            dve.tensor_tensor(past[:, :, :], tile_no[:, :].unsqueeze(2).to_broadcast(whole),
                              upto_e[:, :].unsqueeze(1).to_broadcast(whole), ALU.is_ge).then_inc(place, 1)
            dve.wait_ge(place, 24)
            dve.tensor_reduce(past_n[:, :], past[:, :, :], AX.X, ALU.add).then_inc(place, 1)
            dve.wait_ge(place, 25)
            dve.tensor_scalar(kit.expert[:, :], past_n[:, :], float(E - 1), None, ALU.min).then_inc(place, 1)
            dve.wait_ge(place, 26)

        @block.gpsimd
        def _(pool):
            pool.wait_ge(place, 23)
            for i in range(2):
                for t in range(NT):
                    pool.indirect_dma_start(out=kit.sorted_d, out_offset=bass.IndirectOffsetOnAxis(ap=kit.slot[:, i, t:t + 1], axis=0),
                                            in_=kit.x[:, t, :], in_offset=None).then_inc(moved, 16)
            pool.wait_ge(moved, 16 * 2 * NT)

        @block.tensor
        def _(pe):
            pe.wait_ge(misc_in, 16 * 5)

            def turn(j, par):
                pe.wait_ge(xn_ready, j + 1)
                for c in range(KC):
                    for t in range(PAIR):
                        last = pe.transpose(ps_x[:, c, P * t:P * (t + 1)], xn[:, par, t, P * c:P * (c + 1)], kit.ident[:, :])
                last.then_inc(x_ps, 1)

            def logits(j):
                pe.wait_ge(xnT_ready, j + 1)
                if not isinstance(j, int) or j > 0:
                    pe.wait_ge(lg_ready, j)
                for t in range(PAIR):
                    for c in range(KC):
                        last = pe.matmul(ps_l[:, t, :], xnT[:, c, P * t:P * (t + 1)], wr[:, c, :],
                                         start=c == 0, stop=c == KC - 1)
                last.then_inc(l_ps, 1)

            turn(0, 0)
            logits(0)
            with pe.Fori(1, NJ - 2, 2) as j:
                turn(j, 1)
                logits(j)
                turn(j + 1, 0)
                logits(j + 1)
            turn(NJ - 1, 1)
            logits(NJ - 1)
            pe.wait_ge(taken_ready, 1)
            pe.wait_ge(setup, 3)
            flat = taken[:, :, :].rearrange("p t e -> p (t e)")
            pe.matmul(ps_r[:, :], before_b[:, :], flat, start=True, stop=True)
            pe.matmul(ps_n[:, :], ones_b[:, :], flat, start=True, stop=True).then_inc(counts_ps, 1)


def experts(nc, kit, d):
    T = SLOT_TILES
    PAIRS_F = FC // 2
    TERMS = ((0, 0), (1, 0), (0, 1))
    with ExitStack() as ctx:
        def sb(name, shape, dt=F32):
            return ctx.enter_context(nc.sbuf_tensor("e_" + name, shape, dt))

        def sem(name):
            return ctx.enter_context(nc.semaphore("e_" + name))

        w1 = [sb(f"w1_{n}", [P, KC, FF], F32R) for n in ("high", "low")]
        w2 = [sb(f"w2_{n}", [P, FC, D], F32R) for n in ("high", "low")]
        rows = sb("rows", [P, RT, D])
        rowsT = [sb(f"rowsT{i}", [P, KC, R], F32R) for i in range(2)]
        b1 = sb("b1_now", [P, FC])
        h = sb("h", [P, 2, 2, R])
        hT = [sb(f"hT{i}", [P, 2, 2, R], F32R) for i in range(2)]
        y = sb("y", [P, RT, D])
        ps_x = ctx.enter_context(nc.psum_tensor("e_ps_x", [P, KC, R], F32))
        ps_h = ctx.enter_context(nc.psum_tensor("e_ps_h", [P, FC, R], F32))
        ps_y = ctx.enter_context(nc.psum_tensor("e_ps_y", [P, RT, D], F32))

        rows_in, y_out = sem("rows_in"), sem("y_out")
        x_ps, xT_high, xT_ready = sem("x_ps"), sem("xT_high"), sem("xT_ready")
        w1_high, w1_ready, w2_high, w2_ready = sem("w1_high"), sem("w1_ready"), sem("w2_high"), sem("w2_ready")
        b1_ready = sem("b1_ready")
        h_ps, h_whole, h_high, h_ready = sem("h_ps"), sem("h_whole"), sem("h_high"), sem("h_ready")
        y_ps, y_ready = sem("y_ps"), sem("y_ready")
        block = ctx.enter_context(nc.Block())

        def expert_of(eng, j):
            return eng.value_load(kit.expert[0:1, bass.ds(j, 1)], min_val=0, max_val=E - 1)

        def tiles(eng, body):
            body(0, True, False)
            with eng.Fori(1, T - 1) as j:
                body(j, False, False)
            body(T - 1, False, True)

        def w1_pair(w, p):
            return w[:, :, 2 * P * p:2 * P * (p + 1)]

        def w2_pair(w, p):
            return w[:, 2 * p:2 * (p + 1), :]

        @block.sync
        def _(sp):
            def load(j):
                sp.dma_start(rows[:, :, :], kit.sorted_d[bass.ds(j * R, R), :].rearrange("(t p) c -> p t c", p=P))\
                    .then_inc(rows_in, 16)

            load(0)

            def body(j, first, last):
                if not last:
                    sp.wait_ge(x_ps, j + 1)
                    load(j + 1)
                sp.wait_ge(y_ready, j + 1)
                sp.dma_start(kit.outs_d[bass.ds(j * R, R), :].rearrange("(t p) c -> p t c", p=P), y[:, :, :])\
                    .then_inc(y_out, 16)

            tiles(sp, body)
            sp.wait_ge(y_out, 16 * T)

        @block.scalar
        def _(act):
            def rows_high(j):
                act.wait_ge(x_ps, j + 1)
                act.activation(rowsT[0][:, :, :], ps_x[:, :, :], ACT.Copy).then_inc(xT_high, 1)

            def whole(j, p, first):
                n = PAIRS_F * j + p
                act.wait_ge(h_ps, n + 1)
                if p == 0:
                    act.wait_ge(b1_ready, j + 1)
                if not first or p >= 2:
                    act.wait_ge(h_ready, n - 1)
                for i in range(2):
                    f = 2 * p + i
                    last = act.activation(h[:, p % 2, i, :], ps_h[:, f, :], ACT.Relu, bias=b1[:, f:f + 1])
                last.then_inc(h_whole, 1)

            def high(j, p, first):
                n = PAIRS_F * j + p
                act.wait_ge(h_whole, n + 1)
                if not first or p >= 2:
                    act.wait_ge(y_ps, n - 1)
                act.activation(hT[0][:, p % 2, :, :], h[:, p % 2, :, :], ACT.Copy).then_inc(h_high, 1)

            rows_high(0)

            def body(j, first, last):
                for p in range(PAIRS_F):
                    whole(j, p, first)
                    high(j, p, first)
                if not last:
                    rows_high(j + 1)

            tiles(act, body)

        @block.gpsimd
        def _(pool):
            def weights_low(j, e, p):
                pool.wait_ge(w1_high, PAIRS_F * j + p + 1)
                pool.tensor_tensor(w1_pair(w1[1], p), kit.w1[:, e, :, 2 * P * p:2 * P * (p + 1)],
                                   w1_pair(w1[0], p).bitcast(F32), ALU.subtract).then_inc(w1_ready, 1)

            with pool.Fori(0, T) as j:
                e = expert_of(pool, j)
                for p in range(PAIRS_F):
                    weights_low(j, e, p)

        @block.vector
        def _(dve):
            def first_high(j, e, p, fresh):
                if not fresh:
                    dve.wait_ge(h_ps, PAIRS_F * (j - 1) + p + 1)
                dve.tensor_scalar(w1_pair(w1[0], p), kit.w1[:, e, :, 2 * P * p:2 * P * (p + 1)], 1.0, None, ALU.mult)\
                    .then_inc(w1_high, 1)

            def second_high(j, e, p, fresh):
                if not fresh:
                    dve.wait_ge(y_ps, PAIRS_F * (j - 1) + p + 1)
                dve.tensor_scalar(w2_pair(w2[0], p), kit.w2[:, e, 2 * p:2 * (p + 1), :], 1.0, None, ALU.mult)\
                    .then_inc(w2_high, 1)

            def second_low(j, e, p):
                dve.wait_ge(w2_high, PAIRS_F * j + p + 1)
                dve.tensor_tensor(w2_pair(w2[1], p), kit.w2[:, e, 2 * p:2 * (p + 1), :],
                                  w2_pair(w2[0], p).bitcast(F32), ALU.subtract).then_inc(w2_ready, 1)

            def rows_low(j):
                dve.wait_ge(xT_high, j + 1)
                dve.tensor_tensor(rowsT[1][:, :, :], ps_x[:, :, :], rowsT[0][:, :, :].bitcast(F32), ALU.subtract)\
                    .then_inc(xT_ready, 1)

            def bias_of(j, e):
                dve.tensor_scalar(b1[:, :], kit.b1[:, e, :], 1.0, None, ALU.mult).then_inc(b1_ready, 1)

            def low(j, p):
                dve.wait_ge(h_high, PAIRS_F * j + p + 1)
                dve.tensor_tensor(hT[1][:, p % 2, :, :], h[:, p % 2, :, :], hT[0][:, p % 2, :, :].bitcast(F32),
                                  ALU.subtract).then_inc(h_ready, 1)

            def finish(j, first):
                dve.wait_ge(y_ps, PAIRS_F * (j + 1))
                if not first:
                    dve.wait_ge(y_out, 16 * j)
                e = expert_of(dve, j)
                dve.tensor_tensor(y[:, :, :], ps_y[:, :, :], kit.b2[:, bass.ds(e, 1), :].to_broadcast([P, RT, D]),
                                  ALU.add).then_inc(y_ready, 1)

            e = expert_of(dve, 0)
            for p in range(PAIRS_F):
                first_high(0, e, p, True)
            bias_of(0, e)
            rows_low(0)
            for p in range(PAIRS_F):
                second_high(0, e, p, True)
            for p in range(PAIRS_F):
                second_low(0, e, p)

            def body(j, first, last):
                if not last:
                    e = expert_of(dve, j + 1)
                    first_high(j + 1, e, 0, False)
                low(j, 0)
                if not last:
                    first_high(j + 1, e, 1, False)
                low(j, 1)
                if not last:
                    first_high(j + 1, e, 2, False)
                    second_high(j + 1, e, 0, False)
                low(j, 2)
                if not last:
                    second_low(j + 1, e, 0)
                    first_high(j + 1, e, 3, False)
                    second_high(j + 1, e, 1, False)
                low(j, 3)
                if not last:
                    bias_of(j + 1, e)
                    second_low(j + 1, e, 1)
                    rows_low(j + 1)
                    second_high(j + 1, e, 2, False)
                    second_low(j + 1, e, 2)
                finish(j, first)
                if not last:
                    second_high(j + 1, e, 3, False)
                    second_low(j + 1, e, 3)

            tiles(dve, body)

        @block.tensor
        def _(pe):
            def turn_rows(j):
                pe.wait_ge(rows_in, 16 * (j + 1))
                for c in range(KC):
                    for t in range(RT):
                        last = pe.transpose(ps_x[:, c, P * t:P * (t + 1)], rows[:, t, P * c:P * (c + 1)], kit.ident[:, :])
                last.then_inc(x_ps, 1)

            def inner(j, p):
                pe.wait_ge(w1_ready, PAIRS_F * j + p + 1)
                if p == 0:
                    pe.wait_ge(xT_ready, j + 1)
                for f in (2 * p, 2 * p + 1):
                    for c in range(KC):
                        for a, b in TERMS:
                            last = pe.matmul(ps_h[:, f, :], w1[a][:, c, P * f:P * (f + 1)], rowsT[b][:, c, :],
                                             start=c == 0 and (a, b) == TERMS[0], stop=c == KC - 1 and (a, b) == TERMS[-1])
                last.then_inc(h_ps, 1)

            def outer(j, p, first):
                pe.wait_ge(h_ready, PAIRS_F * j + p + 1)
                pe.wait_ge(w2_ready, PAIRS_F * j + p + 1)
                if p == 0 and not first:
                    pe.wait_ge(y_ready, j)
                for t in range(RT):
                    for i in range(2):
                        for a, b in TERMS:
                            last = pe.matmul(ps_y[:, t, :], hT[a][:, p % 2, i, P * t:P * (t + 1)], w2[b][:, 2 * p + i, :],
                                             start=p == 0 and t == 0 and i == 0 and (a, b) == TERMS[0],
                                             stop=p == PAIRS_F - 1 and i == 1 and (a, b) == TERMS[-1],
                                             skip_group_check=True)
                last.then_inc(y_ps, 1)

            turn_rows(0)

            def body(j, first, last):
                inner(j, 0)
                inner(j, 1)
                inner(j, 2)
                outer(j, 0, first)
                inner(j, 3)
                outer(j, 1, first)
                if not last:
                    turn_rows(j + 1)
                outer(j, 2, first)
                outer(j, 3, first)

            tiles(pe, body)


def combine(nc, kit, out):
    N = 4
    with ExitStack() as ctx:
        x = ctx.enter_context(nc.sbuf_tensor("f_x", [P, NT, D], F32, side="right"))
        y = ctx.enter_context(nc.sbuf_tensor("f_y", [P, N, 2, D], F32))
        x_in = [ctx.enter_context(nc.semaphore(f"f_x_in{i}")) for i in range(4)]
        y_in = [ctx.enter_context(nc.semaphore(f"f_y_in{i}")) for i in range(N)]
        half_sum, row_sum, stored = (ctx.enter_context(nc.semaphore("f_" + n)) for n in ("half_sum", "row_sum", "stored"))
        block = ctx.enter_context(nc.Block())
        n4 = NT // 4

        @block.sync
        def _(sp):
            for i in range(4):
                sp.dma_start(x[:, n4 * i:n4 * (i + 1), :],
                             kit.x_d[P * n4 * i:P * n4 * (i + 1), :].rearrange("(t p) c -> p t c", p=P)).then_inc(x_in[i], 16)
            for i in range(8):
                sp.wait_ge(x_in[4 * i // n4], 16)
                sp.wait_ge(row_sum, 4 * (i + 1))
                sp.dma_start(out[P * 4 * i:P * 4 * (i + 1), :].rearrange("(t p) c -> p t c", p=P),
                             x[:, 4 * i:4 * (i + 1), :]).then_inc(stored, 16)
            sp.wait_ge(stored, 16 * 8)

        @block.gpsimd
        def _(pool):
            for t in range(NT):
                if t >= N:
                    pool.wait_ge(y_in[t % N], 32 * (t // N))
                    pool.wait_ge(row_sum, t - N + 1)
                for i in range(2):
                    pool.indirect_dma_start(out=y[:, t % N, i, :], out_offset=None, in_=kit.outs_d,
                                            in_offset=bass.IndirectOffsetOnAxis(ap=kit.slot[:, i, t:t + 1], axis=0))\
                        .then_inc(y_in[t % N], 16)

        @block.vector
        def _(dve):
            for t in range(NT):
                if t % n4 == 0:
                    dve.wait_ge(x_in[t // n4], 16)
                dve.wait_ge(y_in[t % N], 32 * (t // N + 1))
                for i in range(2):
                    dve.scalar_tensor_tensor(out=x[:, t, :], in0=y[:, t % N, i, :], scalar=kit.gate[:, i, t:t + 1],
                                             in1=x[:, t, :], op0=ALU.mult, op1=ALU.add).then_inc((half_sum, row_sum)[i], 1)
                    if i == 0:
                        dve.wait_ge(half_sum, t + 1)


def network(nc, d, out):
    with ExitStack() as ctx:
        kit = Kit()
        x_rows = ctx.enter_context(ExitStack())
        kit.x = x_rows.enter_context(nc.sbuf_tensor("x_rows", [P, NT, D], F32, side="right"))
        kit.mv = ctx.enter_context(nc.sbuf_tensor("mean_var", [P, NT, 2], F32))
        kit.ident = ctx.enter_context(nc.sbuf_tensor("identity", [P, P], F32))
        kit.ident_d = d["ident"]
        kit.sorted_d = nc.dram_tensor("sorted_rows", [SLOT_TILES * R, D], F32, kind="Internal").ap()
        kit.outs_d = nc.dram_tensor("expert_rows", [SLOT_TILES * R, D], F32, kind="Internal").ap()
        kit.q_parts_d = nc.dram_tensor("q_parts", [2, 3, D, S], BF16, kind="Internal").ap()
        kit.k_parts_d = nc.dram_tensor("k_parts", [2, 3, D, S], BF16, kind="Internal").ap()
        kit.x_d = nc.dram_tensor("x_waiting", [NT * P, D], F32, kind="Internal").ap()

        def of(prefix):
            return {k[len(prefix):]: v for k, v in d.items() if k.startswith(prefix)} | \
                {k: d[k] for k in ("ctxT", "head_of", "mask")}

        load_x(nc, kit, d["x"])
        for phase, prefix in ((attend_keys, "A_"), (channel_mix, "B_"), (attend_heads, "C_")):
            with nc.cleanup_on_exit():
                phase(nc, kit, of(prefix))
        with ExitStack() as moe:
            kit.w1 = moe.enter_context(nc.sbuf_tensor("w1", [P, E, KC, FF], F32))
            kit.w2 = moe.enter_context(nc.sbuf_tensor("w2", [P, E, FC, D], F32))
            kit.b1 = moe.enter_context(nc.sbuf_tensor("b1", [P, E, FC], F32))
            kit.b2 = moe.enter_context(nc.sbuf_tensor("b2", [P, E, D], F32))
            kit.gate = moe.enter_context(nc.sbuf_tensor("gate", [P, 2, NT], F32))
            kit.slot = moe.enter_context(nc.sbuf_tensor("slot", [P, 2, NT], U32))
            kit.expert = moe.enter_context(nc.sbuf_tensor("expert", [P, SLOT_TILES], I32))
            kit.w_in = moe.enter_context(nc.semaphore("w_in"))
            route(nc, kit, of("D_"))
            x_rows.close()
            experts(nc, kit, of("D_"))
            combine(nc, kit, out)


def kernel(**inputs):
    from concourse import bacc
    from concourse.bass_utils import run_bass_kernel_spmd

    def turned(w):
        return np.ascontiguousarray(w.T)

    def columns(v):
        return np.ascontiguousarray(v.reshape(-1, P).T)

    def to_all(v):
        return np.ascontiguousarray(np.broadcast_to(v, (P,) + v.shape))

    split_order = np.arange(D).reshape(H, DK).T.reshape(P, KC).T.reshape(D)
    z = {k: np.asarray(v) for k, v in inputs.items()}
    a = {"x": z["x"].reshape(B * S, D), "ctxT": turned(z["ctx_1024"].reshape(B * S, D)),
         "mask": z["mask_1x1xSxS2_ik0"].reshape(S, S), "ident": np.eye(P, dtype=np.float32),
         "head_of": np.repeat(np.eye(HC, dtype=np.float32), DK, 0)}
    for to, p in (("A_", "L0_xattn_"), ("C_", "L1_xattn_")):
        for w in "qkvo":
            a[f"{to}w{w}T"] = turned(z[f"{p}W{w}"])
        for b in "qk":
            a[f"{to}w{b}T"] = np.ascontiguousarray(a[f"{to}w{b}T"][:, split_order])
            a[f"{to}b{b}"] = columns(z[f"{p}b{b}"][split_order])
        for b in "vo":
            a[f"{to}b{b}"] = to_all(z[f"{p}b{b}"])
    spaced = np.zeros((H, 2 * DK, D), np.float32)
    spaced[:, :DK] = a["C_woT"].reshape(H, DK, D)
    a["C_woT"] = spaced.reshape(2 * D, D)
    for w in "rkv":
        a[f"B_w{w}T"] = turned(z[f"L0_ffn_W_{w}"])
    for m in "rk":
        a[f"B_mu_{m}"] = columns(z[f"L0_ffn_mu_{m}"])
    a["D_w1"], a["D_w2"] = z["L1_ffn_W1"], z["L1_ffn_W2"]
    a["D_b1"] = np.ascontiguousarray(z["L1_ffn_b1"].reshape(E, FC, P).transpose(2, 0, 1))
    a["D_b2"] = to_all(z["L1_ffn_b2"])
    a["D_wr"], a["D_br"] = z["L1_ffn_router_w"], to_all(z["L1_ffn_router_b"])
    a["D_order"] = to_all(np.arange(-E, 0, dtype=np.float32))
    a["D_tile_no"] = to_all(np.arange(SLOT_TILES, dtype=np.float32))
    a["D_before"] = np.triu(np.ones((P, P), np.float32), 1)

    nc = bacc.Bacc("TRN2", target_bir_lowering=False, num_devices=1)
    d = {k: nc.dram_tensor("in_" + k, v.shape, mybir.dt.from_np(v.dtype), kind="ExternalInput").ap() for k, v in a.items()}
    out = nc.dram_tensor("out", [B * S, D], F32, kind="ExternalOutput").ap()
    network(nc, d, out)
    r = run_bass_kernel_spmd(nc, [{"in_" + k: v for k, v in a.items()}], core_ids=[0])
    return r.results[0]["out"].reshape(B, S, D)
```

```python
from contextlib import ExitStack

import numpy as np

import concourse.bass as bass
from concourse import mybir

F32 = mybir.dt.float32
BF16 = mybir.dt.bfloat16
F32R = mybir.dt.float32r
I32 = mybir.dt.int32
U32 = mybir.dt.uint32
ALU = mybir.AluOpType
ACT = mybir.ActivationFunctionType
AX = mybir.AxisListType

P = 128
B, S, D = 16, 256, 256
H = 16
DK = D // H
QT = S // P
NT = B * QT
KC = D // P
G = 4
E, FF = 8, 1024
FC = FF // P
R = 2 * P
RT = R // P
SLOT_TILES = (2 * B * S + E * (R - 1)) // R
Q_PART, K_PART = (0, 1, 2, 0, 1, 0), (0, 0, 0, 1, 1, 2)
PAIRS = len(Q_PART)
SCALE = DK ** -0.5
EPS = 1e-5
MASKED = -1e30


class Kit:
    pass


def keep_rows(dve, kit, tiles, upd, xnew, stats, aggr, x_ready, i):
    n = upd.shape[1]
    dve.tensor_tensor(xnew[:, :, :], kit.x[:, tiles, :], upd[:, :, :], ALU.add).then_inc(x_ready, 1)
    dve.wait_ge(x_ready, 3 * i + 1)
    for t in range(n):
        last = dve.bn_stats(stats[:, t, :], xnew[:, t, :])
    last.then_inc(x_ready, 1)
    dve.wait_ge(x_ready, 3 * i + 2)
    dve.tensor_scalar(kit.x[:, tiles, :], xnew[:, :, :], 1.0, None, ALU.mult)
    for t in range(n):
        last = dve.bn_aggr(aggr[:, t, :], stats[:, t, :])
    last.then_inc(x_ready, 1)
    dve.wait_ge(x_ready, 3 * i + 3)
    dve.tensor_scalar(kit.mv[:, tiles, :], aggr[:, :, :], 1.0, None, ALU.mult)


class Split:

    def __init__(self, nc, ctx, name, parts_d, part_of_pair, zero=None):
        def sb(n, shape, dt=BF16):
            return ctx.enter_context(nc.sbuf_tensor(f"{name}_{n}", shape, dt))

        def sem(n):
            return nc.alloc_semaphore(f"{name}_{n}")

        self.parts_d, self.part_of_pair = parts_d, part_of_pair
        if zero is not None:
            self.zero = zero
            self.whole, self.rest = sb("whole", [P, KC, S], F32), sb("rest", [P, KC, S], F32)
            self.taken = sem("taken")
        else:
            self.subtracted = sem("subtracted")
        self.parts = sb("parts", [P, 2, 3, KC, S])
        self.stacked = sb("stacked", [PAIRS * DK, 2, H, S])
        self.parting, self.parted = sem("parting"), sem("parted")
        self.written, self.stacks = [sem("written0"), sem("written1")], [sem("stack0"), sem("stack1")]

    def take(self, act, b, ps, bias):
        if not isinstance(b, int) or b > 0:
            act.wait_ge(self.parted, b)
        for c in range(KC):
            last = act.activation(self.whole[:, c, :], ps[:, c, :], ACT.Identity, bias=bias[:, c:c + 1])
        last.then_inc(self.taken, 1)

    def split(self, eng, b, par):
        high, middle, low = (self.parts[:, par, j, :, :] for j in range(3))
        eng.wait_ge(self.taken, b + 1)
        if not isinstance(b, int) or b >= 2:
            eng.wait_ge(self.written[par], (b - par) * 8)
        eng.tensor_tensor(high, self.whole[:, :, :], self.zero[:, 0:1].unsqueeze(2).to_broadcast([P, KC, S]), ALU.add)\
            .then_inc(self.parting, 1)
        eng.wait_ge(self.parting, 2 * b + 1)
        eng.tensor_tensor(self.rest[:, :, :], self.whole[:, :, :], high, ALU.subtract)
        eng.tensor_tensor(middle, self.whole[:, :, :], high, ALU.subtract).then_inc(self.parting, 1)
        eng.wait_ge(self.parting, 2 * b + 2)
        eng.tensor_tensor(low, self.rest[:, :, :], middle, ALU.subtract).then_inc(self.parted, 1)

    def take_part(self, act, b, par, j, ready, ps, bias):
        if j == 0:
            if not isinstance(b, int) or b >= 2:
                act.wait_ge(self.written[par], (b - par) * 8)
            act.wait_ge(ready, b + 1)
        else:
            act.wait_ge(self.subtracted, 2 * b + j)
        for c in range(KC):
            last = act.activation(self.parts[:, par, j, c, :], ps[:, c, :], ACT.Identity, bias=bias[:, c:c + 1])
        last.then_inc(self.parted if j == 2 else self.parting, 1)

    def subtract(self, pe, b, par, j, ps, minus_i):
        pe.wait_ge(self.parting, 2 * b + j + 1)
        pe.matmul(ps[:, :, :], minus_i[:, :], self.parts[:, par, j, :, :], start=False, stop=True,
                  skip_group_check=True).then_inc(self.subtracted, 1)

    def write(self, sp, b, par):
        sp.wait_ge(self.parted, b + 1)
        sp.dma_start(self.parts_d[par].rearrange("j (p c) t -> p j c t", c=KC), self.parts[:, par, :, :, :])\
            .then_inc(self.written[par], 16)

    def stack(self, sp, b, par):
        sp.wait_ge(self.written[par], (b - par) * 8 + 16)
        rows = self.parts_d[par].rearrange("j (d h) t -> j d h t", h=H)
        i = 0
        for n in (3, 2, 1):
            j = self.part_of_pair[i]
            src = rows[j:j + 1, :, :, :].to_broadcast([n, DK, H, S]) if self.part_of_pair is K_PART else rows[j:j + n, :, :, :]
            sp.dma_start(self.stacked[DK * i:DK * (i + n), par, :, :], src).then_inc(self.stacks[par], 16)
            i += n

    def wait_stacked(self, pe, b, par):
        pe.wait_ge(self.stacks[par], (b - par) * 24 + 48)


def attend_keys(nc, kit, d):
    U = H // 2
    n4 = NT // 4
    PARTS = slice(0, n4), slice(n4, NT)
    with ExitStack() as ctx:
        def sb(name, shape, dt=F32):
            return ctx.enter_context(nc.sbuf_tensor("a_" + name, shape, dt))

        def sem(name):
            return nc.alloc_semaphore("a_" + name)

        wq, wk, wv, wo = (sb(n, [P, KC, D]) for n in ("wq", "wk", "wv", "wo"))
        bq, bk = sb("bq", [P, KC]), sb("bk", [P, KC])
        bv = sb("bv", [P, D])
        all_stats = sb("all_stats", [P, NT, 6])
        added = sb("added", [P, QT, D])
        mask_i = sb("mask_i", [P, QT, S], I32)
        mask_b = sb("mask_b", [P, QT, S], BF16)
        ident_b = sb("ident_b", [P, P], BF16)
        seen = sb("seen", [P, 3, QT])
        rstd = sb("rstd", [P, 2, NT])
        zeros = sb("zeros", [P, D])
        ctxT = sb("ctxT", [P, 2, KC, S])
        centred, xn = sb("centred", [P, QT, D]), sb("xn", [P, QT, D])
        xnT = sb("xnT", [P, KC, S])
        q, k = Split(nc, ctx, "a_q", kit.q_parts_d, Q_PART, zeros), Split(nc, ctx, "a_k", kit.k_parts_d, K_PART, zeros)
        va = sb("va", [P, 2, QT, H, 2 * DK])
        mx, nmx = sb("mx", [P, 2, 4]), sb("nmx", [P, 2, 4])
        pr = sb("pr", [P, 2, 4, S])
        prT = sb("prT", [P, 4, 2, QT, S])
        oT = sb("oT", [P, 2, H // G, S])
        rden = sb("rden", [P, QT, H])
        on = sb("on", [P, QT, D])
        onT = sb("onT", [P, KC, S])
        upd = sb("upd", [P, QT, D])
        xnew = sb("xnew", [P, QT, D])
        stats, aggr = sb("stats", [P, QT, 6]), sb("aggr", [P, QT, 2])

        ps_step = ctx.enter_context(nc.psum_tensor("a_ps_step", [P, 512], F32))
        ps_o = ctx.enter_context(nc.psum_tensor("a_ps_o", [P, 512], F32))
        ps_s = ctx.enter_context(nc.psum_tensor("a_ps_s", [P, 2, 2, QT, S], F32))
        ps_t = ctx.enter_context(nc.psum_tensor("a_ps_t", [P, 2, QT, S], F32))
        step4 = ps_step[:, :].rearrange("p (a b) -> p a b", a=2)

        w_in, misc_in, ident_in = sem("w_in"), sem("misc_in"), sem("ident_in")
        x_in = [sem(f"x_in{i}") for i in range(4)]
        part_stats, var_ready = sem("part_stats"), sem("var_ready")
        ctx_in = [sem("ctx_in0"), sem("ctx_in1")]
        setup = sem("setup")
        sd_ready = sem("sd_ready")
        ones_ready = sem("ones_ready")
        centred_ready, xn_ready, xnT_ps, xnT_ready = sem("centred_ready"), sem("xn_ready"), sem("xnT_ps"), sem("xnT_ready")
        k_ps, q_ps = sem("k_ps"), sem("q_ps")
        v_ps, v_ready = sem("v_ps"), sem("v_ready")
        s_ps, mx_ready, nmx_ready, pr_ready = sem("s_ps"), sem("mx_ready"), sem("nmx_ready"), sem("pr_ready")
        t_ps, prT_dve, prT_act = sem("t_ps"), sem("prT_dve"), sem("prT_act")
        o_ps, oT_ready = sem("o_ps"), sem("oT_ready")
        back_ps, rden_ready, on_ready = sem("back_ps"), sem("rden_ready"), sem("on_ready")
        onT_ps, onT_ready = sem("onT_ps"), sem("onT_ready")
        y_ps, upd_ready, x_ready = sem("y_ps"), sem("upd_ready"), sem("x_ready")
        block = ctx.enter_context(nc.Block())

        def batches(eng, body):
            body(0, 0, True, False)
            with eng.Fori(1, B - 2, 2) as b:
                body(b, 1, False, False)
                body(b + 1, 0, False, False)
            body(B - 1, 1, False, True)

        @block.sync
        def _(sp):
            def load_x(i):
                sp.dma_start(kit.x[:, n4 * i:n4 * (i + 1), :],
                             d["x"][P * n4 * i:P * n4 * (i + 1), :].rearrange("(t p) c -> p t c", p=P)).then_inc(x_in[i], 16)

            load_x(0)
            for buf, w in ((wk, "wkT"), (wq, "wqT"), (wv, "wvT"), (wo, "woT")):
                sp.dma_start(buf[:, :, :], d[w].rearrange("(c p) n -> p c n", p=P)).then_inc(w_in, 16)

            def load(b, par):
                sp.dma_start(ctxT[:, par, :, :], d["ctxT"][:, bass.ds(b * S, S)].rearrange("(c p) n -> p c n", p=P))\
                    .then_inc(ctx_in[par], 16)

            load(0, 0)
            load_x(1)
            load(1, 1)
            load_x(2)
            load_x(3)
            for b, parts in ((0, (k, q)), (1, (q, k))):
                for part in parts:
                    part.write(sp, b, b)
                for part in parts:
                    part.stack(sp, b, b)
            with sp.Fori(2, B - 1, 2) as b:
                sp.wait_ge(v_ready, b - 1)
                load(b, 0)
                q.write(sp, b, 0)
                k.write(sp, b, 0)
                q.stack(sp, b, 0)
                k.stack(sp, b, 0)
                sp.wait_ge(v_ready, b)
                load(b + 1, 1)
                q.write(sp, b + 1, 1)
                k.write(sp, b + 1, 1)
                q.stack(sp, b + 1, 1)
                k.stack(sp, b + 1, 1)

        @block.scalar
        def _(act):
            act.dma_start(kit.ident[:, :], kit.ident_d).then_inc(ident_in, 16)
            act.dma_start(mask_i[:, :, :], d["mask"].rearrange("(t p) k -> p t k", p=P)).then_inc(misc_in, 16)
            for buf, n in ((bq, "bq"), (bk, "bk"), (bv, "bv")):
                act.dma_start(buf[:, :], d[n]).then_inc(misc_in, 16)
            for t in range(QT):
                act.dma_start(added[:, t, :], d["bo"]).then_inc(misc_in, 16)
            def deviations(i):
                act.wait_ge(var_ready, i + 1)
                act.activation(rstd[:, 1, PARTS[i]], rstd[:, 0, PARTS[i]], ACT.Sqrt).then_inc(sd_ready, 1)

            deviations(0)
            act.wait_ge(misc_in, 16 * (4 + QT))

            def step_xnT(b):
                act.wait_ge(xnT_ps, b + 1)
                act.activation(xnT[:, :, :], step4, ACT.Copy).then_inc(xnT_ready, 1)

            def step_k(b):
                act.wait_ge(k_ps, b + 1)
                k.take(act, b, step4, bk)

            def step_q(b):
                act.wait_ge(q_ps, b + 1)
                q.take(act, b, step4, bq)

            def numerators(b, u, par):
                n = b * U + u
                for i in range(2):
                    act.wait_ge(nmx_ready, 2 * n + i + 1)
                    for t in range(QT):
                        last = act.activation(pr[:, par, QT * i + t, :], ps_s[:, par, i, t, :], ACT.Exp,
                                              bias=nmx[:, par, QT * i + t:QT * i + t + 1], scale=SCALE)
                    last.then_inc(pr_ready, 1)

            step_k(0)
            step_xnT(0)
            step_q(0)
            deviations(1)
            numerators(0, 0, 0)

            def body(b, par, first, last):
                for u in range(U):
                    if u == 0 and not last:
                        step_xnT(b + 1)
                    if not (last and u == U - 1):
                        numerators(b, u + 1, (u + 1) % 2)
                    if u == 0 and not last:
                        step_q(b + 1)
                    if u == 1 and not last:
                        step_k(b + 1)
                    if u == 6 and not first:
                        act.wait_ge(onT_ps, b)
                        act.activation(onT[:, :, :], step4, ACT.Copy).then_inc(onT_ready, 1)
                    act.wait_ge(t_ps, 2 * (b * U + u) + 2)
                    act.activation(prT[:, u % 4, 1, :, :], ps_t[:, 1, :, :], ACT.Copy).then_inc(prT_act, 1)

            batches(act, body)
            act.wait_ge(onT_ps, B)
            act.activation(onT[:, :, :], step4, ACT.Copy).then_inc(onT_ready, 1)

        @block.gpsimd
        def _(pool):
            pool.memset(va[:, :, :, :, :], 1.0).then_inc(ones_ready, 1)
            pool.memset(zeros[:, :], 0.0).then_inc(ones_ready, 1)
            pool.wait_ge(ones_ready, 2)

            def normalize(b):
                if not isinstance(b, int) or b > 0:
                    pool.wait_ge(xnT_ps, b)
                rows = bass.ds(QT * b, QT)
                pool.tensor_tensor(centred[:, :, :], kit.x[:, rows, :], kit.mv[:, rows, 0:1].to_broadcast([P, QT, D]),
                                   ALU.subtract).then_inc(centred_ready, 1)
                pool.wait_ge(centred_ready, b + 1)
                pool.tensor_tensor(xn[:, :, :], centred[:, :, :],
                                   rstd[:, 0, rows].unsqueeze(2).to_broadcast([P, QT, D]), ALU.mult).then_inc(xn_ready, 1)

            k.split(pool, 0, 0)
            pool.wait_ge(setup, 9)
            normalize(0)
            q.split(pool, 0, 0)
            normalize(1)
            q.split(pool, 1, 1)
            k.split(pool, 1, 1)
            pool.wait_ge(upd_ready, 1)
            with pool.Fori(2, B - 1, 2) as b:
                for i in range(2):
                    normalize(b + i)
                    q.split(pool, b + i, i)
                    k.split(pool, b + i, i)

        @block.vector
        def _(dve):
            def statistics(i):
                tiles = range(NT)[PARTS[i]]
                for t in tiles:
                    if t % n4 == 0:
                        dve.wait_ge(x_in[t // n4], 16)
                    dve.bn_stats(all_stats[:, t, :], kit.x[:, t, :]).then_inc(part_stats, 1)
                for t in tiles:
                    dve.wait_ge(part_stats, t + i + 1)
                    last = dve.bn_aggr(kit.mv[:, t, :], all_stats[:, t, :])
                last.then_inc(part_stats, 1)
                dve.wait_ge(part_stats, tiles[-1] + i + 2)
                dve.tensor_scalar(rstd[:, 0, PARTS[i]], kit.mv[:, PARTS[i], 1], EPS, None, ALU.add).then_inc(var_ready, 1)

            statistics(0)
            dve.wait_ge(ident_in, 16)
            dve.tensor_copy(ident_b[:, :], kit.ident[:, :]).then_inc(setup, 1)
            dve.wait_ge(sd_ready, 1)
            dve.reciprocal(rstd[:, 0, PARTS[0]], rstd[:, 1, PARTS[0]]).then_inc(setup, 1)
            dve.wait_ge(misc_in, 16 * (4 + QT))
            dve.tensor_scalar(mask_b[:, :, :], mask_i[:, :, :], 0.0, MASKED, ALU.is_equal, ALU.mult).then_inc(setup, 1)
            dve.wait_ge(setup, 3)
            dve.tensor_reduce(seen[:, 0, :], mask_b[:, :, :], AX.X, ALU.max).then_inc(setup, 1)
            dve.wait_ge(setup, 4)
            dve.tensor_scalar(seen[:, 1, :], seen[:, 0, :], 0.0, None, ALU.is_equal).then_inc(setup, 1)
            dve.wait_ge(setup, 5)
            dve.reciprocal(seen[:, 2, :], seen[:, 1, :]).then_inc(setup, 1)
            dve.wait_ge(setup, 6)
            dve.tensor_scalar(seen[:, 0, :], seen[:, 2, :], 0.0, None, ALU.mult).then_inc(setup, 1)
            dve.wait_ge(setup, 7)
            for t in range(QT):
                dve.tensor_scalar(added[:, t, :], added[:, t, :], seen[:, 0, t:t + 1], None, ALU.add).then_inc(setup, 1)
            dve.wait_ge(ones_ready, 1)

            def step_v(b, par):
                dve.wait_ge(v_ps, b + 1)
                dve.tensor_tensor(va[:, par, :, :, 0:DK],
                                  ps_step[:, :].rearrange("p (t h k) -> p t h k", t=QT, h=H),
                                  bv[:, :].rearrange("p (h k) -> p h k", h=H).unsqueeze(1).to_broadcast([P, QT, H, DK]),
                                  ALU.add).then_inc(v_ready, 1)

            def maxima(b, u, par):
                n = b * U + u
                if not isinstance(b, int) or n >= 2:
                    dve.wait_ge(pr_ready, 2 * (n - 1))
                for i in range(2):
                    rows = slice(QT * i, QT * (i + 1))
                    dve.wait_ge(s_ps, 2 * n + i + 1)
                    dve.tensor_reduce(mx[:, par, rows], ps_s[:, par, i, :, :], AX.X, ALU.max).then_inc(mx_ready, 1)
                    dve.wait_ge(mx_ready, 2 * n + i + 1)
                    dve.tensor_scalar(nmx[:, par, rows], mx[:, par, rows], -SCALE, None, ALU.mult).then_inc(nmx_ready, 1)

            def step_back(b, half):
                dve.wait_ge(back_ps, 2 * b + half + 1)
                back = ps_step[:, :].rearrange("p (t h k) -> p t h k", t=QT, k=2 * DK)
                h0 = half * 2 * G
                dve.reciprocal(rden[:, :, h0:h0 + 2 * G], back[:, :, :, DK]).then_inc(rden_ready, 1)
                dve.wait_ge(rden_ready, 2 * b + half + 1)
                dve.tensor_tensor(on[:, :, h0 * DK:(h0 + 2 * G) * DK].rearrange("p t (h k) -> p t h k", k=DK),
                                  back[:, :, :, 0:DK],
                                  rden[:, :, h0:h0 + 2 * G].unsqueeze(3).to_broadcast([P, QT, 2 * G, DK]),
                                  ALU.mult).then_inc(on_ready, 1)

            def step_y(b):
                dve.wait_ge(y_ps, b + 1)
                dve.tensor_tensor(upd[:, :, :], step4, added[:, :, :], ALU.add).then_inc(upd_ready, 1)
                dve.wait_ge(upd_ready, b + 2)

            step_v(0, 0)
            statistics(1)
            dve.wait_ge(sd_ready, 2)
            dve.reciprocal(rstd[:, 0, PARTS[1]], rstd[:, 1, PARTS[1]]).then_inc(upd_ready, 1)
            maxima(0, 0, 0)
            maxima(0, 1, 1)

            def body(b, par, first, last):
                for u in range(U):
                    dve.wait_ge(t_ps, 2 * (b * U + u) + 1)
                    dve.tensor_copy(prT[:, u % 4, 0, :, :], ps_t[:, 0, :, :]).then_inc(prT_dve, 1)
                    if u == 3 and not last:
                        step_v(b + 1, 1 - par)
                    if u == 4 and not first:
                        step_back(b - 1, 0)
                    if u == 5 and not first:
                        step_back(b - 1, 1)
                    if u == 7 and not first:
                        step_y(b - 1)
                    if not (last and u >= U - 2):
                        maxima(b, u + 2, u % 2)
                    if u % 2 == 0 and not (first and u == 0):
                        dve.wait_ge(o_ps, b * (H // G) + u // 2)
                        take_group((u // 2 - 1) % (H // G), 1 - par if u == 0 else par)
                    if u == 7 and not first:
                        keep_rows(dve, kit, bass.ds(QT * (b - 1), QT), upd, xnew, stats, aggr, x_ready, b - 1)

            def take_group(group, par):
                dve.tensor_copy(oT[:, par, group, :], ps_o[:, 0:S]).then_inc(oT_ready, 1)

            batches(dve, body)
            dve.wait_ge(o_ps, B * H // G)
            take_group(H // G - 1, 1)
            step_back(B - 1, 0)
            step_back(B - 1, 1)
            step_y(B - 1)
            keep_rows(dve, kit, bass.ds(QT * (B - 1), QT), upd, xnew, stats, aggr, x_ready, B - 1)

        @block.tensor
        def _(pe):
            pe.wait_ge(ident_in, 16)
            pe.wait_ge(w_in, 64)

            def product(out, lhsT, rhs, n):
                for c in range(n):
                    last = pe.matmul(out, lhsT(c), rhs(c), start=c == 0, stop=c == n - 1)
                return last

            def step_xnT(b):
                pe.wait_ge(xn_ready, b + 1)
                for c in range(KC):
                    for t in range(QT):
                        last = pe.transpose(step4[:, c, P * t:P * (t + 1)], xn[:, t, P * c:P * (c + 1)], kit.ident[:, :])
                last.then_inc(xnT_ps, 1)

            def step_k(b, par, bank_free):
                pe.wait_ge(ctx_in[par], (b - par) * 8 + 16)
                if bank_free:
                    pe.wait_ge(*bank_free)
                for m in range(KC):
                    last = product(step4[:, m, :], lambda c: wk[:, c, P * m:P * (m + 1)], lambda c: ctxT[:, par, c, :], KC)
                last.then_inc(k_ps, 1)

            def step_q(b):
                pe.wait_ge(xnT_ready, b + 1)
                for m in range(KC):
                    last = product(step4[:, m, :], lambda c: wq[:, c, P * m:P * (m + 1)], lambda c: xnT[:, c, :], KC)
                last.then_inc(q_ps, 1)

            def step_v(b, par, bank_free):
                pe.wait_ge(*bank_free)
                for t in range(QT):
                    last = product(step4[:, t, :], lambda c: ctxT[:, par, c, P * t:P * (t + 1)], lambda c: wv[:, c, :], KC)
                last.then_inc(v_ps, 1)

            def step_back(b, par, half, bank_free):
                pe.wait_ge(*bank_free)
                pe.wait_ge(oT_ready, b * (H // G) + 2 * half + 2)
                for t in range(QT):
                    for i in range(2):
                        last = pe.transpose(ps_step[:, (2 * t + i) * P:(2 * t + i + 1) * P],
                                            oT[:, par, 2 * half + i, P * t:P * (t + 1)], kit.ident[:, :])
                last.then_inc(back_ps, 1)

            def step_onT(b, bank_free):
                pe.wait_ge(*bank_free)
                pe.wait_ge(on_ready, 2 * b + 2)
                for c in range(KC):
                    for t in range(QT):
                        last = pe.transpose(step4[:, c, P * t:P * (t + 1)], on[:, t, P * c:P * (c + 1)], kit.ident[:, :])
                last.then_inc(onT_ps, 1)

            def step_y(b):
                pe.wait_ge(onT_ready, b + 1)
                for t in range(QT):
                    last = product(step4[:, t, :], lambda c: onT[:, c, P * t:P * (t + 1)], lambda c: wo[:, c, :], KC)
                last.then_inc(y_ps, 1)

            def scores(b, u, par, i):
                if u == 0 and i == 0:
                    q.wait_stacked(pe, b, par)
                    k.wait_stacked(pe, b, par)
                pe.matmul(ps_s[:, u % 2, i, :, :], ident_b[:, :], mask_b[:, :, :], start=True, stop=False)
                for t in range(QT):
                    last = pe.matmul(ps_s[:, u % 2, i, t, :], q.stacked[:, par, 2 * u + i, P * t:P * (t + 1)],
                                     k.stacked[:, par, 2 * u + i, :], start=False, stop=t == QT - 1)
                last.then_inc(s_ps, 1)

            def turn(b, u, i):
                n = b * U + u
                pe.wait_ge(pr_ready, 2 * n + i + 1)
                if not isinstance(b, int) or n >= 1:
                    pe.wait_ge((prT_dve, prT_act)[i], n)
                for k in range(QT):
                    for t in range(QT):
                        last = pe.transpose(ps_t[:, i, k, P * t:P * (t + 1)],
                                            pr[:, u % 2, 2 * i + t, P * k:P * (k + 1)], kit.ident[:, :])
                last.then_inc(t_ps, 1)

            def values(b, group, par):
                n = b * U + 2 * group
                if group == 0:
                    pe.wait_ge(v_ready, b + 1)
                if not isinstance(b, int) or n > 0:
                    pe.wait_ge(oT_ready, b * (H // G) + group)
                pe.wait_ge(prT_dve, n + 2)
                pe.wait_ge(prT_act, n + 2)
                for k in range(QT):
                    for h in range(G):
                        last = pe.matmul(ps_o[2 * DK * h:2 * DK * (h + 1), 0:S], va[:, par, k, G * group + h, :],
                                         prT[:, (2 * group + h // 2) % 4, h % 2, k, :],
                                         start=k == 0, stop=k == QT - 1)
                last.then_inc(o_ps, 1)

            step_k(0, 0, None)
            step_v(0, 0, (k.taken, 1))
            pe.wait_ge(v_ready, 1)
            step_xnT(0)
            step_q(0)
            pe.wait_ge(q.taken, 1)
            pe.wait_ge(setup, 3)
            for u in range(2):
                for i in range(2):
                    scores(0, u, 0, i)

            def body(b, par, first, last):
                for u in range(U):
                    if u == 0 and not last:
                        if first:
                            pe.wait_ge(v_ready, 1)
                        else:
                            pe.wait_ge(upd_ready, b)
                            pe.wait_ge(v_ready, b + 1)
                        step_xnT(b + 1)
                    if u == 1 and not last:
                        step_k(b + 1, 1 - par, (q.taken, b + 2))
                    if u == 3 and not last:
                        step_v(b + 1, 1 - par, (k.taken, b + 2))
                    if u == 4 and not first:
                        step_back(b - 1, 1 - par, 0, (v_ready, b + 2) if not last else (upd_ready, b))
                    if u == 5 and not first:
                        step_back(b - 1, 1 - par, 1, (on_ready, 2 * b - 1))
                    if u == 6 and not first:
                        step_onT(b - 1, (on_ready, 2 * b))
                    if u == 7 and not first:
                        step_y(b - 1)
                    for i in range(2):
                        turn(b, u, i)
                        if u < U - 2:
                            scores(b, u + 2, par, i)
                        elif not last:
                            scores(b + 1, u + 2 - U, 1 - par, i)
                        if u == 0 and i == 0 and not last:
                            step_q(b + 1)
                    if u % 2 == 0 and u > 0:
                        values(b, u // 2 - 1, par)
                    elif u == 0 and not first:
                        values(b - 1, H // G - 1, 1 - par)

            batches(pe, body)
            values(B - 1, H // G - 1, 1)
            step_back(B - 1, 1, 0, (upd_ready, B))
            step_back(B - 1, 1, 1, (on_ready, 2 * B - 1))
            step_onT(B - 1, (on_ready, 2 * B))
            step_y(B - 1)


def channel_mix(nc, kit, d):
    with ExitStack() as ctx:
        def sb(name, shape, dt=F32):
            return ctx.enter_context(nc.sbuf_tensor("b_" + name, shape, dt))

        def sem(name):
            return nc.alloc_semaphore("b_" + name)

        def psum(name):
            return ctx.enter_context(nc.psum_tensor("b_" + name, [P, 2, S], F32))

        wr, wk, wv = (sb(n, [P, KC, D]) for n in ("wr", "wk", "wv"))
        mu, rest = sb("mu", [P, 2, KC]), sb("rest", [P, 2, KC])
        rstd = sb("rstd", [P, 2, NT])
        centred, xn = sb("centred", [P, QT, D]), sb("xn", [P, QT, D])
        xT = sb("xT", [P, KC, S + 1])
        part = sb("part", [P, 2, KC, S])
        mix = sb("mix", [P, 2, 2, KC, S])
        relu, kk = sb("relu", [P, KC, S]), sb("kk", [P, KC, S])
        gate = sb("gate", [P, QT, D])
        upd, xnew = sb("upd", [P, QT, D]), sb("xnew", [P, QT, D])
        stats, aggr = sb("stats", [P, QT, 6]), sb("aggr", [P, QT, 2])
        zeros = sb("zeros", [P, D])
        zeros_ready, zeroed = sem("zeros_ready"), sem("zeroed")
        ps_x, ps_r, ps_k, ps_y = (psum(n) for n in ("ps_x", "ps_r", "ps_k", "ps_y"))

        w_in, mu_in = sem("w_in"), sem("mu_in")
        setup, sd_ready = sem("setup"), sem("sd_ready")
        centred_ready, relu_ready = sem("centred_ready"), sem("relu_ready")
        xn_ready, x_ps, xT_ready, part_ready = sem("xn_ready"), sem("x_ps"), sem("xT_ready"), sem("part_ready")
        mixed = sem("mixed")
        k_ps, kk_ready, r_ps, gate_ready = sem("k_ps"), sem("kk_ready"), sem("r_ps"), sem("gate_ready")
        y_ps, upd_ready, x_ready = sem("y_ps"), sem("upd_ready"), sem("x_ready")
        block = ctx.enter_context(nc.Block())

        def batches(eng, body):
            body(0, 0, True, False)
            with eng.Fori(1, B - 2, 2) as b:
                body(b, 1, False, False)
                body(b + 1, 0, False, False)
            body(B - 1, 1, False, True)

        @block.sync
        def _(sp):
            for i, n in enumerate(("mu_r", "mu_k")):
                sp.dma_start(mu[:, i, :], d[n]).then_inc(mu_in, 16)
            for buf, w in ((wk, "wkT"), (wr, "wrT"), (wv, "wvT")):
                sp.dma_start(buf[:, :, :], d[w].rearrange("(c p) n -> p c n", p=P)).then_inc(w_in, 16)
            sp.wait_ge(zeros_ready, 1)
            sp.dma_start(kit.sorted_d.rearrange("(t p) c -> p t c", p=P),
                         zeros[:, :].unsqueeze(1).to_broadcast([P, kit.sorted_d.shape[0] // P, D])).then_inc(zeroed, 16)
            sp.wait_ge(zeroed, 16)

        @block.gpsimd
        def _(pool):
            pool.memset(zeros[:, :], 0.0).then_inc(zeros_ready, 1)
            pool.wait_ge(setup, 4)

            def normalize(b):
                if not isinstance(b, int) or b > 0:
                    pool.wait_ge(x_ps, b)
                rows = bass.ds(QT * b, QT)
                pool.tensor_tensor(centred[:, :, :], kit.x[:, rows, :], kit.mv[:, rows, 0:1].to_broadcast([P, QT, D]),
                                   ALU.subtract).then_inc(centred_ready, 1)
                pool.wait_ge(centred_ready, b + 1)
                pool.tensor_tensor(xn[:, :, :], centred[:, :, :],
                                   rstd[:, 0, rows].unsqueeze(2).to_broadcast([P, QT, D]), ALU.mult).then_inc(xn_ready, 1)

            normalize(0)

            def body(b, par, first, last):
                if not last:
                    normalize(b + 1)
                pool.wait_ge(relu_ready, b + 1)
                if not first:
                    pool.wait_ge(y_ps, b)
                pool.tensor_tensor(kk[:, :, :], relu[:, :, :], relu[:, :, :], ALU.mult).then_inc(kk_ready, 1)

            batches(pool, body)

        @block.scalar
        def _(act):
            act.wait_ge(setup, 1)
            act.activation(rstd[:, 1, :], rstd[:, 0, :], ACT.Sqrt).then_inc(sd_ready, 1)
            act.wait_ge(mu_in, 32)

            def turned(b):
                act.wait_ge(x_ps, b + 1)
                if not isinstance(b, int) or b > 0:
                    act.wait_ge(mixed, 2 * b)
                act.activation(xT[:, :, 1:S + 1], ps_x[:, :, :], ACT.Copy).then_inc(xT_ready, 1)
                for i in (1, 0):
                    for c in range(KC):
                        last = act.activation(part[:, i, c, :], ps_x[:, c, :], ACT.Copy, scale=mu[:, i, c:c + 1])
                    last.then_inc(part_ready, 1)

            def gates(b):
                act.wait_ge(r_ps, b + 1)
                if not isinstance(b, int) or b > 0:
                    act.wait_ge(upd_ready, b)
                act.activation(gate[:, :, :], ps_r[:, :, :], ACT.Sigmoid).then_inc(gate_ready, 1)

            turned(0)

            def body(b, par, first, last):
                if not last:
                    turned(b + 1)
                gates(b)

            batches(act, body)

        @block.vector
        def _(dve):
            dve.tensor_scalar(rstd[:, 0, :], kit.mv[:, :, 1], EPS, None, ALU.add).then_inc(setup, 1)
            dve.memset(xT[:, :, 0:1], 0.0).then_inc(setup, 1)
            dve.wait_ge(mu_in, 32)
            dve.tensor_scalar(rest[:, :, :], mu[:, :, :], -1.0, 1.0, ALU.mult, ALU.add).then_inc(setup, 1)
            dve.wait_ge(sd_ready, 1)
            dve.reciprocal(rstd[:, 0, :], rstd[:, 1, :]).then_inc(setup, 1)
            dve.wait_ge(setup, 4)

            def mixing(b, par):
                dve.wait_ge(xT_ready, b + 1)
                for n, i in enumerate((1, 0)):
                    dve.wait_ge(part_ready, 2 * b + n + 1)
                    for c in range(KC):
                        last = dve.scalar_tensor_tensor(out=mix[:, par, i, c, :], in0=xT[:, c, 0:S],
                                                        scalar=rest[:, i, c:c + 1], in1=part[:, i, c, :],
                                                        op0=ALU.mult, op1=ALU.add)
                    last.then_inc(mixed, 1)

            def keep(b):
                dve.wait_ge(upd_ready, b + 1)
                keep_rows(dve, kit, bass.ds(QT * b, QT), upd, xnew, stats, aggr, x_ready, b)

            mixing(0, 0)

            def body(b, par, first, last):
                dve.wait_ge(k_ps, b + 1)
                if not first:
                    dve.wait_ge(kk_ready, b)
                dve.tensor_scalar(relu[:, :, :], ps_k[:, :, :], 0.0, None, ALU.max).then_inc(relu_ready, 1)
                if not first:
                    keep(b - 1)
                if not last:
                    mixing(b + 1, 1 - par)
                dve.wait_ge(y_ps, b + 1)
                dve.wait_ge(gate_ready, b + 1)
                dve.tensor_tensor(upd[:, :, :], ps_y[:, :, :], gate[:, :, :], ALU.mult).then_inc(upd_ready, 1)

            batches(dve, body)
            keep(B - 1)

        @block.tensor
        def _(pe):
            pe.wait_ge(w_in, 48)

            def turn(b):
                pe.wait_ge(xn_ready, b + 1)
                if not isinstance(b, int) or b > 0:
                    pe.wait_ge(part_ready, 2 * b)
                for c in range(KC):
                    for t in range(QT):
                        last = pe.transpose(ps_x[:, c, P * t:P * (t + 1)], xn[:, t, P * c:P * (c + 1)], kit.ident[:, :])
                last.then_inc(x_ps, 1)

            turn(0)

            def body(b, par, first, last):
                pe.wait_ge(mixed, 2 * b + 1)
                for m in range(KC):
                    for c in range(KC):
                        mm = pe.matmul(ps_k[:, m, :], wk[:, c, P * m:P * (m + 1)], mix[:, par, 1, c, :],
                                       start=c == 0, stop=c == KC - 1)
                mm.then_inc(k_ps, 1)
                if not last:
                    turn(b + 1)
                pe.wait_ge(mixed, 2 * b + 2)
                if not isinstance(b, int) or b > 0:
                    pe.wait_ge(gate_ready, b)
                for t in range(QT):
                    for c in range(KC):
                        mm = pe.matmul(ps_r[:, t, :], mix[:, par, 0, c, P * t:P * (t + 1)], wr[:, c, :],
                                       start=c == 0, stop=c == KC - 1)
                mm.then_inc(r_ps, 1)
                pe.wait_ge(kk_ready, b + 1)
                if not isinstance(b, int) or b > 0:
                    pe.wait_ge(upd_ready, b)
                for t in range(QT):
                    for c in range(KC):
                        mm = pe.matmul(ps_y[:, t, :], kk[:, c, P * t:P * (t + 1)], wv[:, c, :],
                                       start=c == 0, stop=c == KC - 1)
                mm.then_inc(y_ps, 1)

            batches(pe, body)


def attend_heads(nc, kit, d):
    U = QT * QT
    HB = H // G
    HALF = H // 2
    HV = 12
    KEEP_AWAKE = 4
    with ExitStack() as ctx:
        def sb(name, shape, dt=F32):
            return ctx.enter_context(nc.sbuf_tensor("c_" + name, shape, dt))

        def sem(name):
            return nc.alloc_semaphore("c_" + name)

        wq, wk, wv = (sb(n, [P, KC, D]) for n in ("wq", "wk", "wv"))
        wo = sb("wo", [P, H // G, D])
        bq, bk = sb("bq", [P, KC]), sb("bk", [P, KC])
        bv, bo = sb("bv", [P, D]), sb("bo", [P, D])
        one_row = sb("one_row", [1, P])
        minus_i = sb("minus_i", [P, P], BF16)
        rstd = sb("rstd", [P, 2, NT])
        shift_mean = sb("shift_mean", [P, 2, NT])
        ctxT = sb("ctxT", [P, 2, KC, S])
        xn = sb("xn", [P, QT, D])
        xnT = sb("xnT", [P, KC, S])
        q, k = Split(nc, ctx, "c_q", kit.q_parts_d, Q_PART), Split(nc, ctx, "c_k", kit.k_parts_d, K_PART)
        va = sb("va", [P, 2, QT, H, 2 * DK])
        mx = sb("mx", [P, 2, P])
        mxb = sb("mxb", [P, P], BF16)
        pr = sb("pr", [P, U, H, P])
        tree = sb("tree", [P, HALF, P])
        den, rden = sb("den", [P, 2, P]), sb("rden", [P, 2, P])
        oT = sb("oT", [P, H // G, P])
        xnew = sb("xnew", [P, 1, D])
        stats, aggr = sb("stats", [P, 1, 6]), sb("aggr", [P, 1, 2])

        ps_a = ctx.enter_context(nc.psum_tensor("c_ps_a", [P, 2, S], F32))
        ps_b = ctx.enter_context(nc.psum_tensor("c_ps_b", [P, 2, S], F32))
        ps_o = ctx.enter_context(nc.psum_tensor("c_ps_o", [P, H // G, P], F32))
        ps_s = ctx.enter_context(nc.psum_tensor("c_ps_s", [P, H, P], F32))

        ps_k = ctx.enter_context(nc.psum_tensor("c_ps_k", [P, 2, S], F32))
        w_in, misc_in, x_saved = sem("w_in"), sem("misc_in"), sem("x_saved")
        ctx_in = [sem("ctx_in0"), sem("ctx_in1")]
        setup, sd_ready, zeros_ready = sem("setup"), sem("sd_ready"), sem("zeros_ready")
        xn_ready, xnT_ps, xnT_ready = sem("xn_ready"), sem("xnT_ps"), sem("xnT_ready")
        k_ps, q_ps, v_ps, v_ready = sem("k_ps"), sem("q_ps"), sem("v_ps"), sem("v_ready")
        s_ps, halves_ready, max_ready, shifted = sem("s_ps"), sem("halves_ready"), sem("max_ready"), sem("shifted")
        e_ready, tree_ready, den_ready, rden_ready = sem("e_ready"), sem("tree_ready"), sem("den_ready"), sem("rden_ready")
        pr_dve, pr_pool, pv_done = sem("pr_dve"), sem("pr_pool"), sem("pv_done")
        oT_ready, y_ps, x_ready = sem("oT_ready"), sem("y_ps"), sem("x_ready")
        block = ctx.enter_context(nc.Block())

        def batches(eng, body):
            body(0, 0, True, False)
            with eng.Fori(1, B - 2, 2) as b:
                body(b, 1, False, False)
                body(b + 1, 0, False, False)
            body(B - 1, 1, False, True)

        @block.sync
        def _(sp):
            for buf, w in ((wk, "wkT"), (wq, "wqT"), (wv, "wvT"), (wo, "woT")):
                sp.dma_start(buf[:, :, :], d[w].rearrange("(c p) n -> p c n", p=P)).then_inc(w_in, 16)

            def load(b, par):
                sp.dma_start(ctxT[:, par, :, :], d["ctxT"][:, bass.ds(b * S, S)].rearrange("(c p) n -> p c n", p=P))\
                    .then_inc(ctx_in[par], 16)

            def save_x(b):
                sp.wait_ge(x_ready, 3 * QT * (b + 1) + 3)
                sp.dma_start(kit.x_d[bass.ds(b * S, S), :].rearrange("(t p) c -> p t c", p=P),
                             kit.x[:, bass.ds(QT * b, QT), :]).then_inc(x_saved, 16)

            load(0, 0)
            load(1, 1)
            for b in range(2):
                k.write(sp, b, b)
                q.write(sp, b, b)
                k.stack(sp, b, b)
                q.stack(sp, b, b)
            with sp.Fori(2, B - 1, 2) as b:
                for i in range(2):
                    sp.wait_ge(v_ready, b + i - 1)
                    load(b + i, i)
                    k.write(sp, b + i, i)
                    q.write(sp, b + i, i)
                    k.stack(sp, b + i, i)
                    q.stack(sp, b + i, i)
                    save_x(b + i - 2)
            save_x(B - 2)
            save_x(B - 1)
            sp.wait_ge(x_saved, 16 * B)

        @block.scalar
        def _(act):
            for buf, n in ((bq, "bq"), (bk, "bk"), (bv, "bv"), (bo, "bo")):
                act.dma_start(buf[:, :], d[n]).then_inc(misc_in, 16)
            act.wait_ge(setup, 1)
            act.activation(rstd[:, 1, :], rstd[:, 0, :], ACT.Sqrt).then_inc(sd_ready, 1)
            act.wait_ge(misc_in, 16 * 4)
            act.wait_ge(x_ready, 3)
            act.wait_ge(zeros_ready, 2)

            def step_xnT(b):
                act.wait_ge(xnT_ps, b + 1)
                act.activation(xnT[:, :, :], ps_b[:, :, :], ACT.Copy).then_inc(xnT_ready, 1)

            def normalize(b):
                for t in range(QT):
                    tile = bass.ds(QT * b + t, 1)
                    last = act.activation(xn[:, t, :], kit.x[:, tile, :].rearrange("p t c -> p (t c)"), ACT.Identity,
                                          bias=shift_mean[:, 1, tile], scale=rstd[:, 0, tile])
                last.then_inc(xn_ready, 1)

            def numerators(b, i):
                n = b * U + i
                if not isinstance(b, int) or b > 0:
                    act.wait_ge(pv_done, n - U + 1)
                act.wait_ge(shifted, n + 1)
                for half in range(2):
                    hs = slice(HALF * half, HALF * (half + 1))
                    act.activation(pr[:, i, hs, :], ps_s[:, hs, :], ACT.Exp, scale=SCALE).then_inc(e_ready, 1)

            def step_v(b, par):
                act.wait_ge(v_ps, b + 1)
                act.activation(va[:, par, :, :, 0:DK], ps_b[:, :, :].rearrange("p t (h k) -> p t h k", h=H), ACT.Copy)\
                    .then_inc(v_ready, 1)

            def take_o(j):
                act.wait_ge(pv_done, 2 * j + 2)
                if not isinstance(j, int) or j > 0:
                    act.wait_ge(y_ps, j)
                act.activation(oT[:, :, :], ps_o[:, :, :], ACT.Copy).then_inc(oT_ready, 1)

            normalize(0)
            step_xnT(0)
            for j in range(3):
                k.take_part(act, 0, 0, j, k_ps, ps_k, bk)
                q.take_part(act, 0, 0, j, q_ps, ps_b, bq)
            step_v(0, 0)

            def body(b, par, first, last):
                for i in range(U):
                    if i == 0 and not last:
                        normalize(b + 1)
                    numerators(b, i)
                    if i == 0 and not last:
                        step_xnT(b + 1)
                        k.take_part(act, b + 1, 1 - par, 0, k_ps, ps_k, bk)
                        q.take_part(act, b + 1, 1 - par, 0, q_ps, ps_b, bq)
                    if i == 1 and not last:
                        for j in (1, 2):
                            k.take_part(act, b + 1, 1 - par, j, k_ps, ps_k, bk)
                            q.take_part(act, b + 1, 1 - par, j, q_ps, ps_b, bq)
                    if i == 0 and not first:
                        take_o(2 * b - 2)
                    if i == 2 and not first:
                        take_o(2 * b - 1)
                    if i == 2 and not last:
                        step_v(b + 1, 1 - par)

            batches(act, body)
            take_o(2 * B - 2)
            take_o(2 * B - 1)

        @block.gpsimd
        def _(pool):
            pool.memset(one_row[:, :], 1.0).then_inc(zeros_ready, 1)
            pool.memset(va[:, :, :, :, :], 0.0).then_inc(zeros_ready, 1)

            def add_heads(n, i, early):
                if not isinstance(n, int) or n > 0:
                    pool.wait_ge(den_ready, n)
                pool.wait_ge(e_ready, 2 * n + 2)
                pool.tensor_tensor(tree[:, :, :], pr[:, i, 0:8, :], pr[:, i, 8:16, :], ALU.add).then_inc(tree_ready, 1)
                pool.wait_ge(tree_ready, 3 * n + 1)
                pool.tensor_tensor(tree[:, 0:4, :], tree[:, 0:4, :], tree[:, 4:8, :], ALU.add).then_inc(tree_ready, 1)
                pool.wait_ge(tree_ready, 3 * n + 2)
                pool.tensor_tensor(tree[:, 0:2, :], tree[:, 0:2, :], tree[:, 2:4, :], ALU.add).then_inc(tree_ready, 1)
                if not early:
                    pool.wait_ge(rden_ready, n - 1)
                pool.wait_ge(tree_ready, 3 * n + 3)
                pool.tensor_tensor(den[:, i % 2, :], tree[:, 0, :], tree[:, 1, :], ALU.add).then_inc(den_ready, 1)

            def probabilities(n, i):
                pool.wait_ge(rden_ready, n + 1)
                pool.tensor_tensor(pr[:, i, HV:H, :], pr[:, i, HV:H, :],
                                   rden[:, i % 2, :].unsqueeze(1).to_broadcast([P, H - HV, P]), ALU.mult).then_inc(pr_pool, 1)

            def body(b, par, first, last):
                for i in range(U):
                    n = b * U + i
                    add_heads(n, i, first and i < 2)
                    if not first or i > 0:
                        probabilities(n - 1, (i - 1) % U)

            batches(pool, body)
            probabilities(B * U - 1, U - 1)

        @block.vector
        def _(dve):
            dve.tensor_scalar(rstd[:, 0, :], kit.mv[:, :, 1], EPS, None, ALU.add).then_inc(setup, 1)
            dve.tensor_scalar(minus_i[:, :], kit.ident[:, :], -1.0, None, ALU.mult).then_inc(setup, 1)
            dve.wait_ge(misc_in, 16 * 4)
            dve.wait_ge(sd_ready, 1)
            dve.reciprocal(rstd[:, 0, :], rstd[:, 1, :]).then_inc(setup, 1)
            dve.tensor_scalar(shift_mean[:, 0, :], kit.mv[:, :, 0], -1.0, None, ALU.mult).then_inc(setup, 1)
            dve.wait_ge(setup, 4)
            dve.tensor_tensor(shift_mean[:, 1, :], shift_mean[:, 0, :], rstd[:, 0, :], ALU.mult)\
                .then_inc(x_ready, 3)

            def maxima(b, i):
                n = b * U + i
                for half in range(2):
                    hs = slice(HALF * half, HALF * (half + 1))
                    dve.wait_ge(s_ps, 2 * n + half + 1)
                    dve.tensor_reduce(mx[:, half, :], ps_s[:, hs, :].rearrange("p h q -> p q h"), AX.X, ALU.max)\
                        .then_inc(halves_ready, 1)
                dve.wait_ge(halves_ready, 2 * n + 2)
                dve.tensor_tensor(mxb[:, :], mx[:, 0, :], mx[:, 1, :], ALU.max).then_inc(max_ready, 1)

            def denominators(n, i, early):
                dve.wait_ge(den_ready, n + 1)
                if not early:
                    dve.wait_ge(pr_pool, n - 1)
                    dve.wait_ge(pr_dve, n - 1)
                dve.reciprocal(rden[:, i % 2, :], den[:, i % 2, :]).then_inc(rden_ready, 1)

            def probabilities(n, i):
                dve.wait_ge(rden_ready, n + 1)
                dve.tensor_tensor(pr[:, i, 0:HV, :], pr[:, i, 0:HV, :],
                                  rden[:, i % 2, :].unsqueeze(1).to_broadcast([P, HV, P]), ALU.mult).then_inc(pr_dve, 1)

            def step_y(j):
                dve.wait_ge(y_ps, j + 1)
                keep_rows(dve, kit, bass.ds(j, 1), ps_a[:, 0:1, :], xnew, stats, aggr, x_ready, j + 1)

            def body(b, par, first, last):
                for i in range(U):
                    maxima(b, i)
                    if not first or i > 1:
                        probabilities(b * U + i - 2, (i - 2) % U)
                    if not first or i > 0:
                        denominators(b * U + i - 1, (i - 1) % U, first and i < 3)
                    if i >= 2 and not first:
                        step_y(2 * b - 4 + i)

            batches(dve, body)
            probabilities(B * U - 2, U - 2)
            denominators(B * U - 1, U - 1, False)
            probabilities(B * U - 1, U - 1)
            for j in (2 * B - 2, 2 * B - 1):
                step_y(j)

        @block.tensor
        def _(pe):
            pe.wait_ge(setup, 2)
            pe.wait_ge(zeros_ready, 2)
            pe.wait_ge(misc_in, 16 * 4)
            pe.wait_ge(w_in, 64)

            def project(ps, w, xT):
                for m in range(KC):
                    for c in range(KC):
                        last = pe.matmul(ps[:, m, :], w[:, c, P * m:P * (m + 1)], xT[:, c, :],
                                         start=m == 0 and c == 0, stop=c == KC - 1, skip_group_check=True)
                return last

            def step_xnT(b):
                pe.wait_ge(xn_ready, b + 1)
                for c in range(KC):
                    for t in range(QT):
                        last = pe.transpose(ps_b[:, c, P * t:P * (t + 1)], xn[:, t, P * c:P * (c + 1)], kit.ident[:, :])
                last.then_inc(xnT_ps, 1)

            def step_k(b, par):
                pe.wait_ge(ctx_in[par], (b - par) * 8 + 16)
                project(ps_k, wk, ctxT[:, par, :, :]).then_inc(k_ps, 1)

            def step_q(b):
                pe.wait_ge(xnT_ready, b + 1)
                project(ps_b, wq, xnT).then_inc(q_ps, 1)

            def step_v(b, par):
                for t in range(QT):
                    pe.matmul(ps_b[:, t, :], one_row[:, :], bv[0:1, :], start=True, stop=False)
                    for c in range(KC):
                        last = pe.matmul(ps_b[:, t, :], ctxT[:, par, c, P * t:P * (t + 1)], wv[:, c, :],
                                         start=False, stop=c == KC - 1)
                last.then_inc(v_ps, 1)

            def step_y(j):
                pe.wait_ge(oT_ready, j + 1)
                pe.matmul(ps_a[:, 0, :], one_row[:, :], bo[0:1, :], start=True, stop=False)
                for g in range(H // G):
                    last = pe.matmul(ps_a[:, 0, :], oT[:, g, :], wo[:, g, :], start=False, stop=g == H // G - 1)
                last.then_inc(y_ps, 1)

            def scores(b, i, par):
                t, kt = i // QT, i % QT
                n = b * U + i
                if i == 0:
                    k.wait_stacked(pe, b, par)
                    q.wait_stacked(pe, b, par)
                for h in range(H):
                    if h % HALF == 0 and (not isinstance(b, int) or n > 0):
                        pe.wait_ge(e_ready, 2 * n - 1 + h // HALF)
                    last = pe.matmul(ps_s[:, h, :], k.stacked[:, par, h, P * kt:P * (kt + 1)],
                                     q.stacked[:, par, h, P * t:P * (t + 1)],
                                     start=h % G == 0, stop=False, skip_group_check=True)
                    if h % HALF == HALF - 1:
                        last.then_inc(s_ps, 1)

            def shift(b, i):
                n = b * U + i
                pe.wait_ge(max_ready, n + 1)
                for g in range(HB):
                    last = pe.matmul(ps_s[:, G * g:G * (g + 1), :], minus_i[:, :],
                                     mxb[:, :].unsqueeze(1).to_broadcast([P, G, P]),
                                     start=False, stop=True, skip_group_check=True)
                last.then_inc(shifted, 1)

            def values(b, i, par):
                k = i % QT
                n = b * U + i
                if i == 0:
                    pe.wait_ge(v_ready, b + 1)
                if k == 0 and (not isinstance(b, int) or n > 0):
                    pe.wait_ge(oT_ready, 2 * b + i // QT)
                pe.wait_ge(pr_dve, n + 1)
                pe.wait_ge(pr_pool, n + 1)
                for h in range(H):
                    j = 2 * DK * (h % G)
                    last = pe.matmul(ps_o[j:j + 2 * DK, h // G, :], va[:, par, k, h, :], pr[:, i, h, :],
                                     start=k == 0 and h < G, stop=k == QT - 1, skip_group_check=True)
                last.then_inc(pv_done, 1)

            step_k(0, 0)
            step_xnT(0)
            step_q(0)
            for j in range(2):
                k.subtract(pe, 0, 0, j, ps_k, minus_i)
                q.subtract(pe, 0, 0, j, ps_b, minus_i)
            pe.wait_ge(q.parted, 1)
            step_v(0, 0)
            scores(0, 0, 0)

            def body(b, par, first, last):
                for i in range(U):
                    shift(b, i)
                    if i == 3 and not first:
                        pe.wait_ge(x_ready, 6 * b - 2)
                        step_y(2 * b - 1)
                    if i < 3 and not first:
                        values(b - 1, i + 1, 1 - par)
                    if i == 1 and not last:
                        k.subtract(pe, b + 1, 1 - par, 0, ps_k, minus_i)
                        q.subtract(pe, b + 1, 1 - par, 0, ps_b, minus_i)
                    if i == 0 and not last:
                        pe.wait_ge(v_ready, b + 1)
                        step_xnT(b + 1)
                    if i < U - 1:
                        scores(b, i + 1, par)
                    elif not last:
                        scores(b + 1, 0, 1 - par)
                    if i == 0 and not last:
                        pe.wait_ge(k.parted, b + 1)
                        step_k(b + 1, 1 - par)
                        step_q(b + 1)
                    if i == 1 and not first:
                        pe.wait_ge(x_ready, 6 * b - 5)
                        step_y(2 * b - 2)
                    if i == 1 and not last:
                        k.subtract(pe, b + 1, 1 - par, 1, ps_k, minus_i)
                        q.subtract(pe, b + 1, 1 - par, 1, ps_b, minus_i)
                    if i == 2 and not last:
                        pe.wait_ge(q.parted, b + 2)
                        step_v(b + 1, 1 - par)
                    if i == 3:
                        values(b, 0, par)
                    if i == 3 and not last:
                        pe.wait_ge(k.parted, b + 2)
                        for _ in range(KEEP_AWAKE):
                            pe.matmul(ps_k[:, :, :], minus_i[:, :], minus_i[:, :].unsqueeze(1).to_broadcast([P, G, P]),
                                      start=True, stop=True)

            batches(pe, body)
            values(B - 1, 1, 1)
            values(B - 1, 2, 1)
            values(B - 1, 3, 1)
            pe.wait_ge(x_ready, 6 * B - 5)
            step_y(2 * B - 2)
            pe.wait_ge(x_ready, 6 * B - 2)
            step_y(2 * B - 1)


def route(nc, kit, d):
    PAIR = 2
    NJ = NT // PAIR
    with ExitStack() as ctx:
        def sb(name, shape, dt=F32):
            return ctx.enter_context(nc.sbuf_tensor("r_" + name, shape, dt))

        def sem(name):
            return ctx.enter_context(nc.semaphore("r_" + name))

        wr, br = sb("wr", [P, KC, E]), sb("br", [P, E])
        order = sb("order", [P, E])
        tile_no = sb("tile_no", [P, SLOT_TILES])
        before = sb("before", [P, P])
        before_b, ones_b = sb("before_b", [P, P], BF16), sb("ones_b", [P, P], BF16)
        ones = sb("ones", [P, NT])
        rstd = sb("rstd", [P, 2, NT])
        xn = sb("xn", [P, 2, PAIR, D])
        xnT = sb("xnT", [P, 2, KC, PAIR * P])
        lg = sb("lg", [P, NT, E])
        low, hit = sb("low", [P, NT, E]), sb("hit", [P, NT, E])
        top = sb("top", [P, 2, NT])
        first_at = sb("first_at", [P, NT])
        one_hot = sb("one_hot", [P, 2, NT, E])
        taken = sb("taken", [P, NT, E], BF16)
        ex = sb("ex", [P, NT])
        rank, total, upto = sb("rank", [P, NT, E]), sb("total", [P, NT, E]), sb("upto", [P, NT, E])
        tiles_i, tiles_f = sb("tiles_i", [P, E], I32), sb("tiles_f", [P, E])
        upto_e, start_e = sb("upto_e", [P, E]), sb("start_e", [P, E])
        slot_f = sb("slot_f", [P, NT])
        past = sb("past", [P, SLOT_TILES, E])
        past_n = sb("past_n", [P, SLOT_TILES])
        ps_x = ctx.enter_context(nc.psum_tensor("r_ps_x", [P, 2, KC, PAIR * P], F32))
        ps_l = ctx.enter_context(nc.psum_tensor("r_ps_l", [P, 2, 512 // E, E], F32))
        ps_r = ctx.enter_context(nc.psum_tensor("r_ps_r", [P, NT * E], F32))
        ps_n = ctx.enter_context(nc.psum_tensor("r_ps_n", [P, NT * E], F32))

        misc_in = sem("misc_in")
        setup, sd_ready = sem("setup"), sem("sd_ready")
        xn_ready, xn_kept, x_ps, xnT_ready = sem("xn_ready"), sem("xn_kept"), sem("x_ps"), sem("xnT_ready")
        l_ps, lg_ready = sem("l_ps"), sem("lg_ready")
        pick = sem("pick")
        ex_ready, taken_ready, counts_ps, place = sem("ex_ready"), sem("taken_ready"), sem("counts_ps"), sem("place")
        moved = sem("moved")
        block = ctx.enter_context(nc.Block())

        @block.sync
        def _(sp):
            sp.wait_ge(misc_in, 16 * 5)
            for e in range(E):
                sp.dma_start(kit.w1[:, e, :, :], d["w1"][e].rearrange("(c p) f -> p c f", p=P)).then_inc(kit.w_in, 16)
                sp.dma_start(kit.w2[:, e, :, :], d["w2"][e].rearrange("(f p) n -> p f n", p=P)).then_inc(kit.w_in, 16)
            for buf, n in ((kit.b1, "b1"), (kit.b2, "b2")):
                sp.dma_start(buf[:, :, :], d[n]).then_inc(kit.w_in, 16)
            sp.wait_ge(kit.w_in, 16 * (2 * E + 2))

        @block.scalar
        def _(act):
            act.dma_start(wr[:, :, :], d["wr"].rearrange("(c p) e -> p c e", p=P)).then_inc(misc_in, 16)
            for buf, n in ((br, "br"), (order, "order"), (tile_no, "tile_no"), (before, "before")):
                act.dma_start(buf[:, :], d[n]).then_inc(misc_in, 16)
            act.wait_ge(setup, 1)
            act.activation(rstd[:, 1, :], rstd[:, 0, :], ACT.Sqrt).then_inc(sd_ready, 1)
            act.wait_ge(misc_in, 16 * 5)

            def take(j, par, early):
                act.wait_ge(x_ps, j + 1)
                if not early:
                    act.wait_ge(l_ps, j - 1)
                act.activation(xnT[:, par, :, :], ps_x[:, par, :, :], ACT.Copy).then_inc(xnT_ready, 1)

            take(0, 0, True)
            take(1, 1, True)
            with act.Fori(2, NJ - 1, 2) as j:
                take(j, 0, False)
                take(j + 1, 1, False)
            act.wait_ge(pick, 8)
            act.activation(ex[:, :], first_at[:, :], ACT.Exp).then_inc(ex_ready, 1)

        @block.vector
        def _(dve):
            dve.tensor_scalar(rstd[:, 0, :], kit.mv[:, :, 1], EPS, None, ALU.add).then_inc(setup, 1)
            dve.wait_ge(misc_in, 16 * 5)
            dve.tensor_copy(before_b[:, :], before[:, :]).then_inc(setup, 1)
            dve.memset(ones_b[:, :], 1.0).then_inc(setup, 1)
            dve.memset(ones[:, :], 1.0).then_inc(setup, 1)
            dve.wait_ge(sd_ready, 1)
            dve.reciprocal(rstd[:, 0, :], rstd[:, 1, :]).then_inc(setup, 1)
            dve.wait_ge(setup, 5)

            def rows(j, par):
                for t in range(PAIR):
                    last = dve.tensor_scalar(xn[:, par, t, :], kit.x[:, PAIR * j + t, :], kit.mv[:, PAIR * j + t, 0:1],
                                             rstd[:, 0, bass.ds(PAIR * j + t, 1)], ALU.subtract, ALU.mult)
                last.then_inc(xn_ready, 1)
                dve.wait_ge(xn_ready, j + 1)
                dve.tensor_scalar(kit.x[:, bass.ds(PAIR * j, PAIR), :], xn[:, par, :, :], 1.0, None, ALU.mult).then_inc(xn_kept, 1)

            rows(0, 0)

            def logits(j, par):
                dve.wait_ge(l_ps, j + 1)
                dve.tensor_tensor(lg[:, bass.ds(PAIR * j, PAIR), :], ps_l[:, par, 0:PAIR, :],
                                  br[:, :].unsqueeze(1).to_broadcast([P, PAIR, E]), ALU.add).then_inc(lg_ready, 1)

            rows(1, 1)
            with dve.Fori(2, NJ - 1, 2) as j:
                for i in range(2):
                    dve.wait_ge(x_ps, j + i - 1)
                    rows(j + i, i)
                    logits(j + i - 2, i)
            logits(NJ - 2, 0)
            logits(NJ - 1, 1)
            dve.wait_ge(lg_ready, NJ)
            dve.wait_ge(xn_kept, NJ)

            every = [P, NT, E]
            order_b = order[:, :].unsqueeze(1).to_broadcast(every)

            def spread(v):
                return v.unsqueeze(2).to_broadcast(every)

            for i in range(2):
                of = low if i else lg
                dve.tensor_reduce(top[:, i, :], of[:, :, :], AX.X, ALU.max).then_inc(pick, 1)
                dve.wait_ge(pick, 4 * i + 1)
                dve.tensor_tensor(hit[:, :, :], of[:, :, :], spread(top[:, i, :]), ALU.is_equal).then_inc(pick, 1)
                dve.wait_ge(pick, 4 * i + 2)
                dve.tensor_tensor(hit[:, :, :], hit[:, :, :], order_b, ALU.mult).then_inc(pick, 1)
                dve.wait_ge(pick, 4 * i + 3)
                dve.tensor_reduce(first_at[:, :], hit[:, :, :], AX.X, ALU.min).then_inc(place, 1)
                dve.wait_ge(place, 3 * i + 1)
                dve.tensor_tensor(one_hot[:, i, :, :], order_b, spread(first_at[:, :]), ALU.is_equal).then_inc(place, 1)
                dve.wait_ge(place, 3 * i + 2)
                if i == 0:
                    dve.tensor_scalar(low[:, :, :], one_hot[:, 0, :, :], -3e38, None, ALU.mult).then_inc(place, 1)
                    dve.wait_ge(place, 3)
                    dve.tensor_tensor(low[:, :, :], low[:, :, :], lg[:, :, :], ALU.add).then_inc(pick, 1)
                    dve.wait_ge(pick, 4)
                else:
                    dve.tensor_tensor(taken[:, :, :], one_hot[:, 0, :, :], one_hot[:, 1, :, :], ALU.add).then_inc(taken_ready, 1)
                    dve.tensor_tensor(first_at[:, :], top[:, 1, :], top[:, 0, :], ALU.subtract).then_inc(pick, 1)
            dve.wait_ge(ex_ready, 1)
            dve.tensor_scalar(top[:, 0, :], ex[:, :], 1.0, None, ALU.add).then_inc(pick, 1)
            dve.wait_ge(pick, 9)
            dve.reciprocal(kit.gate[:, 0, :], top[:, 0, :]).then_inc(pick, 1)
            dve.wait_ge(pick, 10)
            dve.tensor_tensor(kit.gate[:, 1, :], kit.gate[:, 0, :], ex[:, :], ALU.mult).then_inc(pick, 1)
            dve.wait_ge(counts_ps, 1)
            dve.tensor_copy(rank[:, :, :], ps_r[:, :].rearrange("p (t e) -> p t e", e=E)).then_inc(place, 1)
            dve.tensor_copy(total[:, :, :], ps_n[:, :].rearrange("p (t e) -> p t e", e=E)).then_inc(place, 1)
            dve.wait_ge(place, 7)
            for e in range(E):
                last = dve.tensor_tensor_scan(upto[:, :, e], ones[:, :], total[:, :, e], 0.0, ALU.mult, ALU.add)
            last.then_inc(place, 1)
            dve.wait_ge(place, 8)
            dve.tensor_tensor(rank[:, :, :], rank[:, :, :], upto[:, :, :], ALU.add).then_inc(place, 1)
            dve.tensor_scalar(tiles_i[:, :], upto[:, NT - 1, :], float(R - 1), None, ALU.add).then_inc(place, 1)
            dve.wait_ge(place, 10)
            dve.tensor_tensor(rank[:, :, :], rank[:, :, :], total[:, :, :], ALU.subtract).then_inc(place, 1)
            dve.tensor_scalar(tiles_i[:, :], tiles_i[:, :], R.bit_length() - 1, None, ALU.logical_shift_right).then_inc(place, 1)
            dve.wait_ge(place, 12)
            dve.tensor_copy(tiles_f[:, :], tiles_i[:, :]).then_inc(place, 1)
            dve.wait_ge(place, 13)
            dve.tensor_tensor_scan(upto_e[:, :], ones[:, 0:E], tiles_f[:, :], 0.0, ALU.mult, ALU.add).then_inc(place, 1)
            dve.wait_ge(place, 14)
            dve.tensor_tensor(start_e[:, :], upto_e[:, :], tiles_f[:, :], ALU.subtract).then_inc(place, 1)
            dve.wait_ge(place, 15)
            dve.tensor_scalar(start_e[:, :], start_e[:, :], float(R), None, ALU.mult).then_inc(place, 1)
            dve.wait_ge(place, 16)
            dve.tensor_tensor(rank[:, :, :], rank[:, :, :], start_e[:, :].unsqueeze(1).to_broadcast(every), ALU.add)\
                .then_inc(place, 1)
            dve.wait_ge(place, 17)
            for i in range(2):
                dve.tensor_tensor(hit[:, :, :], one_hot[:, i, :, :], rank[:, :, :], ALU.mult).then_inc(place, 1)
                dve.wait_ge(place, 18 + 3 * i)
                dve.tensor_reduce(slot_f[:, :], hit[:, :, :], AX.X, ALU.add).then_inc(place, 1)
                dve.wait_ge(place, 19 + 3 * i)
                dve.tensor_copy(kit.slot[:, i, :], slot_f[:, :]).then_inc(place, 1)
                dve.wait_ge(place, 20 + 3 * i)
            whole = [P, SLOT_TILES, E]
            dve.tensor_tensor(past[:, :, :], tile_no[:, :].unsqueeze(2).to_broadcast(whole),
                              upto_e[:, :].unsqueeze(1).to_broadcast(whole), ALU.is_ge).then_inc(place, 1)
            dve.wait_ge(place, 24)
            dve.tensor_reduce(past_n[:, :], past[:, :, :], AX.X, ALU.add).then_inc(place, 1)
            dve.wait_ge(place, 25)
            dve.tensor_scalar(kit.expert[:, :], past_n[:, :], float(E - 1), None, ALU.min).then_inc(place, 1)
            dve.wait_ge(place, 26)

        @block.gpsimd
        def _(pool):
            pool.wait_ge(place, 23)
            for i in range(2):
                for t in range(NT):
                    pool.indirect_dma_start(out=kit.sorted_d, out_offset=bass.IndirectOffsetOnAxis(ap=kit.slot[:, i, t:t + 1], axis=0),
                                            in_=kit.x[:, t, :], in_offset=None).then_inc(moved, 16)
            pool.wait_ge(moved, 16 * 2 * NT)

        @block.tensor
        def _(pe):
            pe.wait_ge(misc_in, 16 * 5)

            def turn(j, par, early):
                pe.wait_ge(xn_ready, j + 1)
                if not early:
                    pe.wait_ge(xnT_ready, j - 1)
                for c in range(KC):
                    for t in range(PAIR):
                        last = pe.transpose(ps_x[:, par, c, P * t:P * (t + 1)], xn[:, par, t, P * c:P * (c + 1)],
                                            kit.ident[:, :])
                last.then_inc(x_ps, 1)

            def logits(j, par, early):
                pe.wait_ge(xnT_ready, j + 1)
                if not early:
                    pe.wait_ge(lg_ready, j - 1)
                for t in range(PAIR):
                    for c in range(KC):
                        last = pe.matmul(ps_l[:, par, t, :], xnT[:, par, c, P * t:P * (t + 1)], wr[:, c, :],
                                         start=c == 0, stop=c == KC - 1)
                last.then_inc(l_ps, 1)

            turn(0, 0, True)
            turn(1, 1, True)
            logits(0, 0, True)
            turn(2, 0, False)
            logits(1, 1, True)
            with pe.Fori(3, NJ - 2, 2) as j:
                turn(j, 1, False)
                logits(j - 1, 0, False)
                turn(j + 1, 0, False)
                logits(j, 1, False)
            turn(NJ - 1, 1, False)
            logits(NJ - 2, 0, False)
            logits(NJ - 1, 1, False)
            pe.wait_ge(taken_ready, 1)
            pe.wait_ge(setup, 3)
            flat = taken[:, :, :].rearrange("p t e -> p (t e)")
            pe.matmul(ps_r[:, :], before_b[:, :], flat, start=True, stop=True)
            pe.matmul(ps_n[:, :], ones_b[:, :], flat, start=True, stop=True).then_inc(counts_ps, 1)


def experts(nc, kit, d):
    T = SLOT_TILES
    PAIRS_F = FC // 2
    TERMS = ((0, 0), (1, 0), (0, 1))
    with ExitStack() as ctx:
        def sb(name, shape, dt=F32):
            return ctx.enter_context(nc.sbuf_tensor("e_" + name, shape, dt))

        def sem(name):
            return ctx.enter_context(nc.semaphore("e_" + name))

        w1 = [sb(f"w1_{n}", [P, KC, FF], F32R) for n in ("high", "low")]
        w2 = [sb(f"w2_{n}", [P, FC, D], F32R) for n in ("high", "low")]
        rows = sb("rows", [P, RT, D])
        rowsT = [sb(f"rowsT{i}", [P, KC, R], F32R) for i in range(2)]
        b1 = sb("b1_now", [P, FC])
        h = sb("h", [P, 2, 2, R])
        hT = [sb(f"hT{i}", [P, 2, 2, R], F32R) for i in range(2)]
        y = sb("y", [P, RT, D])
        ps_x = ctx.enter_context(nc.psum_tensor("e_ps_x", [P, KC, R], F32))
        ps_h = ctx.enter_context(nc.psum_tensor("e_ps_h", [P, FC, R], F32))
        ps_y = ctx.enter_context(nc.psum_tensor("e_ps_y", [P, RT, D], F32))

        rows_in, y_out = sem("rows_in"), sem("y_out")
        x_ps, xT_high, xT_ready = sem("x_ps"), sem("xT_high"), sem("xT_ready")
        w1_high, w1_ready, w2_high, w2_ready = sem("w1_high"), sem("w1_ready"), sem("w2_high"), sem("w2_ready")
        b1_ready = sem("b1_ready")
        h_ps, h_whole, h_high, h_ready = sem("h_ps"), sem("h_whole"), sem("h_high"), sem("h_ready")
        y_ps, y_ready = sem("y_ps"), sem("y_ready")
        block = ctx.enter_context(nc.Block())

        def expert_of(eng, j):
            return eng.value_load(kit.expert[0:1, bass.ds(j, 1)], min_val=0, max_val=E - 1)

        def tiles(eng, body):
            body(0, True, False)
            with eng.Fori(1, T - 1) as j:
                body(j, False, False)
            body(T - 1, False, True)

        def w1_pair(w, p):
            return w[:, :, 2 * P * p:2 * P * (p + 1)]

        def w2_pair(w, p):
            return w[:, 2 * p:2 * (p + 1), :]

        @block.sync
        def _(sp):
            def load(j):
                sp.dma_start(rows[:, :, :], kit.sorted_d[bass.ds(j * R, R), :].rearrange("(t p) c -> p t c", p=P))\
                    .then_inc(rows_in, 16)

            load(0)

            def body(j, first, last):
                if not last:
                    sp.wait_ge(x_ps, j + 1)
                    load(j + 1)
                sp.wait_ge(y_ready, j + 1)
                sp.dma_start(kit.outs_d[bass.ds(j * R, R), :].rearrange("(t p) c -> p t c", p=P), y[:, :, :])\
                    .then_inc(y_out, 16)

            tiles(sp, body)
            sp.wait_ge(y_out, 16 * T)

        @block.scalar
        def _(act):
            def rows_high(j):
                act.wait_ge(x_ps, j + 1)
                act.activation(rowsT[0][:, :, :], ps_x[:, :, :], ACT.Copy).then_inc(xT_high, 1)

            def whole(j, p, first):
                n = PAIRS_F * j + p
                act.wait_ge(h_ps, n + 1)
                if p == 0:
                    act.wait_ge(b1_ready, j + 1)
                if not first or p >= 2:
                    act.wait_ge(h_ready, n - 1)
                for i in range(2):
                    f = 2 * p + i
                    last = act.activation(h[:, p % 2, i, :], ps_h[:, f, :], ACT.Relu, bias=b1[:, f:f + 1])
                last.then_inc(h_whole, 1)

            def high(j, p, first):
                n = PAIRS_F * j + p
                act.wait_ge(h_whole, n + 1)
                if not first or p >= 2:
                    act.wait_ge(y_ps, n - 1)
                act.activation(hT[0][:, p % 2, :, :], h[:, p % 2, :, :], ACT.Copy).then_inc(h_high, 1)

            rows_high(0)

            def body(j, first, last):
                for p in range(PAIRS_F):
                    whole(j, p, first)
                    high(j, p, first)
                if not last:
                    rows_high(j + 1)

            tiles(act, body)

        @block.gpsimd
        def _(pool):
            def weights_low(j, e, p):
                pool.wait_ge(w1_high, PAIRS_F * j + p + 1)
                pool.tensor_tensor(w1_pair(w1[1], p), kit.w1[:, e, :, 2 * P * p:2 * P * (p + 1)],
                                   w1_pair(w1[0], p).bitcast(F32), ALU.subtract).then_inc(w1_ready, 1)

            with pool.Fori(0, T) as j:
                e = expert_of(pool, j)
                for p in range(PAIRS_F):
                    weights_low(j, e, p)

        @block.vector
        def _(dve):
            def first_high(j, e, p, fresh):
                if not fresh:
                    dve.wait_ge(h_ps, PAIRS_F * (j - 1) + p + 1)
                dve.tensor_scalar(w1_pair(w1[0], p), kit.w1[:, e, :, 2 * P * p:2 * P * (p + 1)], 1.0, None, ALU.mult)\
                    .then_inc(w1_high, 1)

            def second_high(j, e, p, fresh):
                if not fresh:
                    dve.wait_ge(y_ps, PAIRS_F * (j - 1) + p + 1)
                dve.tensor_scalar(w2_pair(w2[0], p), kit.w2[:, e, 2 * p:2 * (p + 1), :], 1.0, None, ALU.mult)\
                    .then_inc(w2_high, 1)

            def second_low(j, e, p):
                dve.wait_ge(w2_high, PAIRS_F * j + p + 1)
                dve.tensor_tensor(w2_pair(w2[1], p), kit.w2[:, e, 2 * p:2 * (p + 1), :],
                                  w2_pair(w2[0], p).bitcast(F32), ALU.subtract).then_inc(w2_ready, 1)

            def rows_low(j):
                dve.wait_ge(xT_high, j + 1)
                dve.tensor_tensor(rowsT[1][:, :, :], ps_x[:, :, :], rowsT[0][:, :, :].bitcast(F32), ALU.subtract)\
                    .then_inc(xT_ready, 1)

            def bias_of(j, e):
                dve.tensor_scalar(b1[:, :], kit.b1[:, e, :], 1.0, None, ALU.mult).then_inc(b1_ready, 1)

            def low(j, p):
                dve.wait_ge(h_high, PAIRS_F * j + p + 1)
                dve.tensor_tensor(hT[1][:, p % 2, :, :], h[:, p % 2, :, :], hT[0][:, p % 2, :, :].bitcast(F32),
                                  ALU.subtract).then_inc(h_ready, 1)

            def finish(j, first):
                dve.wait_ge(y_ps, PAIRS_F * (j + 1))
                if not first:
                    dve.wait_ge(y_out, 16 * j)
                e = expert_of(dve, j)
                dve.tensor_tensor(y[:, :, :], ps_y[:, :, :], kit.b2[:, bass.ds(e, 1), :].to_broadcast([P, RT, D]),
                                  ALU.add).then_inc(y_ready, 1)

            e = expert_of(dve, 0)
            for p in range(PAIRS_F):
                first_high(0, e, p, True)
            bias_of(0, e)
            rows_low(0)
            for p in range(PAIRS_F):
                second_high(0, e, p, True)
            for p in range(PAIRS_F):
                second_low(0, e, p)

            def body(j, first, last):
                low(j, 0)
                if not last:
                    e = expert_of(dve, j + 1)
                    first_high(j + 1, e, 0, False)
                    first_high(j + 1, e, 1, False)
                low(j, 1)
                if not last:
                    first_high(j + 1, e, 2, False)
                    second_high(j + 1, e, 0, False)
                low(j, 2)
                if not last:
                    second_low(j + 1, e, 0)
                    first_high(j + 1, e, 3, False)
                    second_high(j + 1, e, 1, False)
                low(j, 3)
                if not last:
                    bias_of(j + 1, e)
                    second_low(j + 1, e, 1)
                    rows_low(j + 1)
                    second_high(j + 1, e, 2, False)
                    second_low(j + 1, e, 2)
                finish(j, first)
                if not last:
                    second_high(j + 1, e, 3, False)
                    second_low(j + 1, e, 3)

            tiles(dve, body)

        @block.tensor
        def _(pe):
            def turn_rows(j):
                pe.wait_ge(rows_in, 16 * (j + 1))
                for c in range(KC):
                    for t in range(RT):
                        last = pe.transpose(ps_x[:, c, P * t:P * (t + 1)], rows[:, t, P * c:P * (c + 1)], kit.ident[:, :])
                last.then_inc(x_ps, 1)

            def inner(j, p):
                pe.wait_ge(w1_ready, PAIRS_F * j + p + 1)
                if p == 0:
                    pe.wait_ge(xT_ready, j + 1)
                for f in (2 * p, 2 * p + 1):
                    for c in range(KC):
                        for a, b in TERMS:
                            last = pe.matmul(ps_h[:, f, :], w1[a][:, c, P * f:P * (f + 1)], rowsT[b][:, c, :],
                                             start=c == 0 and (a, b) == TERMS[0], stop=c == KC - 1 and (a, b) == TERMS[-1])
                last.then_inc(h_ps, 1)

            def outer(j, p, first):
                pe.wait_ge(h_ready, PAIRS_F * j + p + 1)
                pe.wait_ge(w2_ready, PAIRS_F * j + p + 1)
                if p == 0 and not first:
                    pe.wait_ge(y_ready, j)
                for t in range(RT):
                    for i in range(2):
                        for a, b in TERMS:
                            last = pe.matmul(ps_y[:, t, :], hT[a][:, p % 2, i, P * t:P * (t + 1)], w2[b][:, 2 * p + i, :],
                                             start=p == 0 and t == 0 and i == 0 and (a, b) == TERMS[0],
                                             stop=p == PAIRS_F - 1 and i == 1 and (a, b) == TERMS[-1],
                                             skip_group_check=True)
                last.then_inc(y_ps, 1)

            turn_rows(0)

            def body(j, first, last):
                inner(j, 0)
                inner(j, 1)
                inner(j, 2)
                outer(j, 0, first)
                inner(j, 3)
                outer(j, 1, first)
                if not last:
                    turn_rows(j + 1)
                outer(j, 2, first)
                outer(j, 3, first)

            tiles(pe, body)


def combine(nc, kit, out):
    N = 7
    PIECES = 8
    with ExitStack() as ctx:
        x = ctx.enter_context(nc.sbuf_tensor("f_x", [P, NT, D], F32, side="right"))
        y = ctx.enter_context(nc.sbuf_tensor("f_y", [P, N, 2, D], F32))
        x_in = [ctx.enter_context(nc.semaphore(f"f_x_in{i}")) for i in range(PIECES)]
        y_in = [ctx.enter_context(nc.semaphore(f"f_y_in{i}")) for i in range(N)]
        half_sum, row_sum, stored = (ctx.enter_context(nc.semaphore("f_" + n)) for n in ("half_sum", "row_sum", "stored"))
        block = ctx.enter_context(nc.Block())
        n = NT // PIECES

        @block.sync
        def _(sp):
            for i in range(PIECES):
                sp.dma_start(x[:, n * i:n * (i + 1), :],
                             kit.x_d[P * n * i:P * n * (i + 1), :].rearrange("(t p) c -> p t c", p=P)).then_inc(x_in[i], 16)
            for i in range(PIECES):
                sp.wait_ge(x_in[i], 16)
                sp.wait_ge(row_sum, n * (i + 1))
                sp.dma_start(out[P * n * i:P * n * (i + 1), :].rearrange("(t p) c -> p t c", p=P),
                             x[:, n * i:n * (i + 1), :]).then_inc(stored, 16)
            sp.wait_ge(stored, 16 * PIECES)

        @block.gpsimd
        def _(pool):
            for t in range(NT):
                if t >= N:
                    pool.wait_ge(y_in[t % N], 32 * (t // N))
                    pool.wait_ge(row_sum, t - N + 1)
                for i in range(2):
                    pool.indirect_dma_start(out=y[:, t % N, i, :], out_offset=None, in_=kit.outs_d,
                                            in_offset=bass.IndirectOffsetOnAxis(ap=kit.slot[:, i, t:t + 1], axis=0))\
                        .then_inc(y_in[t % N], 16)

        @block.vector
        def _(dve):
            for t in range(NT):
                if t % n == 0:
                    dve.wait_ge(x_in[t // n], 16)
                dve.wait_ge(y_in[t % N], 32 * (t // N + 1))
                for i in range(2):
                    dve.scalar_tensor_tensor(out=x[:, t, :], in0=y[:, t % N, i, :], scalar=kit.gate[:, i, t:t + 1],
                                             in1=x[:, t, :], op0=ALU.mult, op1=ALU.add).then_inc((half_sum, row_sum)[i], 1)
                    if i == 0:
                        dve.wait_ge(half_sum, t + 1)


def network(nc, d, out):
    with ExitStack() as ctx:
        kit = Kit()
        x_rows = ctx.enter_context(ExitStack())
        kit.x = x_rows.enter_context(nc.sbuf_tensor("x_rows", [P, NT, D], F32, side="right"))
        kit.mv = ctx.enter_context(nc.sbuf_tensor("mean_var", [P, NT, 2], F32))
        kit.ident = ctx.enter_context(nc.sbuf_tensor("identity", [P, P], F32))
        kit.ident_d = d["ident"]
        kit.sorted_d = nc.dram_tensor("sorted_rows", [SLOT_TILES * R, D], F32, kind="Internal").ap()
        kit.outs_d = nc.dram_tensor("expert_rows", [SLOT_TILES * R, D], F32, kind="Internal").ap()
        kit.q_parts_d = nc.dram_tensor("q_parts", [2, 3, D, S], BF16, kind="Internal").ap()
        kit.k_parts_d = nc.dram_tensor("k_parts", [2, 3, D, S], BF16, kind="Internal").ap()
        kit.x_d = nc.dram_tensor("x_waiting", [NT * P, D], F32, kind="Internal").ap()

        def of(prefix):
            return {k[len(prefix):]: v for k, v in d.items() if k.startswith(prefix)} | \
                {k: d[k] for k in ("x", "ctxT", "mask")}

        for phase, prefix in ((attend_keys, "A_"), (channel_mix, "B_"), (attend_heads, "C_")):
            with nc.cleanup_on_exit():
                phase(nc, kit, of(prefix))
        with ExitStack() as moe:
            kit.w1 = moe.enter_context(nc.sbuf_tensor("w1", [P, E, KC, FF], F32))
            kit.w2 = moe.enter_context(nc.sbuf_tensor("w2", [P, E, FC, D], F32))
            kit.b1 = moe.enter_context(nc.sbuf_tensor("b1", [P, E, FC], F32))
            kit.b2 = moe.enter_context(nc.sbuf_tensor("b2", [P, E, D], F32))
            kit.gate = moe.enter_context(nc.sbuf_tensor("gate", [P, 2, NT], F32))
            kit.slot = moe.enter_context(nc.sbuf_tensor("slot", [P, 2, NT], U32))
            kit.expert = moe.enter_context(nc.sbuf_tensor("expert", [P, SLOT_TILES], I32))
            kit.w_in = moe.enter_context(nc.semaphore("w_in"))
            route(nc, kit, of("D_"))
            x_rows.close()
            experts(nc, kit, of("D_"))
            combine(nc, kit, out)


def kernel(**inputs):
    from concourse import bacc
    from concourse.bass_utils import run_bass_kernel_spmd

    def turned(w):
        return np.ascontiguousarray(w.T)

    def columns(v):
        return np.ascontiguousarray(v.reshape(-1, P).T)

    def to_all(v):
        return np.ascontiguousarray(np.broadcast_to(v, (P,) + v.shape))

    split_order = np.arange(D).reshape(H, DK).T.reshape(P, KC).T.reshape(D)
    z = {k: np.asarray(v) for k, v in inputs.items()}
    a = {"x": z["x"].reshape(B * S, D), "ctxT": turned(z["ctx_1024"].reshape(B * S, D)),
         "mask": z["mask_1x1xSxS2_ik0"].reshape(S, S), "ident": np.eye(P, dtype=np.float32)}
    for to, p in (("A_", "L0_xattn_"), ("C_", "L1_xattn_")):
        for w in "qkvo":
            a[f"{to}w{w}T"] = turned(z[f"{p}W{w}"])
        for b in "qk":
            a[f"{to}w{b}T"] = np.ascontiguousarray(a[f"{to}w{b}T"][:, split_order])
            a[f"{to}b{b}"] = columns(z[f"{p}b{b}"][split_order])
        for b in "vo":
            a[f"{to}b{b}"] = to_all(z[f"{p}b{b}"])
    spaced = np.zeros((H, 2 * DK, D), np.float32)
    spaced[:, :DK] = a["C_woT"].reshape(H, DK, D)
    a["C_woT"] = spaced.reshape(2 * D, D)
    for w in "rkv":
        a[f"B_w{w}T"] = turned(z[f"L0_ffn_W_{w}"])
    for m in "rk":
        a[f"B_mu_{m}"] = columns(z[f"L0_ffn_mu_{m}"])
    a["D_w1"], a["D_w2"] = z["L1_ffn_W1"], z["L1_ffn_W2"]
    a["D_b1"] = np.ascontiguousarray(z["L1_ffn_b1"].reshape(E, FC, P).transpose(2, 0, 1))
    a["D_b2"] = to_all(z["L1_ffn_b2"])
    a["D_wr"], a["D_br"] = z["L1_ffn_router_w"], to_all(z["L1_ffn_router_b"])
    a["D_order"] = to_all(np.arange(-E, 0, dtype=np.float32))
    a["D_tile_no"] = to_all(np.arange(SLOT_TILES, dtype=np.float32))
    a["D_before"] = np.triu(np.ones((P, P), np.float32), 1)

    nc = bacc.Bacc("TRN2", target_bir_lowering=False, num_devices=1)
    d = {k: nc.dram_tensor("in_" + k, v.shape, mybir.dt.from_np(v.dtype), kind="ExternalInput").ap() for k, v in a.items()}
    out = nc.dram_tensor("out", [B * S, D], F32, kind="ExternalOutput").ap()
    network(nc, d, out)
    r = run_bass_kernel_spmd(nc, [{"in_" + k: v for k, v in a.items()}], core_ids=[0])
    return r.results[0]["out"].reshape(B, S, D)
```
